# Optimizing a Trainium2 kernel written in Bass

```python
import numpy as np
import jax
import jax.numpy as jnp

def _softmax(x, axis=-1):
    return jax.nn.softmax(x, axis=axis)

def _gelu(x):
    return jax.nn.gelu(x, approximate=True)

def _silu(x):
    return jax.nn.silu(x)

def _sigmoid(x):
    return jax.nn.sigmoid(x)

def _layernorm(x, axis=-1, eps=1e-05):
    m = jnp.mean(x, axis=axis, keepdims=True)
    v = jnp.var(x, axis=axis, keepdims=True)
    return (x - m) / jnp.sqrt(v + eps)

def _scatter_add(tgt, idx, src, axis=0):
    return tgt.at[idx].add(src)

def _segment_sum(src, seg, n):
    return jax.ops.segment_sum(src, seg, n)
kernel_name = 'mk_flamingo_gated_d2_seqx_r4_47b527'

def setup_inputs(seed: int=0):
    np.random.seed(seed)
    _w = jnp.asarray

    def _rec_inputs():
        import jax
        import jax.numpy as jnp
        _rk = jax.random.key(seed)
        x = -0.000125 + 0.9999 * jax.random.normal(jax.random.fold_in(_rk, 1), (16, 128, 512), jnp.float32)
        _lenS = 128 - jax.random.randint(jax.random.fold_in(_rk, 7), (16,), 0, max(1, 128 // 4) + 1, jnp.int32)
        _lenS2 = 128 - jax.random.randint(jax.random.fold_in(_rk, 8), (16,), 0, max(1, 128 // 4) + 1, jnp.int32)
        _ctx_2048P = jax.random.normal(jax.random.fold_in(_rk, 11), (16, 16, 512), jnp.float32)
        _ctx_2048c = jax.random.dirichlet(jax.random.fold_in(_rk, 511), 0.3 * jnp.ones((16,), jnp.float32), (16, 128))
        _ctx_2048t = jnp.einsum('bsk,bkd->bsd', _ctx_2048c, _ctx_2048P)
        _ctx_2048t = _ctx_2048t * jax.lax.rsqrt(jnp.mean(jnp.square(_ctx_2048t)) + 1e-12) * 0.953939
        ctx_2048 = -0.000514642 + 1.00011 * (_ctx_2048t + 0.3 * jax.random.normal(jax.random.fold_in(_rk, 611), (16, 128, 512), jnp.float32))
        _validS = jnp.arange(128)[None, :] < _lenS[:, None]
        _validS2 = jnp.arange(128)[None, :] < _lenS2[:, None]
        _causal = jnp.tril(jnp.ones((128, 128), dtype=bool))
        mask_BxS2_bk0 = jnp.logical_not(jnp.broadcast_to(_validS2[:, :], (16, 128)))
        _g = jax.random.normal(jax.random.fold_in(_rk, 9001), (2, 2), jnp.float32)
        _g = jnp.sign(_g) * jnp.maximum(jnp.abs(_g), 1.0) + (_g == 0) * 1.0
        g_xattn = _g[0]
        g_ffn = _g[1]
        return (x, ctx_2048, mask_BxS2_bk0, g_xattn, g_ffn)
    x, ctx_2048, mask_BxS2_bk0, g_xattn, g_ffn = _rec_inputs()

    def _L0_xattn_setup():
        import jax, jax.numpy as jnp
        import numpy as np
        H = 512
        NH = 16
        HD = H // NH
        EPS = 1e-06

        def rmsnorm(x, w, eps=EPS):
            var = jnp.mean(x * x, axis=-1, keepdims=True)
            return x * jax.lax.rsqrt(var + eps) * w
        key = jax.random.key(seed)
        ks = jax.random.split(key, 9)
        B, L, M = (4, 1024, 64)
        s = 1.0 / np.sqrt(H)
        return {'hidden_states': jax.random.normal(ks[0], (B, L, H), dtype=jnp.float32), 'memory_tokens': jax.random.normal(ks[1], (B, M, H), dtype=jnp.float32), 'memory_mask': jax.random.randint(ks[2], (B, M), 0, 2).astype(bool), 'norm_w': jnp.ones((H,), dtype=jnp.float32), 'wq': jax.random.normal(ks[3], (H, H), dtype=jnp.float32) * s, 'wk': jax.random.normal(ks[4], (H, H), dtype=jnp.float32) * s, 'wv': jax.random.normal(ks[5], (H, H), dtype=jnp.float32) * s, 'wo': jax.random.normal(ks[6], (H, H), dtype=jnp.float32) * s, 'wg': jax.random.normal(ks[7], (H, H), dtype=jnp.float32) * s}
    _L0_xattn_all = _L0_xattn_setup()
    _L0_xattn_in = {k: v for k, v in _L0_xattn_all.items() if k in ('norm_w', 'wq', 'wk', 'wv', 'wo', 'wg')}
    del _L0_xattn_all

    def _L0_ffn_setup():
        import jax, jax.numpy as jnp
        import numpy as np
        EPS = 1e-08
        QB = 127.0
        key = jax.random.key(seed)
        k1, k2, k3 = jax.random.split(key, 3)
        B, S, DIN, DOUT = (8, 512, 512, 512)
        x = jax.random.normal(k1, (B, S, DIN), dtype=jnp.float32)
        bound = float(np.sqrt(6.0 / DIN))
        weight = jax.random.uniform(k2, (DOUT, DIN), dtype=jnp.float32, minval=-bound, maxval=bound)
        bias = jax.random.normal(k3, (DOUT,), dtype=jnp.float32) * 0.02
        return {'x': x, 'weight': weight, 'bias': bias}
    _L0_ffn_all = _L0_ffn_setup()
    _L0_ffn_in = {k: v for k, v in _L0_ffn_all.items() if k in ('weight', 'bias')}
    del _L0_ffn_all

    def _L1_xattn_setup():
        import jax, jax.numpy as jnp
        import numpy as np
        from math import sqrt
        key = jax.random.key(seed)
        kq, kk, kv = jax.random.split(key, 3)
        B, D, N = (8, 128, 512)
        Q = jax.random.normal(kq, (B, D, N), dtype=jnp.float32)
        K = jax.random.normal(kk, (B, D, N), dtype=jnp.float32)
        V = jax.random.normal(kv, (B, D, N), dtype=jnp.float32)
        return {'Q': Q, 'K': K, 'V': V}
    _L1_xattn_all = _L1_xattn_setup()
    _L1_xattn_in = {k: v for k, v in _L1_xattn_all.items() if k in ()}
    del _L1_xattn_all

    def _L1_ffn_setup():
        import jax, jax.numpy as jnp
        import numpy as np
        DIM = 512
        INTER = 352
        E = 16
        TOPK = 4
        G = 4
        TOPK_G = 2
        N_SHARED = 2
        ROUTE_SCALE = 1.0
        INIT_STD = 0.02
        B, S = (1, 512)
        key = jax.random.key(seed)
        ks = jax.random.split(key, 9)
        std = INIT_STD
        x = jax.random.normal(ks[0], (B, S, DIM), jnp.float32)
        gate_w = jax.random.normal(ks[1], (E, DIM), jnp.float32) * std
        expert_bias = jnp.zeros((E,), jnp.float32)
        w1 = jax.random.normal(ks[2], (E, DIM, INTER), jnp.float32) * std
        w3 = jax.random.normal(ks[3], (E, DIM, INTER), jnp.float32) * std
        w2 = jax.random.normal(ks[4], (E, INTER, DIM), jnp.float32) * std
        sh = N_SHARED * INTER
        sw1 = jax.random.normal(ks[5], (DIM, sh), jnp.float32) * std
        sw3 = jax.random.normal(ks[6], (DIM, sh), jnp.float32) * std
        sw2 = jax.random.normal(ks[7], (sh, DIM), jnp.float32) * std
        return {'x': x, 'gate_w': gate_w, 'expert_bias': expert_bias, 'w1': w1, 'w2': w2, 'w3': w3, 'sw1': sw1, 'sw2': sw2, 'sw3': sw3}
    _L1_ffn_all = _L1_ffn_setup()
    _L1_ffn_in = {k: v for k, v in _L1_ffn_all.items() if k in ('gate_w', 'expert_bias', 'w1', 'w2', 'w3', 'sw1', 'sw2', 'sw3')}
    del _L1_ffn_all
    return {'x': x, 'ctx_2048': ctx_2048, 'mask_BxS2_bk0': mask_BxS2_bk0, 'g_xattn': g_xattn, 'g_ffn': g_ffn, 'L0_xattn_norm_w': _L0_xattn_in['norm_w'], 'L0_xattn_wq': _L0_xattn_in['wq'], 'L0_xattn_wk': _L0_xattn_in['wk'], 'L0_xattn_wv': _L0_xattn_in['wv'], 'L0_xattn_wo': _L0_xattn_in['wo'], 'L0_xattn_wg': _L0_xattn_in['wg'], 'L0_ffn_weight': _L0_ffn_in['weight'], 'L0_ffn_bias': _L0_ffn_in['bias'], 'L1_ffn_gate_w': _L1_ffn_in['gate_w'], 'L1_ffn_expert_bias': _L1_ffn_in['expert_bias'], 'L1_ffn_w1': _L1_ffn_in['w1'], 'L1_ffn_w2': _L1_ffn_in['w2'], 'L1_ffn_w3': _L1_ffn_in['w3'], 'L1_ffn_sw1': _L1_ffn_in['sw1'], 'L1_ffn_sw2': _L1_ffn_in['sw2'], 'L1_ffn_sw3': _L1_ffn_in['sw3']}

def reference(x, ctx_2048, mask_BxS2_bk0, g_xattn, g_ffn, L0_xattn_norm_w, L0_xattn_wq, L0_xattn_wk, L0_xattn_wv, L0_xattn_wo, L0_xattn_wg, L0_ffn_weight, L0_ffn_bias, L1_ffn_gate_w, L1_ffn_expert_bias, L1_ffn_w1, L1_ffn_w2, L1_ffn_w3, L1_ffn_sw1, L1_ffn_sw2, L1_ffn_sw3):
    import jax
    import jax.numpy as jnp

    def _L0_xattn_ref(hidden_states, memory_tokens, memory_mask, norm_w, wq, wk, wv, wo, wg):
        import jax, jax.numpy as jnp
        import numpy as np
        H = 512
        NH = 16
        HD = H // NH
        EPS = 1e-06

        def rmsnorm(x, w, eps=EPS):
            var = jnp.mean(x * x, axis=-1, keepdims=True)
            return x * jax.lax.rsqrt(var + eps) * w
        B, L, C = hidden_states.shape
        M = memory_tokens.shape[1]
        scale = HD ** (-0.5)
        x = rmsnorm(hidden_states, norm_w)
        q = (x @ wq.T).reshape(B, L, NH, HD)
        k = (memory_tokens @ wk.T).reshape(B, M, NH, HD)
        v = (memory_tokens @ wv.T).reshape(B, M, NH, HD)
        attn = jnp.einsum('blhd,bmhd->bhlm', q, k) * scale
        attn = jnp.where(memory_mask[:, None, None, :], attn, -jnp.inf)
        attn = jax.nn.softmax(attn, axis=-1)
        attn = jnp.nan_to_num(attn, nan=0.0)
        out = jnp.einsum('bhlm,bmhd->blhd', attn, v).reshape(B, L, C)
        out = out @ wo.T
        gate = jax.nn.sigmoid(x @ wg.T)
        return gate * out

    def _L0_ffn_ref(x, weight, bias):
        import jax, jax.numpy as jnp
        import numpy as np
        EPS = 1e-08
        QB = 127.0
        rms = jnp.sqrt(jnp.mean(x * x, axis=-1, keepdims=True) + EPS)
        xn = x / rms
        gamma = jnp.mean(jnp.abs(weight), axis=-1, keepdims=True)
        w_ternary = jnp.clip(jnp.round(weight / (gamma + EPS)), -1.0, 1.0)
        x_scale = jnp.max(jnp.abs(xn), axis=-1, keepdims=True) / QB
        x_q = jnp.clip(jnp.round(xn / (x_scale + EPS)), -QB, QB)
        out = jnp.einsum('bsk,nk->bsn', x_q, w_ternary)
        out = out * gamma[:, 0] * x_scale
        return out + bias

    def _L1_xattn_ref(Q, K, V):
        import jax, jax.numpy as jnp
        import numpy as np
        from math import sqrt
        dk = Q.shape[1]
        x = jnp.einsum('bdn,bdm->bnm', Q, K) / sqrt(dk)
        score = jax.nn.sigmoid(x)
        out = jnp.einsum('bvn,bnm->bvm', V, score)
        return out

    def _L1_ffn_ref(x, gate_w, expert_bias, w1, w2, w3, sw1, sw2, sw3):
        import jax, jax.numpy as jnp
        import numpy as np
        DIM = 512
        INTER = 352
        E = 16
        TOPK = 4
        G = 4
        TOPK_G = 2
        N_SHARED = 2
        ROUTE_SCALE = 1.0
        INIT_STD = 0.02
        B, S = (1, 512)
        b, s, d = x.shape
        T = b * s
        xf = x.reshape(T, d)
        scores = jax.nn.sigmoid(xf @ gate_w.T)
        original_scores = scores
        scores = scores + expert_bias
        sg = scores.reshape(T, G, E // G)
        group_scores = sg.max(axis=-1)
        _, gidx = jax.lax.top_k(group_scores, TOPK_G)
        gmask = jnp.zeros((T, G), bool).at[jnp.arange(T)[:, None], gidx].set(True)
        masked = jnp.where(gmask[:, :, None], sg, -jnp.inf).reshape(T, E)
        _, idx = jax.lax.top_k(masked, TOPK)
        w = jnp.take_along_axis(original_scores, idx, axis=1)
        w = w / jnp.sum(w, axis=-1, keepdims=True)
        w = w * ROUTE_SCALE
        cw = jnp.zeros((T, E), x.dtype).at[jnp.arange(T)[:, None], idx].add(w)
        h = jax.nn.silu(jnp.einsum('td,edh->teh', xf, w1)) * jnp.einsum('td,edh->teh', xf, w3)
        y = jnp.einsum('teh,ehd,te->td', h, w2, cw)
        z = jax.nn.silu(xf @ sw1) * (xf @ sw3) @ sw2
        return (y + z).reshape(b, s, d)
    x = x + jnp.tanh(g_xattn[0]) * _L0_xattn_ref(_layernorm(x, axis=-1), ctx_2048, mask_BxS2_bk0, L0_xattn_norm_w, L0_xattn_wq, L0_xattn_wk, L0_xattn_wv, L0_xattn_wo, L0_xattn_wg)
    x = x + jnp.tanh(g_ffn[0]) * _L0_ffn_ref(_layernorm(x, axis=-1), L0_ffn_weight, L0_ffn_bias)
    x = x + jnp.tanh(g_xattn[1]) * _L1_xattn_ref(_layernorm(x, axis=-1), ctx_2048, ctx_2048)
    x = x + jnp.tanh(g_ffn[1]) * _L1_ffn_ref(_layernorm(x, axis=-1), L1_ffn_gate_w, L1_ffn_expert_bias, L1_ffn_w1, L1_ffn_w2, L1_ffn_w3, L1_ffn_sw1, L1_ffn_sw2, L1_ffn_sw3)
    return x

_drawn_inputs = setup_inputs


def setup_inputs(seed=0):
    import zlib

    import numpy as np

    out = dict(_drawn_inputs(seed))
    spreads = {'g_ffn': (-1.0, 0.6), 'L0_xattn_norm_w': (1.0, 0.6), 'L1_ffn_expert_bias': (0.0, 0.8)}
    factors = {'L0_ffn_bias': 2.755,
     'L1_ffn_gate_w': 8.0,
     'L1_ffn_w1': 8.0,
     'L1_ffn_w2': 8.0,
     'L1_ffn_w3': 8.0,
     'L1_ffn_sw1': 8.0,
     'L1_ffn_sw2': 8.0,
     'L1_ffn_sw3': 8.0}
    for name, (base, spread) in spreads.items():
        noise = np.random.default_rng([zlib.crc32(name.encode()), seed]).standard_normal(out[name].shape)
        drawn = base * np.exp(spread * noise) if base else spread * noise
        out[name] = jnp.asarray(drawn.astype(out[name].dtype))
    for name, factor in factors.items():
        out[name] = (out[name] * factor).astype(out[name].dtype)
    return out
```

```python
from contextlib import ExitStack

import concourse.bass as bass
from concourse import mybir

ALU = mybir.AluOpType
ACT = mybir.ActivationFunctionType
AX = mybir.AxisListType
F32 = mybir.dt.float32
F32R = mybir.dt.float32r
BF16 = mybir.dt.bfloat16
U8 = mybir.dt.uint8

P = 128
NB, S, D = 16, 128, 512
KC = D // P
GB = 4
NG = NB // GB
GT = GB * S
NH, HD = 16, 32
HQ = P // HD
SCALE0 = float(HD) ** -0.5
SCALE1 = float(S) ** -0.5
MASKED = -1.0e30
ROUND = 1.5 * 2.0 ** 23
E, I, TOPK = 16, 352, 4
EG, TOPG = 4, 2
NE = E + 2
IC = [P, P, I - 2 * P]


class Count:

    def __init__(self, sem, per, credit=False):
        self.sem, self.per, self.credit = sem, per, credit

    def grant(self, eng):
        eng.sem_inc(self.sem, self.per)

    def wait(self, eng, trip, k, own=None):
        eng.wait_ge(self.sem, trip * self.per + (k + self.per if self.credit else k))
        if own is not None:
            eng.sem_inc(own, 1)


def mm3(pe, out, lhs, rhs, first, last):
    pe.matmul(out, lhs(0), rhs(0), start=first, stop=False)
    pe.matmul(out, lhs(0), rhs(1), start=False, stop=False)
    return pe.matmul(out, lhs(1), rhs(0), start=False, stop=last)


def program(nc, x, ctx_in, mask, g_x, g_f, norm_w, wq, wk, wv, wo, wg, fw, fb,
            gate_w, ebias, w1, w2, w3, sw1, sw2, sw3, out):
    with ExitStack() as top:
        def sb(name, shape, dt=F32):
            return top.enter_context(nc.sbuf_tensor(name, shape, dt))

        X = sb("X", [P, NB, D])
        bst = sb("bst", [P, NB, 6])
        mean = sb("mean", [P, NB])
        rstd = sb("rstd", [P, NB])
        tmp16 = sb("tmp16", [P, 11, NB])
        identF = sb("identF", [P, P])
        identB = sb("identB", [P, P], BF16)
        onesF = sb("onesF", [P, P])
        onesB = sb("onesB", [P, P], BF16)
        nhalf = sb("nhalf", [P, NB])
        tg = sb("tg", [P, 4])
        parts = dict(X=X, bst=bst, mean=mean, rstd=rstd, tmp16=tmp16, identF=identF, identB=identB, onesF=onesF,
                     onesB=onesB, nhalf=nhalf, tg=tg)
        for e in ("pool", "sp", "dve"):
            parts[f"passed_{e}"] = top.enter_context(nc.semaphore(f"passed_{e}"))
        start_up(nc, parts, x, g_x, g_f)
        attention_heads(nc, parts, ctx_in, mask, norm_w, wq, wk, wv, wo, wg)
        ternary_ffn(nc, parts, fw, fb)
        attention_features(nc, parts, ctx_in)
        experts(nc, parts, gate_w, ebias, w1, w2, w3, sw1, sw2, sw3, out)


def start_up(nc, c, x, g_x, g_f):
    with ExitStack() as st:
        def sem(name):
            return st.enter_context(nc.semaphore(name))
        gr = st.enter_context(nc.sbuf_tensor("gr", [1, 4], F32))
        gp = st.enter_context(nc.psum_tensor("gp", [P, 512], F32))
        x_in, g_in = [sem(f"x_in{q}") for q in range(NG)], sem("g_in")
        zeroed, consts, stats, gates_bc, seen = sem("zeroed"), sem("consts"), sem("stats"), sem("gates_bc"), sem("seen")
        block = st.enter_context(nc.Block())

        @block.sync
        def _(sp):
            sp.dma_start(gr[:, 0:2], g_x.rearrange("(a n) -> a n", a=1)).then_inc(g_in, 16)
            sp.dma_start(gr[:, 2:4], g_f.rearrange("(a n) -> a n", a=1)).then_inc(g_in, 16)
            for q in range(NG):
                sp.dma_start(c["X"][:, q * GB:(q + 1) * GB, :],
                             x[q * GB:(q + 1) * GB].rearrange("b p d -> p b d")).then_inc(x_in[q], 16)

        @block.gpsimd
        def _(pool):
            pool.memset(c["identF"][:, :], 0.0).then_inc(zeroed, 1)
            pool.memset(c["identB"][:, :], 0.0).then_inc(zeroed, 1)
            pool.memset(c["onesF"][:, :], 1.0).then_inc(consts, 1)
            pool.memset(c["onesB"][:, :], 1.0).then_inc(consts, 1)
            pool.memset(c["nhalf"][:, :], -0.5).then_inc(consts, 1)
            pool.wait_ge(zeroed, 2)
            for m in (c["identF"], c["identB"]):
                pool.affine_select(out=m[:, :], in_=m[:, :], compare_op=ALU.not_equal, fill=1.0,
                                   base=0, pattern=[[-1, P]], channel_multiplier=1).then_inc(consts, 1)

        @block.tensor
        def _(pe):
            pe.wait_ge(consts, 5)
            pe.wait_ge(g_in, 32)
            pe.matmul(gp[:, 0:4], c["onesF"][0:1, :], gr[0:1, :], start=True, stop=True).then_inc(gates_bc, 1)

        @block.scalar
        def _(act):
            act.wait_ge(gates_bc, 1)
            act.activation(c["tg"][:, :], gp[:, 0:4], ACT.Tanh).then_inc(seen, 1)

        @block.vector
        def _(dve):
            for t in range(NB):
                if t % GB == 0:
                    dve.wait_ge(x_in[t // GB], 16)
                dve.bn_stats(c["bst"][:, t, :], c["X"][:, t, :]).then_inc(stats, 1)


def row_scale(pool, c, done, eps, ms_eps=None):
    t = c["tmp16"]
    bst = c["bst"]
    var = t[:, 10, :]
    n = 0

    def step(instr):
        nonlocal n
        n += 1
        instr.then_inc(done, 1)
        pool.wait_ge(done, n)
    step(pool.tensor_tensor(t[:, 6, :], bst[:, :, 1], bst[:, :, 4], ALU.add))
    step(pool.tensor_scalar(c["mean"][:, :], t[:, 6, :], 0.5, None, ALU.mult))
    step(pool.tensor_tensor(t[:, 7, :], bst[:, :, 1], bst[:, :, 4], ALU.subtract))
    step(pool.tensor_scalar(t[:, 7, :], t[:, 7, :], 0.5, None, ALU.mult))
    step(pool.tensor_tensor(t[:, 7, :], t[:, 7, :], t[:, 7, :], ALU.mult))
    step(pool.tensor_tensor(t[:, 8, :], bst[:, :, 2], bst[:, :, 5], ALU.add))
    step(pool.tensor_scalar(t[:, 9, :], t[:, 8, :], 1.0 / D, None, ALU.mult))
    step(pool.tensor_tensor(var, t[:, 9, :], t[:, 7, :], ALU.add))
    step(pool.tensor_scalar(t[:, 0, :], var, eps, None, ALU.add))
    if ms_eps is None:
        step(pool.tensor_tensor(c["rstd"][:, :], t[:, 0, :], c["nhalf"][:, :], ALU.pow))
        return n
    step(pool.tensor_tensor(t[:, 1, :], t[:, 0, :], c["nhalf"][:, :], ALU.pow))
    step(pool.tensor_tensor(t[:, 2, :], t[:, 1, :], t[:, 1, :], ALU.mult))
    step(pool.tensor_tensor(t[:, 3, :], t[:, 2, :], var, ALU.mult))
    step(pool.tensor_scalar(t[:, 4, :], t[:, 3, :], ms_eps, None, ALU.add))
    step(pool.tensor_tensor(t[:, 5, :], t[:, 4, :], c["nhalf"][:, :], ALU.pow))
    step(pool.tensor_tensor(c["rstd"][:, :], t[:, 1, :], t[:, 5, :], ALU.mult))
    return n


def attention_heads(nc, c, ctx_in, mask, norm_w, wq, wk, wv, wo, wg):
    X, identF = c["X"], c["identF"]
    with ExitStack() as st:
        def sb(name, shape, dt=F32):
            return st.enter_context(nc.sbuf_tensor(name, shape, dt))

        def sem(name):
            return st.enter_context(nc.semaphore(name))

        def bank(name, n):
            return [st.enter_context(nc.psum_tensor(f"{name}{i}", [P, 512], F32)) for i in range(n)]

        W = [sb(f"W{n}", [P, 2, KC, D], F32R) for n in "qkvgo"]
        WQ, WK, WV, WG, WO = W
        nw = sb("nw", [P, KC])
        mcol = sb("mcol", [P, NB])
        mrow = sb("mrow", [P, GB, S], BF16)
        CT = sb("CT", [P, GB, D])
        xn = sb("xn", [P, 2, D])
        xT = sb("xT", [P, 2, KC, GT], F32R)
        cT = sb("cT", [P, 2, KC, GT], F32R)
        qT = sb("qT", [P, KC, GT])
        kT = sb("kT", [P, KC, GT])
        va = sb("va", [P, 2, NH, HD + 1])
        gs = sb("gs", [P, 2, D])
        pr = sb("pr", [P, 2, HQ, S])
        pT = sb("pT", [P, 2, HQ, S])
        mx = sb("mx", [P, 2, HQ])
        rs = sb("rs", [P, 2, 2, HQ])
        o = sb("o", [P, D])
        oT = sb("oT", [P, 2, KC, S], F32R)
        upd = sb("upd", [P, D])
        mask_u8 = sb("mask_u8", [NB, S], U8)
        mask_f = sb("mask_f", [NB, S])
        mrow_u8 = sb("mrow_u8", [P, GB, S], U8)
        T, M, SC, O = bank("T", 2), bank("M", 2), bank("SC", 2), bank("O", 2)

        raw = [qT, kT]
        names = [(WQ, wq, True), (WK, wk, False), (WV, wv, False), (WG, wg, True), (WO, wo, False)]
        w_in = [sem(f"w_in{i}") for i in range(2)]
        nw_in, mask_in, w_tr, w_hi, w_lo = sem("nw_in"), sem("mask_in"), sem("w_tr"), sem("w_hi"), sem("w_lo")
        m_ready, m_tr, m_col, scales = sem("m_ready"), sem("m_tr"), sem("m_col"), sem("scales")
        ones_set = sem("ones_set")
        with nc.Block() as block:
            @block.sync
            def _(sp):
                sp.dma_start(mask_u8[:, :], mask).then_inc(mask_in, 16)
                with nc.allow_non_contiguous_dma(reason="512 scales once"):
                    sp.dma_start(nw[:, :], norm_w.rearrange("(k p) -> p k", p=P)).then_inc(nw_in, 16)
                for n, (_, w, _) in enumerate(names):
                    if n >= 2:
                        sp.wait_ge(w_tr, KC * (n - 1))
                    sp.dma_start(raw[n % 2][:, :, :], w.rearrange("(o p) k -> p o k", p=P)).then_inc(w_in[n % 2], 16)

            @block.gpsimd
            def _(pool):
                row_scale(pool, c, scales, 1e-5, 1e-6)
                for b in range(2):
                    pool.memset(va[:, b, :, HD:HD + 1], 1.0).then_inc(ones_set, 1)

            @block.tensor
            def _(pe):
                for n in range(len(names)):
                    pe.wait_ge(w_in[n % 2], 16 * (n // 2 + 1))
                    for kc in range(KC):
                        f = KC * n + kc
                        if f >= 2:
                            pe.wait_ge(w_hi, f - 1)
                            pe.wait_ge(w_lo, f - 1)
                        for oc in range(KC):
                            m = pe.transpose(T[f % 2][:, oc * P:(oc + 1) * P],
                                             raw[n % 2][:, oc, kc * P:(kc + 1) * P], identF[:, :])
                        m.then_inc(w_tr, 1)
                pe.wait_ge(m_ready, 1)
                pe.transpose(M[0][:, 0:NB], mask_f[:, :], identF[0:NB, 0:NB]).then_inc(m_tr, 1)

            @block.scalar
            def _(act):
                act.wait_ge(nw_in, 16)
                for n, (dst, _, normed) in enumerate(names):
                    for kc in range(KC):
                        f = KC * n + kc
                        act.wait_ge(w_tr, f + 1)
                        act.activation(dst[:, 0, kc, :], T[f % 2][:, :], ACT.Copy,
                                       scale=nw[:, kc:kc + 1] if normed else 1.0).then_inc(w_hi, 1)

            @block.vector
            def _(dve):
                dve.wait_ge(mask_in, 16)
                dve.tensor_copy(mask_f[:, :], mask_u8[:, :]).then_inc(m_ready, 1)
                dve.wait_ge(nw_in, 16)
                for n, (dst, _, normed) in enumerate(names):
                    for kc in range(KC):
                        f = KC * n + kc
                        dve.wait_ge(w_hi, f + 1)
                        dve.scalar_tensor_tensor(out=dst[:, 1, kc, :], in0=T[f % 2][:, :],
                                                 scalar=nw[:, kc:kc + 1] if normed else 1.0,
                                                 in1=dst[:, 0, kc, :].bitcast(F32), op0=ALU.mult,
                                                 op1=ALU.subtract).then_inc(w_lo, 1)
                dve.wait_ge(m_tr, 1)
                dve.tensor_copy(mcol[:, :], M[0][:, 0:NB]).then_inc(m_col, 1)

        plan = []
        for b in range(GB):
            plan += [("xT", b), ("cT", b)]
        plan += [("q", i) for i in range(KC)] + [("k", i) for i in range(KC)]
        for b in range(GB):
            plan += [("S", b, 0), ("S", b, 1), ("v", b), ("g", b)]
            if b:
                plan += [("oT", b - 1), ("oP", b - 1)]
            plan += [("pT", b, 0), ("S", b, 2), ("pv", b, 0), ("pT", b, 1), ("S", b, 3), ("pv", b, 1), ("on", b, 0),
                     ("pT", b, 2), ("pv", b, 2), ("pT", b, 3), ("pv", b, 3), ("on", b, 1)]
        plan += [("oT", GB - 1), ("oP", GB - 1)]
        t_fills = [s for s in plan if s[0] in ("xT", "cT", "pT", "oT")]
        m_fills = [s for s in plan if s[0] in ("q", "k", "v", "g", "oP")]
        t_split = [s for s in t_fills if s[0] != "pT"]
        m_by_act = [s for s in m_fills if s[0] in ("q", "k", "g")]
        m_by_dve = [s for s in m_fills if s[0] in ("v", "oP")]
        assert len(t_fills) % 2 == 0 and len(m_fills) % 2 == 0

        def before(steps, some, i):
            return sum(s in some for s in steps[:i + 1]) if i >= 0 else \
                sum(s in some for s in steps[:i + 1 + len(steps)]) - len(some)

        c_in, mrow_in = sem("c_in"), sem("mrow_in")
        mrow_ready = Count(sem("mrow_ready"), 1)
        x_norm = Count(sem("x_norm"), GB)
        t_fill = Count(sem("t_fill"), len(t_fills))
        t_hi = Count(sem("t_hi"), len(t_fills), True)
        t_lo = Count(sem("t_lo"), len(t_split), True)
        m_fill = Count(sem("m_fill"), len(m_fills))
        m_act = Count(sem("m_act"), len(m_by_act), True)
        m_dve = Count(sem("m_dve"), len(m_by_dve), True)
        NQ = GB * HQ
        s_fill = Count(sem("s_fill"), NQ)
        s_max = Count(sem("s_max"), NQ)
        s_out = Count(sem("s_out"), NQ, True)
        p_exp = Count(sem("p_exp"), NQ)
        pv = Count(sem("pv"), NQ, True)
        o_rec = Count(sem("o_rec"), 2 * GB)
        o_norm = Count(sem("o_norm"), 2 * GB, True)
        added = Count(sem("added"), GB, True)

        with nc.Block() as block:
            @block.sync
            def _(sp):
                with sp.Fori(0, NG) as g:
                    t_lo.wait(sp, g, -len([s for s in t_split if s[0] == "oT"]), c["passed_sp"])
                    sp.dma_start(CT[:, :, :], ctx_in[bass.ds(g * GB, GB)].rearrange("b p d -> p b d")).then_inc(c_in, 16)
                    s_out.wait(sp, g, 0, c["passed_sp"])
                    sp.dma_start(mrow_u8[:, :, :], mask[bass.ds(g * GB, GB)].rearrange("(a b) m -> a b m", a=1)
                                 .to_broadcast([P, GB, S])).then_inc(mrow_in, 16)

            @block.gpsimd
            def _(pool):
                added.grant(pool)
                with pool.Fori(0, NG) as g:
                    pool.wait_ge(mrow_in, 16 * g + 16)
                    pool.sem_inc(c["passed_pool"], 1)
                    s_out.wait(pool, g, 0, c["passed_pool"])
                    pool.tensor_scalar(mrow[:, :, :], mrow_u8[:, :, :], -1.0, -MASKED, ALU.add, ALU.mult)\
                        .then_inc(mrow_ready.sem, 1)
                    for b in range(GB):
                        m_dve.wait(pool, g, m_by_dve.index(("oP", b)) + 1, c["passed_pool"])
                        pool.tensor_tensor(X[:, g * GB + b, :], X[:, g * GB + b, :], upd[:, :], ALU.add)\
                            .then_inc(added.sem, 1)

            @block.tensor
            def _(pe):
                with pe.Fori(0, NG) as g:
                    tf = mf = 0
                    for s in plan:
                        kind, b = s[0], s[1]
                        if s in t_fills:
                            bk = T[tf % 2]
                            t_hi.wait(pe, g, tf - 1)
                            t_lo.wait(pe, g, before(t_fills, t_split, tf - 2))
                            if kind == "xT":
                                x_norm.wait(pe, g, b + 1)
                            if kind == "cT" and b == 0:
                                pe.wait_ge(c_in, 16 * g + 16)
                            if kind == "pT":
                                p_exp.wait(pe, g, b * HQ + s[2] + 1)
                            if kind == "oT":
                                o_norm.wait(pe, g, 2 * b + 2)
                            for k in range(KC):
                                src = {"xT": lambda k: xn[:, b % 2, k * P:(k + 1) * P],
                                       "cT": lambda k: CT[:, b, k * P:(k + 1) * P],
                                       "pT": lambda k: pr[:, s[2] % 2, k, :] if kind == "pT" else None,
                                       "oT": lambda k: o[:, k * P:(k + 1) * P]}[kind](k)
                                i = pe.transpose(bk[:, k * P:(k + 1) * P], src, identF[:, :])
                            i.then_inc(t_fill.sem, 1)
                            tf += 1
                        elif s in m_fills:
                            bk = M[mf % 2]
                            m_act.wait(pe, g, before(m_fills, m_by_act, mf - 2))
                            m_dve.wait(pe, g, before(m_fills, m_by_dve, mf - 2))
                            if kind in ("q", "k"):
                                w, a = (WQ, xT) if kind == "q" else (WK, cT)
                                if kind == "q" and b == 0:
                                    t_lo.wait(pe, g, 2 * GB)
                                    t_hi.wait(pe, g, 2 * GB)
                                for k in range(KC):
                                    i = mm3(pe, bk[:, :], lambda h: w[:, h, k, b * P:(b + 1) * P],
                                            lambda h: a[:, h, k, :], k == 0, k == KC - 1)
                            else:
                                if kind == "oP":
                                    t_lo.wait(pe, g, 2 * GB + b + 1)
                                w = {"v": WV, "g": WG, "oP": WO}[kind]
                                for k in range(KC):
                                    lhs = {"v": lambda h: cT[:, h, k, b * S:(b + 1) * S],
                                           "g": lambda h: xT[:, h, k, b * S:(b + 1) * S],
                                           "oP": lambda h: oT[:, h, k, :]}[kind]
                                    i = mm3(pe, bk[:, :], lhs, lambda h: w[:, h, k, :], k == 0, k == KC - 1)
                            i.then_inc(m_fill.sem, 1)
                            mf += 1
                        elif kind == "S":
                            n = b * HQ + s[2]
                            r = s[2] * HD
                            bk = SC[n % 2]
                            s_out.wait(pe, g, n - 1)
                            if n == 0:
                                mrow_ready.wait(pe, g, 1)
                                m_act.wait(pe, g, 2 * KC)
                            pe.matmul(bk[:, :].rearrange("p (j m) -> p j m", j=HQ), c["onesB"][r:r + 1, :],
                                      mrow[r:r + 1, b:b + 1, :].to_broadcast([1, HQ, S]),
                                      start=True, stop=False)
                            for j in range(KC):
                                i = pe.matmul(bk[:, j * S:(j + 1) * S], qT[r:r + HD, j, b * S:(b + 1) * S],
                                              kT[r:r + HD, j, b * S:(b + 1) * S], start=False, stop=j == KC - 1)
                            i.then_inc(s_fill.sem, 1)
                        elif kind == "pv":
                            n = b * HQ + s[2]
                            t_hi.wait(pe, g, t_fills.index(("pT", b, s[2])) + 1)
                            if s[2] == 0:
                                m_dve.wait(pe, g, before(m_by_dve, m_by_dve, m_by_dve.index(("v", b))))
                            if s[2] % 2 == 0:
                                o_norm.wait(pe, g, 2 * b + s[2] // 2 - 1)
                            for j in range(KC):
                                at = (s[2] % 2 * HQ + j) * (HD + 1)
                                i = pe.matmul(O[s[2] // 2][:, at:at + HD + 1], pT[:, s[2] % 2, j, :],
                                              va[:, b % 2, j * HQ + s[2], :], start=True, stop=True)
                            i.then_inc(pv.sem, 1)

            @block.scalar
            def _(act):
                t_hi.grant(act)
                m_act.grant(act)
                with act.Fori(0, NG) as g:
                    tf = mf = 0
                    for s in plan:
                        kind, b = s[0], s[1]
                        if s in t_fills:
                            t_fill.wait(act, g, tf + 1)
                            src = T[tf % 2][:, :]
                            if kind in ("xT", "cT"):
                                if tf == 0:
                                    m_act.wait(act, g, 0)
                                    m_dve.wait(act, g, 0)
                                dst = (xT if kind == "xT" else cT)[:, 0, :, b * S:(b + 1) * S]
                                src = src.rearrange("p (k t) -> p k t", k=KC)
                            elif kind == "pT":
                                pv.wait(act, g, b * HQ + s[2] - 1)
                                dst = pT[:, s[2] % 2, :, :].rearrange("p j m -> p (j m)")
                            else:
                                m_dve.wait(act, g, before(m_by_dve, m_by_dve, m_by_dve.index(("oP", b - 1))) if b else 0)
                                dst = oT[:, 0, :, :].rearrange("p k t -> p (k t)")
                            act.activation(dst, src, ACT.Copy).then_inc(t_hi.sem, 1)
                            tf += 1
                        elif s in m_fills:
                            mf += 1
                            if s not in m_by_act:
                                continue
                            m_fill.wait(act, g, mf)
                            if kind == "g":
                                m_dve.wait(act, g, m_by_dve.index(("oP", b - 2)) + 1 if b >= 2 else
                                           m_by_dve.index(("oP", b + 2)) + 1 - len(m_by_dve))
                                act.activation(gs[:, b % 2, :], M[(mf - 1) % 2][:, :], ACT.Sigmoid).then_inc(m_act.sem, 1)
                            else:
                                if kind == "q" and b == 0:
                                    s_out.wait(act, g, 0)
                                act.activation((qT if kind == "q" else kT)[:, b, :], M[(mf - 1) % 2][:, :],
                                               ACT.Copy).then_inc(m_act.sem, 1)
                        elif kind == "S":
                            n = b * HQ + s[2]
                            s_out.wait(act, g, n + 1)
                            pp = pr[:, n % 2, :, :].rearrange("p j m -> p (j m)")
                            act.activation(pp, pp, ACT.Exp, scale=SCALE0).then_inc(p_exp.sem, 1)

            @block.vector
            def _(dve):
                for s_ in (t_lo, m_dve, s_out, o_norm, pv):
                    s_.grant(dve)
                with dve.Fori(0, NG) as g:
                    tf = mf = tl = 0

                    def stats(b):
                        added.wait(dve, g, b + 1, c["passed_dve"])
                        dve.bn_stats(c["bst"][:, g * GB + b, :], X[:, g * GB + b, :])

                    for s in plan:
                        kind, b = s[0], s[1]
                        if kind == "xT":
                            t_hi.wait(dve, g, t_fills.index(("xT", b - 2)) + 1 if b >= 2 else 0)
                            dve.tensor_scalar(xn[:, b % 2, :], X[:, g * GB + b, :], c["mean"][:, bass.ds(g * GB + b, 1)],
                                              c["rstd"][:, bass.ds(g * GB + b, 1)], ALU.subtract, ALU.mult)\
                                .then_inc(x_norm.sem, 1)
                        if s in t_fills:
                            tf += 1
                            if s not in t_split:
                                continue
                            t_hi.wait(dve, g, tf)
                            src = T[(tf - 1) % 2][:, :]
                            if kind in ("xT", "cT"):
                                a = xT if kind == "xT" else cT
                                hi, lo = (a[:, h, :, b * S:(b + 1) * S] for h in range(2))
                                src = src.rearrange("p (k t) -> p k t", k=KC)
                            else:
                                hi, lo = (oT[:, h, :, :].rearrange("p k t -> p (k t)") for h in range(2))
                            dve.tensor_tensor(lo, src, hi.bitcast(F32), ALU.subtract).then_inc(t_lo.sem, 1)
                        elif s in m_fills:
                            mf += 1
                            if s not in m_by_dve:
                                continue
                            m_fill.wait(dve, g, mf)
                            if kind == "v":
                                pv.wait(dve, g, (b - 1) * HQ)
                                dve.tensor_scalar(va[:, b % 2, :, 0:HD],
                                                  M[(mf - 1) % 2][:, :].rearrange("p (h d) -> p h d", h=NH),
                                                  mcol[:, bass.ds(g * GB + b, 1)], None, ALU.mult).then_inc(m_dve.sem, 1)
                            else:
                                m_act.wait(dve, g, m_by_act.index(("g", b)) + 1)
                                added.wait(dve, g, b)
                                dve.scalar_tensor_tensor(out=upd[:, :], in0=M[(mf - 1) % 2][:, :],
                                                         scalar=c["tg"][:, 0:1], in1=gs[:, b % 2, :],
                                                         op0=ALU.mult, op1=ALU.mult).then_inc(m_dve.sem, 1)
                                if b:
                                    stats(b - 1)
                        elif kind == "S":
                            n = b * HQ + s[2]
                            s_fill.wait(dve, g, n + 1)
                            sc = SC[n % 2][:, :].rearrange("p (j m) -> p j m", j=HQ)
                            dve.tensor_reduce(mx[:, n % 2, :], sc, AX.X, ALU.max).then_inc(s_max.sem, 1)
                            s_max.wait(dve, g, n + 1)
                            m = (n - 2) % NQ
                            k = t_fills.index(("pT", m // HQ, m % HQ)) - (len(t_fills) if n < 2 else 0)
                            t_hi.wait(dve, g, k + 1)
                            dve.tensor_tensor(pr[:, n % 2, :, :], sc, mx[:, n % 2, :].unsqueeze(2).to_broadcast([P, HQ, S]),
                                              ALU.subtract).then_inc(s_out.sem, 1)
                        elif kind == "on":
                            half = s[2]
                            n = 2 * b + half
                            pv.wait(dve, g, b * HQ + 2 * half + 2)
                            ov = O[half][:, 0:2 * HQ * (HD + 1)].rearrange("p (r j d) -> p r j d", r=2, j=HQ)
                            dve.reciprocal(rs[:, half, :, :], ov[:, :, :, HD]).then_inc(o_rec.sem, 1)
                            o_rec.wait(dve, g, n + 1)
                            if half == 0:
                                t_hi.wait(dve, g, t_fills.index(("oT", b - 1)) + 1 if b else 0)
                            oo = o[:, :].rearrange("p (j r d) -> p r j d", j=KC, r=HQ)
                            dve.tensor_tensor(oo[:, 2 * half:2 * half + 2, :, :], ov[:, :, :, 0:HD],
                                              rs[:, half, :, :].unsqueeze(3).to_broadcast([P, 2, HQ, HD]),
                                              ALU.mult).then_inc(o_norm.sem, 1)
                    stats(GB - 1)



def ternary_ffn(nc, c, fw, fb):
    X = c["X"]
    PAIR = 2
    with ExitStack() as st:
        def sb(name, shape, dt=F32):
            return st.enter_context(nc.sbuf_tensor(name, shape, dt))

        def sem(name):
            return st.enter_context(nc.semaphore(name))

        def bank(name, n, dt=F32):
            return [st.enter_context(nc.psum_tensor(f"{name}{i}", [P, 2048 // mybir.dt.size(dt)], dt)) for i in range(n)]

        raw = sb("fraw", [P, KC, D])
        sm = sb("fsm", [P, 4, KC])
        wr = sb("fwr", [P, KC, D])
        wt = sb("fwt", [P, KC, D], BF16)
        wT = sb("fwT", [P, KC, D], BF16)
        dg = sb("fdg", [P, KC, P])
        bias1 = sb("fbias", [1, D])
        grow = sb("fgrow", [P, D])
        brow = sb("fbrow", [P, D])
        u = sb("fu", [P, PAIR, D])
        ur = sb("fur", [P, PAIR, D])
        uq = sb("fuq", [P, PAIR, D], BF16)
        uT = sb("fuT", [P, PAIR, D], BF16)
        sc = sb("fsc", [P, PAIR, 4])
        upd = sb("fupd", [P, PAIR, D])
        TB = bank("fTB", 2, BF16)
        M = bank("fM", 2)
        w_in, b_in, prep, w_tr, w_out, rows, rows_out, scales = (sem(f"f_{n}") for n in (
            "w_in", "b_in", "prep", "w_tr", "w_out", "rows", "rows_out", "scales"))
        with nc.Block() as block:
            @block.sync
            def _(sp):
                sp.dma_start(raw[:, :, :], fw.rearrange("(o p) k -> p o k", p=P)).then_inc(w_in, 16)
                sp.dma_start(bias1[:, :], fb.rearrange("(a n) -> a n", a=1)).then_inc(b_in, 16)

            @block.gpsimd
            def _(pool):
                row_scale(pool, c, scales, 1e-5, 1e-8)

            @block.vector
            def _(dve):
                n = 0

                def step(instr):
                    nonlocal n
                    n += 1
                    instr.then_inc(prep, 1)
                    dve.wait_ge(prep, n)
                dve.wait_ge(w_in, 16)
                step(dve.tensor_reduce(sm[:, 0, :], raw[:, :, :], AX.X, ALU.add, apply_absolute_value=True))
                step(dve.tensor_scalar(sm[:, 1, :], sm[:, 0, :], 1.0 / D, None, ALU.mult))
                step(dve.tensor_scalar(sm[:, 2, :], sm[:, 1, :], 1e-8, None, ALU.add))
                step(dve.reciprocal(sm[:, 3, :], sm[:, 2, :]))
                for o in range(KC):
                    step(dve.tensor_scalar(wr[:, o, :], raw[:, o, :], sm[:, 3, o:o + 1], ROUND, ALU.mult, ALU.add))
                step(dve.tensor_scalar(wr[:, :, :], wr[:, :, :], -ROUND, 1.0, ALU.add, ALU.min))
                for o in range(KC):
                    step(dve.tensor_scalar(dg[:, o, :], c["identF"][:, :], sm[:, 1, o:o + 1], None, ALU.mult))
                step(dve.tensor_scalar(wt[:, :, :], wr[:, :, :], -1.0, None, ALU.max))
                for k in range(KC):
                    dve.wait_ge(w_tr, k + 1)
                    dve.tensor_copy(wT[:, k, :], TB[k % 2][:, 0:D]).then_inc(w_out, 1)
                for i, (dst, s) in enumerate(((grow, 2), (brow, 2))):
                    dve.wait_ge(rows, i + 1)
                    dve.tensor_scalar(dst[:, :], M[i][:, :], c["tg"][:, s:s + 1], None, ALU.mult).then_inc(rows_out, 1)

            @block.tensor
            def _(pe):
                pe.wait_ge(prep, 4 + KC + 1 + KC + 1)
                for k in range(KC):
                    if k >= 2:
                        pe.wait_ge(w_out, k - 1)
                    for o in range(KC):
                        i = pe.transpose(TB[k % 2][:, o * P:(o + 1) * P], wt[:, o, k * P:(k + 1) * P], c["identB"][:, :])
                    i.then_inc(w_tr, 1)
                for o in range(KC):
                    i = pe.matmul(M[0][:, o * P:(o + 1) * P], c["onesF"][:, :], dg[:, o, :], start=True, stop=True)
                i.then_inc(rows, 1)
                pe.wait_ge(b_in, 16)
                pe.matmul(M[1][:, :], c["onesF"][0:1, :], bias1[:, :], start=True, stop=True).then_inc(rows, 1)

        q_step = Count(sem("q_step"), 7 * PAIR)
        q_done = Count(sem("q_done"), PAIR)
        t_fill = Count(sem("ft_fill"), PAIR)
        t_out = Count(sem("ft_out"), PAIR, True)
        m_fill = Count(sem("fm_fill"), PAIR)
        m_out = Count(sem("fm_out"), PAIR, True)
        added = Count(sem("fadded"), 2 * PAIR, True)
        with nc.Block() as block:
            @block.vector
            def _(dve):
                m_out.grant(dve)
                with dve.Fori(0, NB // PAIR) as i:
                    n = 0

                    def step(instr):
                        nonlocal n
                        n += 1
                        instr.then_inc(q_step.sem, 1)
                        q_step.wait(dve, i, n)
                    for b in range(PAIR):
                        t = i * PAIR + b
                        t_fill.wait(dve, i, b + 1 - PAIR) if False else None
                        t_out.wait(dve, i, b + 1 - PAIR)
                        step(dve.tensor_scalar(u[:, b, :], X[:, t, :], c["mean"][:, bass.ds(t, 1)], c["rstd"][:, bass.ds(t, 1)],
                                               ALU.subtract, ALU.mult))
                        step(dve.tensor_reduce(sc[:, b, 0:1], u[:, b, :], AX.X, ALU.max, apply_absolute_value=True))
                        m_out.wait(dve, i, b + 1 - PAIR)
                        step(dve.tensor_scalar(sc[:, b, 1:2], sc[:, b, 0:1], 1.0 / 127.0, None, ALU.mult))
                        step(dve.tensor_scalar(sc[:, b, 2:3], sc[:, b, 1:2], 1e-8, None, ALU.add))
                        step(dve.reciprocal(sc[:, b, 3:4], sc[:, b, 2:3]))
                        step(dve.tensor_scalar(ur[:, b, :], u[:, b, :], sc[:, b, 3:4], ROUND, ALU.mult, ALU.add))
                        step(dve.tensor_scalar(uq[:, b, :], ur[:, b, :], -ROUND, None, ALU.add))
                    for b in range(PAIR):
                        m_fill.wait(dve, i, b + 1)
                        added.wait(dve, i, 2 * (b + 1 - PAIR))
                        dve.scalar_tensor_tensor(out=upd[:, b, :], in0=M[b][:, :], scalar=sc[:, b, 1:2], in1=grow[:, :],
                                                 op0=ALU.mult, op1=ALU.mult).then_inc(m_out.sem, 1)
                    for b in range(PAIR):
                        t = i * PAIR + b
                        added.wait(dve, i, 2 * (b + 1), c["passed_dve"])
                        dve.bn_stats(c["bst"][:, t, :], X[:, t, :])

            @block.gpsimd
            def _(pool):
                added.grant(pool)
                with pool.Fori(0, NB // PAIR) as i:
                    for b in range(PAIR):
                        t = i * PAIR + b
                        q_step.wait(pool, i, 7 * b + 1, c["passed_pool"])
                        pool.tensor_tensor(X[:, t, :], X[:, t, :], brow[:, :], ALU.add).then_inc(added.sem, 1)
                        m_out.wait(pool, i, b + 1, c["passed_pool"])
                        added.wait(pool, i, 2 * b + 1, c["passed_pool"])
                        pool.tensor_tensor(X[:, t, :], X[:, t, :], upd[:, b, :], ALU.add).then_inc(added.sem, 1)

            @block.scalar
            def _(act):
                t_out.grant(act)
                with act.Fori(0, NB // PAIR) as i:
                    for b in range(PAIR):
                        t_fill.wait(act, i, b + 1)
                        m_out.wait(act, i, b + 1 - PAIR)
                        act.activation(uT[:, b, :], TB[b][:, 0:D], ACT.Copy).then_inc(t_out.sem, 1)

            @block.tensor
            def _(pe):
                with pe.Fori(0, NB // PAIR) as i:
                    for b in range(PAIR):
                        q_step.wait(pe, i, 7 * (b + 1))
                        t_out.wait(pe, i, b + 1 - PAIR)
                        for k in range(KC):
                            x_ = pe.transpose(TB[b][:, k * P:(k + 1) * P], uq[:, b, k * P:(k + 1) * P], c["identB"][:, :])
                        x_.then_inc(t_fill.sem, 1)
                    for b in range(PAIR):
                        t_out.wait(pe, i, b + 1)
                        m_out.wait(pe, i, b + 1 - PAIR)
                        for k in range(KC):
                            x_ = pe.matmul(M[b][:, :], uT[:, b, k * P:(k + 1) * P], wT[:, k, :], start=k == 0, stop=k == KC - 1)
                        x_.then_inc(m_fill.sem, 1)


def attention_features(nc, c, ctx_in):
    X = c["X"]
    PAIR = 2
    with ExitStack() as st:
        def sb(name, shape, dt=F32):
            return st.enter_context(nc.sbuf_tensor(name, shape, dt))

        def sem(name):
            return st.enter_context(nc.semaphore(name))

        def bank(name, n):
            return [st.enter_context(nc.psum_tensor(f"{name}{i}", [P, 512], F32)) for i in range(n)]

        CX = sb("aCX", [P, PAIR, D])
        xn = sb("axn", [P, PAIR, D])
        q = sb("aq", [P, PAIR, 2, D], F32R)
        k_ = sb("ak", [P, PAIR, 2, D], F32R)
        vT = sb("avT", [P, PAIR, 2, D], F32R)
        sg = sb("asg", [P, 2, D])
        s = sb("as", [P, 2, 2, D], F32R)
        T, SC, O = bank("aT", 2), bank("aSC", 2), bank("aO", 2)
        scales = sem("a_scales")
        with nc.Block() as block:
            @block.gpsimd
            def _(pool):
                row_scale(pool, c, scales, 1e-5)
        c_in = [sem(f"ac_in{b}") for b in range(PAIR)]
        normed = Count(sem("a_normed"), PAIR)
        q_hi, k_hi, v_hi = (Count(sem(f"a_{n}"), PAIR) for n in ("q_hi", "k_hi", "v_hi"))
        q_lo, k_lo, v_lo = (Count(sem(f"a_{n}"), PAIR, n != "k_lo") for n in ("q_lo", "k_lo", "v_lo"))
        t_fill = Count(sem("at_fill"), PAIR)
        NS = PAIR * KC
        s_fill = Count(sem("as_fill"), NS)
        s_sig = Count(sem("as_sig"), NS, True)
        s_hi = Count(sem("as_hi"), NS)
        s_lo = Count(sem("as_lo"), NS, True)
        s_used = Count(sem("as_used"), NS, True)
        x_new = Count(sem("ax_new"), PAIR, True)
        with nc.Block() as block:
            @block.sync
            def _(sp):
                with sp.Fori(0, NB // PAIR) as i:
                    for b in range(PAIR):
                        s_used.wait(sp, i, KC * (b + 1) - NS, c["passed_sp"])
                        sp.dma_start(CX[:, b, :], ctx_in[bass.ds(i * PAIR + b, 1)].rearrange("b p d -> p (b d)"))\
                            .then_inc(c_in[b], 16)

            @block.vector
            def _(dve):
                for s_ in (s_lo, x_new, v_lo):
                    s_.grant(dve)
                with dve.Fori(0, NB // PAIR) as i:
                    def norm(b):
                        t = i * PAIR + b
                        q_lo.wait(dve, i, b + 1 - PAIR)
                        dve.tensor_scalar(xn[:, b, :], X[:, t, :], c["mean"][:, bass.ds(t, 1)], c["rstd"][:, bass.ds(t, 1)],
                                          ALU.subtract, ALU.mult).then_inc(normed.sem, 1)
                    norm(0)
                    norm(1)
                    for b in range(PAIR):
                        t = i * PAIR + b
                        v_hi.wait(dve, i, b + 1)
                        dve.tensor_tensor(vT[:, b, 1, :], T[b][:, :], vT[:, b, 0, :].bitcast(F32), ALU.subtract)\
                            .then_inc(v_lo.sem, 1)
                        for n in range(KC):
                            m = b * KC + n
                            s_sig.wait(dve, i, m + 1)
                            s_used.wait(dve, i, m - 1)
                            dve.tensor_copy(s[:, m % 2, 0, :], sg[:, m % 2, :]).then_inc(s_hi.sem, 1)
                            s_hi.wait(dve, i, m + 1)
                            dve.tensor_tensor(s[:, m % 2, 1, :], sg[:, m % 2, :], s[:, m % 2, 0, :].bitcast(F32),
                                              ALU.subtract).then_inc(s_lo.sem, 1)
                        s_used.wait(dve, i, KC * (b + 1))
                        dve.scalar_tensor_tensor(out=X[:, t, :], in0=O[b][:, :], scalar=c["tg"][:, 1:2], in1=X[:, t, :],
                                                 op0=ALU.mult, op1=ALU.add).then_inc(x_new.sem, 1)
                        x_new.wait(dve, i, b + 1, c["passed_dve"])
                        dve.bn_stats(c["bst"][:, t, :], X[:, t, :])

            @block.gpsimd
            def _(pool):
                q_lo.grant(pool)
                with pool.Fori(0, NB // PAIR) as i:
                    for b in range(PAIR):
                        q_hi.wait(pool, i, b + 1, c["passed_pool"])
                        pool.tensor_tensor(q[:, b, 1, :], xn[:, b, :], q[:, b, 0, :].bitcast(F32), ALU.subtract).then_inc(q_lo.sem, 1)
                        k_hi.wait(pool, i, b + 1, c["passed_pool"])
                        pool.tensor_tensor(k_[:, b, 1, :], CX[:, b, :], k_[:, b, 0, :].bitcast(F32), ALU.subtract).then_inc(k_lo.sem, 1)

            @block.scalar
            def _(act):
                s_sig.grant(act)
                with act.Fori(0, NB // PAIR) as i:
                    for b in range(PAIR):
                        s_used.wait(act, i, KC * (b + 1) - NS)
                        normed.wait(act, i, b + 1)
                        act.activation(q[:, b, 0, :], xn[:, b, :], ACT.Copy).then_inc(q_hi.sem, 1)
                        act.wait_ge(c_in[b], 16 * i + 16)
                        act.activation(k_[:, b, 0, :], CX[:, b, :], ACT.Copy).then_inc(k_hi.sem, 1)
                        t_fill.wait(act, i, b + 1)
                        act.activation(vT[:, b, 0, :], T[b][:, :], ACT.Copy).then_inc(v_hi.sem, 1)
                    for m in range(NS):
                        s_fill.wait(act, i, m + 1)
                        s_lo.wait(act, i, m - 1)
                        act.activation(sg[:, m % 2, :], SC[m % 2][:, :], ACT.Sigmoid, scale=SCALE1).then_inc(s_sig.sem, 1)

            @block.tensor
            def _(pe):
                s_used.grant(pe)
                with pe.Fori(0, NB // PAIR) as i:
                    for b in range(PAIR):
                        pe.wait_ge(c_in[b], 16 * i + 16)
                        v_lo.wait(pe, i, b + 1 - PAIR)
                        for k in range(KC):
                            x_ = pe.transpose(T[b][:, k * P:(k + 1) * P], CX[:, b, k * P:(k + 1) * P], c["identF"][:, :])
                        x_.then_inc(t_fill.sem, 1)

                    def score(m):
                        b, n = m // KC, m % KC
                        if n == 0:
                            q_lo.wait(pe, i, b + 1)
                            k_lo.wait(pe, i, b + 1)
                        s_sig.wait(pe, i, m - 1)
                        mm3(pe, SC[m % 2][:, :], lambda h: q[:, b, h, n * P:(n + 1) * P], lambda h: k_[:, b, h, :],
                            True, True).then_inc(s_fill.sem, 1)
                    score(0)
                    score(1)
                    for m in range(NS):
                        b, n = m // KC, m % KC
                        s_lo.wait(pe, i, m + 1)
                        if n == 0:
                            v_lo.wait(pe, i, b + 1)
                            x_new.wait(pe, i, b + 1 - PAIR)
                        mm3(pe, O[b][:, :], lambda h: vT[:, b, h, n * P:(n + 1) * P], lambda h: s[:, m % 2, h, :],
                            n == 0, n == KC - 1).then_inc(s_used.sem, 1)
                        if m + 2 < NS:
                            score(m + 2)


def route(dve, c, r, done, start):
    n = start

    def step(instr):
        nonlocal n
        n += 1
        instr.then_inc(done, 1)
        dve.wait_ge(done, n)
    T16 = [P, NB, E]
    s, sb_, big, eq, tri = r["s"], r["sb"], r["big"], r["eq"], r["tri"]
    step(dve.tensor_tensor(sb_[:, :, :], s[:, :, :], r["bias"][:, :].unsqueeze(1).to_broadcast(T16), ALU.add))

    def ranks(v, m, out):
        full = [P, NB, m, m]
        mine, other = v.unsqueeze(3).to_broadcast(full), v.unsqueeze(2).to_broadcast(full)
        a, b = (x_[:, 0:NB * m * m].rearrange("p (t i j) -> p t i j", t=NB, i=m) for x_ in (big, eq))
        step(dve.tensor_tensor(a, other, mine, ALU.is_gt))
        step(dve.tensor_tensor(b, other, mine, ALU.is_equal))
        step(dve.tensor_tensor(b, b, tri[:, 0:m, 0:m].unsqueeze(1).to_broadcast(full), ALU.mult))
        step(dve.tensor_tensor(a, a, b, ALU.add))
        step(dve.tensor_reduce(out, a, AX.X, ALU.add))
    gm, gr, gs = r["g"][:, 0, :, :], r["g"][:, 1, :, :], r["g"][:, 2, :, :]
    step(dve.tensor_reduce(gm, sb_[:, :, :].rearrange("p t (g e) -> p t g e", g=EG), AX.X, ALU.max))
    ranks(gm, EG, gr)
    step(dve.tensor_scalar(gr, gr, float(TOPG), None, ALU.is_lt))
    step(dve.tensor_scalar(gs, gr, -1.0, -MASKED, ALU.add, ALU.mult))
    in_groups = sb_[:, :, :].rearrange("p t (g e) -> p t g e", g=EG)
    wide = [P, NB, EG, E // EG]
    step(dve.tensor_tensor(in_groups, in_groups, gr.unsqueeze(3).to_broadcast(wide), ALU.mult))
    step(dve.tensor_tensor(in_groups, in_groups, gs.unsqueeze(3).to_broadcast(wide), ALU.add))
    ranks(sb_[:, :, :], E, r["rank"][:, :, :])
    step(dve.tensor_scalar(r["sel"][:, :, :], r["rank"][:, :, :], float(TOPK), None, ALU.is_lt))
    step(dve.tensor_tensor(sb_[:, :, :], s[:, :, :], r["sel"][:, :, :], ALU.mult))
    step(dve.tensor_reduce(r["sum"][:, 0, :], sb_[:, :, :], AX.X, ALU.add))
    step(dve.reciprocal(r["sum"][:, 1, :], r["sum"][:, 0, :]))
    step(dve.tensor_scalar(r["sum"][:, 1, :], r["sum"][:, 1, :], c["tg"][:, 3:4], None, ALU.mult))
    return step


def experts(nc, c, gate_w, ebias, w1, w2, w3, sw1, sw2, sw3, out):
    X = c["X"]
    with ExitStack() as st:
        def sb(name, shape, dt=F32):
            return st.enter_context(nc.sbuf_tensor(name, shape, dt))

        def sem(name):
            return st.enter_context(nc.semaphore(name))

        def bank(name, n):
            return [st.enter_context(nc.psum_tensor(f"{name}{i}", [P, 512], F32)) for i in range(n)]

        XT = sb("XT", [P, 2, KC, NB * S], F32R)
        cw = sb("cw", [P, NE, NB])
        with ExitStack() as st2:
            def sb2(name, shape, dt=F32):
                return st2.enter_context(nc.sbuf_tensor(name, shape, dt))
            xn = sb2("exn", [P, 2, D])
            gw = sb2("egw", [E, D])
            gwT = sb2("egwT", [P, 2, KC, E], F32R)
            b1 = sb2("eb1", [1, E])
            r = dict(s=sb2("r_s", [P, NB, E]), sb=sb2("r_sb", [P, NB, E]), big=sb2("r_big", [P, NB * E * E]),
                     eq=sb2("r_eq", [P, NB * E * E]), tri=sb2("r_tri", [P, E, E]), bias=sb2("r_bias", [P, E]),
                     g=sb2("r_g", [P, 3, NB, EG]), rank=sb2("r_rank", [P, NB, E]), sel=sb2("r_sel", [P, NB, E]),
                     sum=sb2("r_sum", [P, 2, NB]))
            T = [st2.enter_context(nc.psum_tensor(f"eT{i}", [P, 512], F32)) for i in range(2)]
            L = st2.enter_context(nc.psum_tensor("eL", [P, 512], F32))
            G = st2.enter_context(nc.psum_tensor("eG", [P, 512], F32))
            (g_in, scales, tri_ok, gt, g_hi, g_lo, bias_ps, normed, t_fill, t_hi, t_lo, logits, sig, routed) = (
                sem(f"e_{n}") for n in ("g_in", "scales", "tri", "gt", "g_hi", "g_lo", "bias_ps", "normed", "t_fill",
                                        "t_hi", "t_lo", "logits", "sig", "routed"))
            with nc.Block() as block:
                @block.gpsimd
                def _(pool):
                    n = row_scale(pool, c, scales, 1e-5)
                    pool.memset(r["tri"][:, :, :], 1.0).then_inc(tri_ok, 1)
                    pool.memset(cw[:, :, :], 1.0).then_inc(tri_ok, 1)
                    pool.wait_ge(tri_ok, 2)
                    pool.affine_select(out=r["tri"][:, :, :], in_=r["tri"][:, :, :], compare_op=ALU.is_gt, fill=0.0,
                                       base=0, pattern=[[1, E], [-1, E]], channel_multiplier=0).then_inc(tri_ok, 1)

                @block.sync
                def _(sp):
                    sp.dma_start(gw[:, :], gate_w).then_inc(g_in, 16)
                    sp.dma_start(b1[:, :], ebias.rearrange("(a n) -> a n", a=1)).then_inc(g_in, 16)

                @block.tensor
                def _(pe):
                    pe.wait_ge(g_in, 32)
                    for k in range(KC):
                        i = pe.transpose(G[:, k * E:(k + 1) * E], gw[:, k * P:(k + 1) * P], c["identF"][0:E, 0:E])
                    i.then_inc(gt, 1)
                    pe.matmul(L[:, 0:E], c["onesF"][0:1, :], b1[:, :], start=True, stop=True).then_inc(bias_ps, 1)
                    pe.wait_ge(g_lo, 1)

                    def logit(t):
                        pe.wait_ge(t_lo, t + 1)
                        if t == 0:
                            pe.wait_ge(tri_ok, 3)
                            pe.wait_ge(routed, 1)
                        for k in range(KC):
                            i = mm3(pe, L[:, t * E:(t + 1) * E], lambda h: XT[:, h, k, t * P:(t + 1) * P],
                                    lambda h: gwT[:, h, k, :], k == 0, k == KC - 1)
                        i.then_inc(logits, 1)
                    for t in range(NB):
                        pe.wait_ge(normed, t + 1)
                        if t >= 2:
                            pe.wait_ge(t_lo, t - 1)
                            pe.wait_ge(t_hi, t - 1)
                        for k in range(KC):
                            i = pe.transpose(T[t % 2][:, k * P:(k + 1) * P], xn[:, t % 2, k * P:(k + 1) * P], c["identF"][:, :])
                        i.then_inc(t_fill, 1)
                        if t:
                            logit(t - 1)
                    logit(NB - 1)

                @block.scalar
                def _(act):
                    act.wait_ge(gt, 1)
                    act.activation(gwT[:, 0, :, :], G[:, 0:KC * E].rearrange("p (k e) -> p k e", k=KC), ACT.Copy).then_inc(g_hi, 1)
                    for t in range(NB):
                        act.wait_ge(t_fill, t + 1)
                        act.activation(XT[:, 0, :, t * P:(t + 1) * P], T[t % 2][:, :].rearrange("p (k n) -> p k n", k=KC),
                                       ACT.Copy).then_inc(t_hi, 1)
                    act.wait_ge(logits, NB)
                    act.activation(r["s"][:, :, :], L[:, 0:NB * E].rearrange("p (t e) -> p t e", t=NB), ACT.Sigmoid)\
                        .then_inc(sig, 1)

                @block.vector
                def _(dve):
                    dve.wait_ge(g_hi, 1)
                    dve.tensor_tensor(gwT[:, 1, :, :], G[:, 0:KC * E].rearrange("p (k e) -> p k e", k=KC),
                                      gwT[:, 0, :, :].bitcast(F32), ALU.subtract).then_inc(g_lo, 1)
                    dve.wait_ge(bias_ps, 1)
                    dve.tensor_copy(r["bias"][:, :], L[:, 0:E]).then_inc(routed, 1)
                    dve.wait_ge(scales, 10)
                    for t in range(NB):
                        if t >= 2:
                            dve.wait_ge(t_fill, t - 1)
                        dve.tensor_scalar(xn[:, t % 2, :], X[:, t, :], c["mean"][:, bass.ds(t, 1)], c["rstd"][:, t:t + 1],
                                          ALU.subtract, ALU.mult).then_inc(normed, 1)
                        dve.wait_ge(t_hi, t + 1)
                        dve.tensor_tensor(XT[:, 1, :, t * P:(t + 1) * P], T[t % 2][:, :].rearrange("p (k n) -> p k n", k=KC),
                                          XT[:, 0, :, t * P:(t + 1) * P].bitcast(F32), ALU.subtract).then_inc(t_lo, 1)
                    dve.wait_ge(sig, 1)
                    step = route(dve, c, r, routed, 1)
                    step(dve.tensor_tensor(cw[:, 2:NE, :], r["sb"][:, :, :].rearrange("p t e -> p e t"),
                                           r["sum"][:, 1, :].unsqueeze(1).to_broadcast([P, E, NB]), ALU.mult))
                    step(dve.tensor_scalar(cw[:, 0:2, :], cw[:, 0:2, :], c["tg"][:, 3:4], None, ALU.mult))

        r1, r3, r2 = sb("er1", [P, KC, I]), sb("er3", [P, KC, I]), sb("er2", [P, 3, D])
        W1 = [sb(f"eW1{i}", [P, 2, KC, I], F32R) for i in range(2)]
        W3 = [sb(f"eW3{i}", [P, 2, KC, I], F32R) for i in range(2)]
        W2 = [sb(f"eW2{i}", [P, 2, 3, D], F32R) for i in range(2)]
        sl = sb("esl", [P, 2, D])
        h = sb("eh", [P, 1, D])
        hT = sb("ehT", [P, 2, 3, GT], F32R)
        A, B, Y = bank("eA", 2), bank("eB", 2), bank("eY", 2)
        w_in = sem("ew_in")
        w_split = Count(sem("ew_split"), 2 * 8)
        NU = 2 * NG
        ab_fill = Count(sem("eab_fill"), 3 * NU)
        a_out = Count(sem("ea_out"), 3 * NU)
        b_out = Count(sem("eb_out"), 3 * NU, True)
        h_hi = Count(sem("eh_hi"), 3 * NU)
        h_lo = Count(sem("eh_lo"), 3 * NU, True)
        y_fill = Count(sem("ey_fill"), GB * NU, True)
        y_out = Count(sem("ey_out"), GB * NU, True)
        stored = sem("stored")
        with nc.Block() as block:
            @block.sync
            def _(sp):
                def load(trip, b, a1, a3, a2):
                    if b:
                        sp.wait_ge(w_split.sem, 8 * b)
                    sp.dma_start(r1[:, :, :], a1.rearrange("(k p) i -> p k i", p=P)).then_inc(w_in, 16)
                    sp.dma_start(r3[:, :, :], a3.rearrange("(k p) i -> p k i", p=P)).then_inc(w_in, 16)
                    sp.dma_start(r2[:, 0:2, :], a2[0:2 * P, :].rearrange("(k p) i -> p k i", p=P)).then_inc(w_in, 16)
                    sp.dma_start(r2[0:IC[2], 2, :], a2[2 * P:I, :]).then_inc(w_in, 16)
                load(None, 0, sw1[:, 0:I], sw3[:, 0:I], sw2[0:I, :])
                load(0, 1, sw1[:, I:2 * I], sw3[:, I:2 * I], sw2[I:2 * I, :])
                with sp.Fori(0, E // 2) as i:
                    for b in range(2):
                        e = i * 2 + b
                        sp.wait_ge(w_split.sem, 16 * i + 16 + 8 * b)
                        sp.sem_inc(c["passed_sp"], 1)
                        sp.dma_start(r1[:, :, :], w1[bass.ds(e, 1)].rearrange("e (k p) i -> p (e k) i", p=P)).then_inc(w_in, 16)
                        sp.dma_start(r3[:, :, :], w3[bass.ds(e, 1)].rearrange("e (k p) i -> p (e k) i", p=P)).then_inc(w_in, 16)
                        sp.dma_start(r2[:, 0:2, :], w2[bass.ds(e, 1), 0:2 * P, :].rearrange("e (k p) i -> p (e k) i", p=P)).then_inc(w_in, 16)
                        sp.dma_start(r2[0:IC[2], 2, :], w2[bass.ds(e, 1), 2 * P:I, :].rearrange("e p i -> p (e i)")).then_inc(w_in, 16)
                sp.wait_ge(y_out.sem, GB * NU * (NE // 2 + 1))
                for q in range(NG):
                    sp.dma_start(out[q * GB:(q + 1) * GB].rearrange("b p d -> p b d"),
                                 X[:, q * GB:(q + 1) * GB, :]).then_inc(stored, 16)
                sp.wait_ge(stored, 16 * NG)

            @block.gpsimd
            def _(pool):
                with pool.Fori(0, NE // 2) as i:
                    for b in range(2):
                        pool.wait_ge(w_in, 128 * i + 64 * (b + 1))
                        pool.sem_inc(c["passed_pool"], 1)
                        y_fill.wait(pool, i, GB * NG * (b + 1) - GB * NU, c["passed_pool"])
                        n = 8 * b
                        for raw, dst, pp in ((r1[:, :, :], W1[b], P), (r3[:, :, :], W3[b], P), (r2[:, 0:2, :], W2[b], P),
                                             (r2[0:IC[2], 2:3, :], W2[b], IC[2])):
                            hi, lo = (dst[0:pp, j, 0:raw.shape[1], :] if pp == P else dst[0:pp, j, 2:3, :] for j in range(2))
                            pool.tensor_copy(hi, raw).then_inc(w_split.sem, 1)
                            n += 1
                            w_split.wait(pool, i, n, c["passed_pool"])
                            pool.tensor_tensor(lo, raw, hi.bitcast(F32), ALU.subtract).then_inc(w_split.sem, 1)
                            n += 1

            @block.tensor
            def _(pe):
                y_fill.grant(pe)
                with pe.Fori(0, NE // 2) as i:
                    def hidden(m):
                        u, ch = m // 3, m % 3
                        b, gr = u // NG, u % NG
                        if u % NG == 0 and ch == 0:
                            w_split.wait(pe, i, 8 * (b + 1))
                        b_out.wait(pe, i, m - 1)
                        cols = slice(ch * P, ch * P + IC[ch])
                        for W_, bk in ((W1[b], A[m % 2]), (W3[b], B[m % 2])):
                            for k in range(KC):
                                x_ = mm3(pe, bk[0:IC[ch], :], lambda j: W_[:, j, k, cols],
                                         lambda j: XT[:, j, k, gr * GT:(gr + 1) * GT], k == 0, k == KC - 1)
                        x_.then_inc(ab_fill.sem, 1)

                    def outer(u):
                        b = u // NG
                        h_lo.wait(pe, i, 3 * u + 3)
                        for t in range(GB):
                            n = u * GB + t
                            y_out.wait(pe, i, n - 1)
                            for ch in range(3):
                                x_ = mm3(pe, Y[n % 2][:, :], lambda j: hT[0:IC[ch], j, ch, t * P:(t + 1) * P],
                                         lambda j: W2[b][0:IC[ch], j, ch, :], ch == 0, ch == 2)
                            x_.then_inc(y_fill.sem, 1)
                    hidden(0)
                    for u in range(NU):
                        hidden(3 * u + 1)
                        hidden(3 * u + 2)
                        if u + 1 < NU:
                            hidden(3 * u + 3)
                        outer(u)

            @block.scalar
            def _(act):
                with act.Fori(0, NE // 2) as i:
                    def hi(m):
                        n = IC[m % 3]
                        b_out.wait(act, i, m + 1)
                        y_fill.wait(act, i, GB * (m // 3))
                        act.activation(hT[0:n, 0, m % 3, :], h[0:n, 0, :], ACT.Copy).then_inc(h_hi.sem, 1)
                    for m in range(3 * NU):
                        n = IC[m % 3]
                        ab_fill.wait(act, i, m + 1)
                        b_out.wait(act, i, m - 1)
                        act.activation(sl[0:n, m % 2, :], A[m % 2][0:n, :], ACT.Silu).then_inc(a_out.sem, 1)
                        hi(m)

            @block.vector
            def _(dve):
                for s_ in (b_out, h_lo, y_out):
                    s_.grant(dve)
                with dve.Fori(0, NE // 2) as i:
                    def mix(m):
                        n = IC[m % 3]
                        a_out.wait(dve, i, m + 1)
                        h_lo.wait(dve, i, m)
                        dve.tensor_tensor(h[0:n, 0, :], B[m % 2][0:n, :], sl[0:n, m % 2, :], ALU.mult).then_inc(b_out.sem, 1)

                    def lo(m):
                        n = IC[m % 3]
                        h_hi.wait(dve, i, m + 1)
                        dve.tensor_tensor(hT[0:n, 1, m % 3, :], h[0:n, 0, :], hT[0:n, 0, m % 3, :].bitcast(F32),
                                          ALU.subtract).then_inc(h_lo.sem, 1)
                    for u in range(NU):
                        for ch in range(3):
                            mix(3 * u + ch)
                            lo(3 * u + ch)
                        b, gr = u // NG, u % NG
                        for t in range(GB):
                            n = u * GB + t
                            y_fill.wait(dve, i, n + 1)
                            tt = gr * GB + t
                            e = i * 2 + b
                            dve.scalar_tensor_tensor(out=X[:, tt, :], in0=Y[n % 2][:, :], scalar=cw[:, bass.ds(e, 1), tt],
                                                     in1=X[:, tt, :], op0=ALU.mult, op1=ALU.add).then_inc(y_out.sem, 1)


_INS = ['x', 'ctx_2048', 'mask_BxS2_bk0', 'g_xattn', 'g_ffn', 'L0_xattn_norm_w', 'L0_xattn_wq', 'L0_xattn_wk',
        'L0_xattn_wv', 'L0_xattn_wo', 'L0_xattn_wg', 'L0_ffn_weight', 'L0_ffn_bias', 'L1_ffn_gate_w',
        'L1_ffn_expert_bias', 'L1_ffn_w1', 'L1_ffn_w2', 'L1_ffn_w3', 'L1_ffn_sw1', 'L1_ffn_sw2', 'L1_ffn_sw3']
_OUTS = [((NB, S, D), 'float32')]


def kernel(**inputs):
    import numpy as _np
    import concourse.bacc as _bacc
    from concourse import mybir as _mybir
    from concourse.bass_utils import run_bass_kernel_spmd as _run

    nc = _bacc.Bacc("TRN2", target_bir_lowering=False, num_devices=1)
    arrays, args = {}, []
    for name in _INS:
        a = _np.ascontiguousarray(inputs[name])
        arrays[f"in_{name}_dram"] = a
        args.append(nc.dram_tensor(f"in_{name}_dram", a.shape, _mybir.dt.from_np(a.dtype), kind="ExternalInput").ap())
    for i, (shape, dtype) in enumerate(_OUTS):
        args.append(nc.dram_tensor(f"out_{i}_dram", shape, _mybir.dt.from_np(_np.dtype(dtype)), kind="ExternalOutput").ap())
    program(nc, *args)
    r = _run(nc, [arrays], core_ids=[0])
    return r.results[0]["out_0_dram"]
```

```python
from contextlib import ExitStack

import concourse.bass as bass
from concourse import mybir

ALU = mybir.AluOpType
ACT = mybir.ActivationFunctionType
AX = mybir.AxisListType
F32 = mybir.dt.float32
F32R = mybir.dt.float32r
BF16 = mybir.dt.bfloat16
U8 = mybir.dt.uint8
U32 = mybir.dt.uint32
I32 = mybir.dt.int32

P = 128
NB, S, D = 16, 128, 512
KC = D // P
GB = 4
NG = NB // GB
GT = GB * S
NH, HD = 16, 32
HQ = P // HD
SCALE0 = float(HD) ** -0.5
SCALE1 = float(S) ** -0.5
MASKED = -1.0e30
ROUND = 1.5 * 2.0 ** 23
E, I, TOPK = 16, 352, 4
EG, TOPG = 4, 2
T_ALL = NB * S
NT = T_ALL * TOPK // P + E
PADS = P
NSH = 2
UT = 4
IC = [P, P, I - 2 * P]


class Count:

    def __init__(self, sem, per, credit=False, before=0):
        self.sem, self.per, self.base = sem, per, before + (per if credit else 0)

    def grant(self, eng):
        eng.sem_inc(self.sem, self.per)

    def wait(self, eng, trip, k, own=None):
        eng.wait_ge(self.sem, trip * self.per + (self.base + k))
        if own is not None:
            eng.sem_inc(own, 1)


def mm3(pe, out, lhs, rhs, first, last):
    pe.matmul(out, lhs(0), rhs(0), start=first, stop=False)
    pe.matmul(out, lhs(0), rhs(1), start=False, stop=False)
    return pe.matmul(out, lhs(1), rhs(0), start=False, stop=last)


def program(nc, x, ctx_in, mask, g_x, g_f, norm_w, wq, wk, wv, wo, wg, fw, fb,
            gate_w, ebias, w1, w2, w3, sw1, sw2, sw3, out):
    with ExitStack() as top:
        def sb(name, shape, dt=F32):
            return top.enter_context(nc.sbuf_tensor(name, shape, dt))

        X = sb("X", [P, NB, D])
        bst = sb("bst", [P, NB, 6])
        mean = sb("mean", [P, NB])
        rstd = sb("rstd", [P, NB])
        tmp16 = sb("tmp16", [P, 11, NB])
        identF = sb("identF", [P, P])
        identB = sb("identB", [P, P], BF16)
        onesF = sb("onesF", [P, P])
        onesB = sb("onesB", [P, P], BF16)
        nhalf = sb("nhalf", [P, NB])
        tg = sb("tg", [P, 4])
        parts = dict(X=X, bst=bst, mean=mean, rstd=rstd, tmp16=tmp16, identF=identF, identB=identB, onesF=onesF,
                     onesB=onesB, nhalf=nhalf, tg=tg)
        for e in ("pool", "sp", "dve", "act"):
            parts[f"passed_{e}"] = top.enter_context(nc.semaphore(f"passed_{e}"))
        start_up(nc, parts, x, g_x, g_f)
        attention_heads(nc, parts, ctx_in, mask, norm_w, wq, wk, wv, wo, wg)
        ternary_ffn(nc, parts, fw, fb)
        attention_features(nc, parts, ctx_in)
        experts(nc, parts, gate_w, ebias, w1, w2, w3, sw1, sw2, sw3, out)


def start_up(nc, c, x, g_x, g_f):
    with ExitStack() as st:
        def sem(name):
            return st.enter_context(nc.semaphore(name))
        gr = st.enter_context(nc.sbuf_tensor("gr", [1, 4], F32))
        gp = st.enter_context(nc.psum_tensor("gp", [P, 512], F32))
        x_in, g_in = [sem(f"x_in{q}") for q in range(NG)], sem("g_in")
        zeroed, consts, stats, gates_bc, seen = sem("zeroed"), sem("consts"), sem("stats"), sem("gates_bc"), sem("seen")
        block = st.enter_context(nc.Block())

        @block.sync
        def _(sp):
            sp.dma_start(gr[:, 0:2], g_x.rearrange("(a n) -> a n", a=1)).then_inc(g_in, 16)
            sp.dma_start(gr[:, 2:4], g_f.rearrange("(a n) -> a n", a=1)).then_inc(g_in, 16)
            for q in range(NG):
                sp.dma_start(c["X"][:, q * GB:(q + 1) * GB, :],
                             x[q * GB:(q + 1) * GB].rearrange("b p d -> p b d")).then_inc(x_in[q], 16)

        @block.gpsimd
        def _(pool):
            pool.memset(c["identF"][:, :], 0.0).then_inc(zeroed, 1)
            pool.memset(c["identB"][:, :], 0.0).then_inc(zeroed, 1)
            pool.memset(c["onesF"][:, :], 1.0).then_inc(consts, 1)
            pool.memset(c["onesB"][:, :], 1.0).then_inc(consts, 1)
            pool.memset(c["nhalf"][:, :], -0.5).then_inc(consts, 1)
            pool.wait_ge(zeroed, 2)
            for m in (c["identF"], c["identB"]):
                pool.affine_select(out=m[:, :], in_=m[:, :], compare_op=ALU.not_equal, fill=1.0,
                                   base=0, pattern=[[-1, P]], channel_multiplier=1).then_inc(consts, 1)

        @block.tensor
        def _(pe):
            pe.wait_ge(consts, 5)
            pe.wait_ge(g_in, 32)
            pe.matmul(gp[:, 0:4], c["onesF"][0:1, :], gr[0:1, :], start=True, stop=True).then_inc(gates_bc, 1)

        @block.scalar
        def _(act):
            act.wait_ge(gates_bc, 1)
            act.activation(c["tg"][:, :], gp[:, 0:4], ACT.Tanh).then_inc(seen, 1)

        @block.vector
        def _(dve):
            for t in range(NB):
                if t % GB == 0:
                    dve.wait_ge(x_in[t // GB], 16)
                dve.bn_stats(c["bst"][:, t, :], c["X"][:, t, :]).then_inc(stats, 1)


def row_scale(pool, c, done, eps, ms_eps=None):
    t = c["tmp16"]
    bst = c["bst"]
    var = t[:, 10, :]
    n = 0

    def step(instr):
        nonlocal n
        n += 1
        instr.then_inc(done, 1)
        pool.wait_ge(done, n)
    step(pool.tensor_tensor(t[:, 6, :], bst[:, :, 1], bst[:, :, 4], ALU.add))
    step(pool.tensor_scalar(c["mean"][:, :], t[:, 6, :], 0.5, None, ALU.mult))
    step(pool.tensor_tensor(t[:, 7, :], bst[:, :, 1], bst[:, :, 4], ALU.subtract))
    step(pool.tensor_scalar(t[:, 7, :], t[:, 7, :], 0.5, None, ALU.mult))
    step(pool.tensor_tensor(t[:, 7, :], t[:, 7, :], t[:, 7, :], ALU.mult))
    step(pool.tensor_tensor(t[:, 8, :], bst[:, :, 2], bst[:, :, 5], ALU.add))
    step(pool.tensor_scalar(t[:, 9, :], t[:, 8, :], 1.0 / D, None, ALU.mult))
    step(pool.tensor_tensor(var, t[:, 9, :], t[:, 7, :], ALU.add))
    step(pool.tensor_scalar(t[:, 0, :], var, eps, None, ALU.add))
    if ms_eps is None:
        step(pool.tensor_tensor(c["rstd"][:, :], t[:, 0, :], c["nhalf"][:, :], ALU.pow))
        return n
    step(pool.tensor_tensor(t[:, 1, :], t[:, 0, :], c["nhalf"][:, :], ALU.pow))
    step(pool.tensor_tensor(t[:, 2, :], t[:, 1, :], t[:, 1, :], ALU.mult))
    step(pool.tensor_tensor(t[:, 3, :], t[:, 2, :], var, ALU.mult))
    step(pool.tensor_scalar(t[:, 4, :], t[:, 3, :], ms_eps, None, ALU.add))
    step(pool.tensor_tensor(t[:, 5, :], t[:, 4, :], c["nhalf"][:, :], ALU.pow))
    step(pool.tensor_tensor(c["rstd"][:, :], t[:, 1, :], t[:, 5, :], ALU.mult))
    return n


def attention_heads(nc, c, ctx_in, mask, norm_w, wq, wk, wv, wo, wg):
    X, identF = c["X"], c["identF"]
    with ExitStack() as st:
        def sb(name, shape, dt=F32):
            return st.enter_context(nc.sbuf_tensor(name, shape, dt))

        def sem(name):
            return st.enter_context(nc.semaphore(name))

        def bank(name, n):
            return [st.enter_context(nc.psum_tensor(f"{name}{i}", [P, 512], F32)) for i in range(n)]

        W = [sb(f"W{n}", [P, 2, KC, D], F32R) for n in "qkvgo"]
        WQ, WK, WV, WG, WO = W
        nw = sb("nw", [P, KC])
        hg = sb("hg", [P, 1])
        mcol = sb("mcol", [P, NB])
        mrow = sb("mrow", [P, GB, S], BF16)
        CT = sb("CT", [P, 2, GB // 2, D])
        xn = sb("xn", [P, 2, D])
        xT = sb("xT", [P, 2, 2, KC, GT // 2], F32R)
        cT = sb("cT", [P, 2, 2, KC, GT // 2], F32R)
        qT = sb("qT", [P, 2, KC, GT // 2])
        kT = sb("kT", [P, 2, KC, GT // 2])
        va = sb("va", [P, 2, NH, HD + 1])
        gs = sb("gs", [P, 2, D])
        pr = sb("pr", [P, 2, HQ, S])
        pT = sb("pT", [P, 2, HQ, S])
        mx = sb("mx", [P, 2, HQ])
        rs = sb("rs", [P, 2, 2, HQ])
        o = sb("o", [P, 2, D])
        oT = sb("oT", [P, 2, KC, S], F32R)
        upd = sb("upd", [P, 2, D])
        mask_u8 = sb("mask_u8", [NB, S], U8)
        mask_f = sb("mask_f", [NB, S])
        mask_all = sb("mask_all", [P, NB, S], U8)
        T, M, SC, O = bank("T", 2), bank("M", 2), bank("SC", 2), bank("O", 2)

        raw = [t_[:, :, :, :].rearrange("p a k t -> p (a k t)").rearrange("p (o k) -> p o k", o=KC) for t_ in (qT, kT)]
        names = [(WQ, wq, "norm"), (WK, wk, None), (WV, wv, None), (WG, wg, "norm"), (WO, wo, "gate")]

        def scale_of(how, kc):
            return nw[:, kc:kc + 1] if how == "norm" else hg[:, 0:1] if how == "gate" else 1.0
        w_in = [sem(f"w_in{i}") for i in range(2)]
        nw_in, mask_in, w_tr, w_hi, w_lo = sem("nw_in"), sem("mask_in"), sem("w_tr"), sem("w_hi"), sem("w_lo")
        m_ready, m_tr, m_col, scales = sem("m_ready"), sem("m_tr"), sem("m_col"), sem("scales")
        ones_set, hg_ready = sem("ones_set"), sem("hg_ready")
        with nc.Block() as block:
            @block.sync
            def _(sp):
                sp.dma_start(mask_u8[:, :], mask).then_inc(mask_in, 16)
                with nc.allow_non_contiguous_dma(reason="512 scales once"):
                    sp.dma_start(nw[:, :], norm_w.rearrange("(k p) -> p k", p=P)).then_inc(nw_in, 16)
                for n, (_, w, _) in enumerate(names):
                    if n >= 2:
                        sp.wait_ge(w_tr, KC * (n - 1))
                    sp.dma_start(raw[n % 2][:, :, :], w.rearrange("(o p) k -> p o k", p=P)).then_inc(w_in[n % 2], 16)

            @block.gpsimd
            def _(pool):
                pool.tensor_scalar(hg[:, :], c["tg"][:, 0:1], 0.5, None, ALU.mult).then_inc(hg_ready, 1)
                row_scale(pool, c, scales, 1e-5, 1e-6)
                for b in range(2):
                    pool.memset(va[:, b, :, HD:HD + 1], 1.0).then_inc(ones_set, 1)

            @block.tensor
            def _(pe):
                for n in range(len(names)):
                    pe.wait_ge(w_in[n % 2], 16 * (n // 2 + 1))
                    for kc in range(KC):
                        f = KC * n + kc
                        if f >= 2:
                            pe.wait_ge(w_hi, f - 1)
                            pe.wait_ge(w_lo, f - 1)
                        for oc in range(KC):
                            m = pe.transpose(T[f % 2][:, oc * P:(oc + 1) * P],
                                             raw[n % 2][:, oc, kc * P:(kc + 1) * P], identF[:, :])
                        m.then_inc(w_tr, 1)
                pe.wait_ge(m_ready, 1)
                pe.transpose(M[0][:, 0:NB], mask_f[:, :], identF[0:NB, 0:NB]).then_inc(m_tr, 1)

            @block.scalar
            def _(act):
                act.wait_ge(nw_in, 16)
                act.wait_ge(hg_ready, 1)
                for n, (dst, _, normed) in enumerate(names):
                    for kc in range(KC):
                        f = KC * n + kc
                        act.wait_ge(w_tr, f + 1)
                        act.activation(dst[:, 0, kc, :], T[f % 2][:, :], ACT.Copy,
                                       scale=scale_of(normed, kc)).then_inc(w_hi, 1)

            @block.vector
            def _(dve):
                dve.wait_ge(mask_in, 16)
                dve.tensor_copy(mask_f[:, :], mask_u8[:, :]).then_inc(m_ready, 1)
                dve.wait_ge(nw_in, 16)
                dve.wait_ge(hg_ready, 1)
                for n, (dst, _, normed) in enumerate(names):
                    for kc in range(KC):
                        f = KC * n + kc
                        dve.wait_ge(w_hi, f + 1)
                        dve.scalar_tensor_tensor(out=dst[:, 1, kc, :], in0=T[f % 2][:, :],
                                                 scalar=scale_of(normed, kc),
                                                 in1=dst[:, 0, kc, :].bitcast(F32), op0=ALU.mult,
                                                 op1=ALU.subtract).then_inc(w_lo, 1)
                dve.wait_ge(m_tr, 1)
                dve.tensor_copy(mcol[:, :], M[0][:, 0:NB]).then_inc(m_col, 1)

        def prep(grp):
            return [[("xT", grp, 0), ("cT", grp, 0)], [("xT", grp, 1), ("cT", grp, 1)]] + \
                [[(n, grp, i)] for n in "qk" for i in range(KC)]

        NQ = GB * HQ
        ahead = {0: prep(1), GB // 2: prep(2)}
        plan = []
        for b in range(GB):
            if b in ahead:
                todo = ahead[b]
            mine = [[("v", b)], [("g", b)], [("oT", b - 1)] if b else [], [("oP", b - 1)] if b else []]
            for r in range(HQ):
                n = b * HQ + r
                fill = list(mine[r])
                take = (1, 1, 2, 1, 1, 1, 2, 2)[n % 8] if b < GB - 1 else (1, 1, 1, 0)[r]
                for _ in range(min(take, len(todo))):
                    fill += todo.pop(0)
                plan += [("S", n)] + fill[:1]
                plan += [("pT", n - 1)] if n >= 1 else []
                plan += fill[1:]
                plan += [("pv", n - 2)] if n >= 2 else []
                if n >= 2 and (n - 2) % 2:
                    plan += [("on", (n - 2) // 2)]
        rest = [x_ for y_ in todo for x_ in y_]
        plan += rest[:1] + [("pT", NQ - 1)] + rest[1:2] + [("pv", NQ - 2)] + rest[2:] + [("pv", NQ - 1), ("on", NQ // 2 - 1),
                                                                              ("oT", GB - 1), ("oP", GB - 1)]
        prologue = [x_ for y_ in prep(2) for x_ in y_]

        T_KINDS, M_KINDS = ("xT", "cT", "pT", "oT"), ("q", "k", "v", "g", "oP")
        SPLIT, BY_ACT, BY_DVE = ("xT", "cT", "oT"), ("q", "k", "g"), ("v", "oP")

        def of(kinds, steps=None):
            return [s for s in (plan if steps is None else steps) if s[0] in kinds]

        def at(kinds, s):
            back = 0
            if s[0] in ("xT", "cT", "q", "k") and s[1] == 0:
                s, back = (s[0], 2, s[2]), 1
            elif s[0] in ("oT", "oP", "v", "g") and s[1] < 0:
                s, back = (s[0], s[1] + GB), 1
            elif s[0] in ("pT", "pv") and s[1] < 0:
                s, back = (s[0], s[1] + NQ), 1
            some = of(kinds)
            return some.index(s) + 1 - back * len(some)

        def upto(kinds, sub, n):
            some = of(kinds)
            if n >= 0:
                return len([s for s in some[:n] if s[0] in sub])
            return len([s for s in some[:n] if s[0] in sub]) - len(of(sub))

        assert len(of(T_KINDS)) % 2 == 0 and len(of(M_KINDS)) % 2 == 0
        c_in = [sem(f"c_in{q}") for q in range(2)]
        mask_all_in = sem("mask_all_in")
        mrow_ready = Count(sem("mrow_ready"), GB, before=GB)
        x_norm = Count(sem("x_norm"), GB, before=2)
        t_fill = Count(sem("t_fill"), len(of(T_KINDS)), True, 4)
        t_hi = Count(sem("t_hi"), len(of(T_KINDS)), True, 4)
        t_lo = Count(sem("t_lo"), len(of(SPLIT)), True, 4)
        m_fill = Count(sem("m_fill"), len(of(M_KINDS)), True, 2 * KC)
        m_act = Count(sem("m_act"), len(of(BY_ACT)), True, 2 * KC)
        m_dve = Count(sem("m_dve"), len(of(BY_DVE)), True)
        s_fill = Count(sem("s_fill"), NQ)
        s_max = Count(sem("s_max"), NQ)
        s_out = Count(sem("s_out"), NQ, True)
        p_exp = Count(sem("p_exp"), NQ)
        pv = Count(sem("pv"), NQ, True)
        o_rec = Count(sem("o_rec"), 2 * GB)
        o_norm = Count(sem("o_norm"), 2 * GB, True)
        added = Count(sem("added"), GB, True)
        HG = GB // 2
        GC = HG * S

        def tile_of(g, grp, j):
            return ((g + 1) * GB) % NB + j if grp == 2 else g * GB + grp * HG + j

        with nc.Block() as block:
            @block.sync
            def _(sp):
                def load(par, tile):
                    sp.dma_start(CT[:, par, :, :], ctx_in[bass.ds(tile, HG)].rearrange("b p d -> p b d"))\
                        .then_inc(c_in[par], 16)
                sp.dma_start(mask_all[:, :, :], mask.rearrange("(a b) m -> a b m", a=1).to_broadcast([P, NB, S]))\
                    .then_inc(mask_all_in, 16)
                load(0, 0)
                with sp.Fori(0, NG) as g:
                    for grp in (1, 2):
                        t_lo.wait(sp, g, at(SPLIT, ("cT", 1, HG - 1)) - len(of(SPLIT)) if grp == 1 else 0, c["passed_sp"])
                        load(grp % 2, tile_of(g, grp, 0))
                sp.wait_ge(c_in[0], 16 * (NG + 1))

            @block.gpsimd
            def _(pool):
                added.grant(pool)
                def add(b):
                    pool.tensor_tensor(X[:, g * GB + b, :], X[:, g * GB + b, :], upd[:, b % 2, :], ALU.add)\
                        .then_inc(added.sem, 1)
                with pool.Fori(0, NG) as g:
                    for b in range(GB):
                        m_dve.wait(pool, g, at(BY_DVE, ("oP", b)), c["passed_pool"])
                        add(b)

            @block.tensor
            def _(pe):
                def transposes(s, g, n):
                    kind = s[0]
                    bk = T[(n - 1) % 2]
                    if kind == "xT":
                        src = lambda k: xn[:, s[2] % 2, k * P:(k + 1) * P]
                    elif kind == "cT":
                        src = lambda k: CT[:, s[1] % 2, s[2], k * P:(k + 1) * P]
                    elif kind == "pT":
                        src = lambda k: pr[:, s[1] % 2, k, :]
                    else:
                        src = lambda k: o[:, s[1] % 2, k * P:(k + 1) * P]
                    for k in range(KC):
                        i = pe.transpose(bk[:, k * P:(k + 1) * P], src(k), identF[:, :])
                    i.then_inc(t_fill.sem, 1)

                def project(s, n):
                    kind, bk = s[0], M[(n - 1) % 2]
                    if kind in ("q", "k"):
                        w, a = (WQ, xT) if kind == "q" else (WK, cT)
                        for k in range(KC):
                            i = mm3(pe, bk[:, 0:GC], lambda h: w[:, h, k, s[2] * P:(s[2] + 1) * P],
                                    lambda h: a[:, s[1] % 2, h, k, :], k == 0, k == KC - 1)
                    else:
                        b = s[1]
                        w = {"v": WV, "g": WG, "oP": WO}[kind]
                        cols = slice(b % HG * S, b % HG * S + S)
                        for k in range(KC):
                            lhs = {"v": lambda h: cT[:, b // HG, h, k, cols], "g": lambda h: xT[:, b // HG, h, k, cols],
                                   "oP": lambda h: oT[:, h, k, :]}[kind]
                            i = mm3(pe, bk[:, :], lhs, lambda h: w[:, h, k, :], k == 0, k == KC - 1)
                    i.then_inc(m_fill.sem, 1)
                for s_ in (t_fill, m_fill, pv):
                    s_.grant(pe)
                tf = mf = 0
                for s in prologue:
                    if s[0] in T_KINDS:
                        tf += 1
                        t_hi.wait(pe, 0, tf - 2 - 4)
                        t_lo.wait(pe, 0, tf - 2 - 4)
                        if s[0] == "xT":
                            pe.wait_ge(x_norm.sem, s[2] + 1)
                        else:
                            pe.wait_ge(c_in[0], 16)
                        transposes(s, None, tf)
                    else:
                        mf += 1
                        if mf == 1:
                            t_hi.wait(pe, 0, 0)
                            t_lo.wait(pe, 0, 0)
                        m_act.wait(pe, 0, mf - 2 - 2 * KC)
                        project(s, mf)
                m_act.wait(pe, 0, 0)
                with pe.Fori(0, NG) as g:
                    tf = mf = 0
                    for s in plan:
                        kind = s[0]
                        if kind in T_KINDS:
                            tf += 1
                            t_hi.wait(pe, g, tf - 2)
                            t_lo.wait(pe, g, upto(T_KINDS, SPLIT, tf - 2))
                            if kind == "xT":
                                x_norm.wait(pe, g, (s[1] - 1) * HG + s[2] + 1)
                            if kind == "cT" and s[2] == 0:
                                pe.wait_ge(c_in[s[1] % 2], 16 * g + 16 * s[1])
                            if kind == "pT":
                                p_exp.wait(pe, g, s[1] + 1)
                            if kind == "oT":
                                o_norm.wait(pe, g, 2 * s[1] + 2)
                            transposes(s, g, tf)
                        elif kind in M_KINDS:
                            mf += 1
                            m_act.wait(pe, g, upto(M_KINDS, BY_ACT, mf - 2))
                            m_dve.wait(pe, g, upto(M_KINDS, BY_DVE, mf - 2))
                            if kind in ("q", "k") and s[2] == 0:
                                t_lo.wait(pe, g, at(SPLIT, ("cT", s[1], HG - 1)))
                            if kind in ("v", "g"):
                                t_lo.wait(pe, g, at(SPLIT, ("cT", s[1] // HG, HG - 1)))
                            if kind == "oP":
                                t_lo.wait(pe, g, at(SPLIT, ("oT", s[1])))
                            project(s, mf)
                        elif kind == "S":
                            n = s[1]
                            b, r = n // HQ, n % HQ * HD
                            bk = SC[n % 2]
                            s_out.wait(pe, g, n - 1)
                            if r == 0:
                                mrow_ready.wait(pe, g, b + 1 - GB)
                                m_act.wait(pe, g, at(BY_ACT, ("k", b // HG, KC - 1)))
                            pe.matmul(bk[:, :].rearrange("p (j m) -> p j m", j=HQ), c["onesB"][r:r + 1, :],
                                      mrow[r:r + 1, b:b + 1, :].to_broadcast([1, HQ, S]), start=True, stop=False)
                            cols = slice(b % HG * S, b % HG * S + S)
                            for j in range(KC):
                                i = pe.matmul(bk[:, j * S:(j + 1) * S], qT[r:r + HD, b // HG, j, cols],
                                              kT[r:r + HD, b // HG, j, cols], start=False, stop=j == KC - 1)
                            i.then_inc(s_fill.sem, 1)
                        elif kind == "pv":
                            n = s[1]
                            b, r = n // HQ, n % HQ
                            t_hi.wait(pe, g, at(T_KINDS, ("pT", n)))
                            if r == 0:
                                m_dve.wait(pe, g, at(BY_DVE, ("v", b)))
                            if r % 2 == 0:
                                o_norm.wait(pe, g, 2 * b + r // 2 - 1)
                            for j in range(KC):
                                col = (r % 2 * HQ + j) * (HD + 1)
                                i = pe.matmul(O[r // 2][:, col:col + HD + 1], pT[:, n % 2, j, :],
                                              va[:, b % 2, j * HQ + r, :], start=True, stop=True)
                            i.then_inc(pv.sem, 1)

            @block.scalar
            def _(act):
                t_hi.grant(act)
                m_act.grant(act)

                def evac(s, n):
                    kind, src = s[0], (T if s[0] in T_KINDS else M)[(n - 1) % 2][:, :]
                    if kind in ("xT", "cT"):
                        dst = (xT if kind == "xT" else cT)[:, s[1] % 2, 0, :, s[2] * S:(s[2] + 1) * S]
                        act.activation(dst, src.rearrange("p (k t) -> p k t", k=KC), ACT.Copy).then_inc(t_hi.sem, 1)
                    elif kind == "pT":
                        act.activation(pT[:, s[1] % 2, :, :].rearrange("p j m -> p (j m)"), src, ACT.Copy).then_inc(t_hi.sem, 1)
                    elif kind == "oT":
                        act.activation(oT[:, 0, :, :].rearrange("p k t -> p (k t)"), src, ACT.Copy).then_inc(t_hi.sem, 1)
                    elif kind == "g":
                        act.activation(gs[:, s[1] % 2, :], src, ACT.Tanh, scale=0.5).then_inc(m_act.sem, 1)
                    else:
                        act.activation((qT if kind == "q" else kT)[:, s[1] % 2, s[2], :], src[:, 0:GC], ACT.Copy)\
                            .then_inc(m_act.sem, 1)
                tf = mf = 0
                for s in prologue:
                    if s[0] in T_KINDS:
                        tf += 1
                        t_fill.wait(act, 0, tf - 4)
                        evac(s, tf)
                    else:
                        mf += 1
                        m_fill.wait(act, 0, mf - 2 * KC)
                        evac(s, mf)
                with act.Fori(0, NG) as g:
                    tf = mf = 0
                    for s in plan:
                        kind = s[0]
                        if kind in T_KINDS:
                            tf += 1
                            t_fill.wait(act, g, tf)
                            if kind in ("xT", "cT"):
                                if s[1] == 1:
                                    m_fill.wait(act, g, at(M_KINDS, ("g", -1)))
                                else:
                                    m_fill.wait(act, g, at(M_KINDS, ("g", HG - 1)))
                            elif kind == "pT":
                                pv.wait(act, g, s[1] - 1)
                            else:
                                m_fill.wait(act, g, at(M_KINDS, ("oP", s[1] - 1)))
                            evac(s, tf)
                        elif kind in M_KINDS:
                            mf += 1
                            if kind not in BY_ACT:
                                continue
                            m_fill.wait(act, g, mf)
                            if kind == "g":
                                m_dve.wait(act, g, at(BY_DVE, ("oP", s[1] - 2)))
                            else:
                                s_out.wait(act, g, 0 if s[1] == 1 else NQ // 2)
                            evac(s, mf)
                        elif kind == "S":
                            n = s[1]
                            s_out.wait(act, g, n + 1)
                            pp = pr[:, n % 2, :, :].rearrange("p j m -> p (j m)")
                            act.activation(pp, pp, ACT.Exp, scale=SCALE0).then_inc(p_exp.sem, 1)

            @block.vector
            def _(dve):
                for s_ in (t_lo, m_dve, s_out, o_norm):
                    s_.grant(dve)

                def norm(tile, j):
                    dve.tensor_scalar(xn[:, j % 2, :], X[:, tile, :], c["mean"][:, bass.ds(tile, 1)],
                                      c["rstd"][:, bass.ds(tile, 1)], ALU.subtract, ALU.mult).then_inc(x_norm.sem, 1)

                def lo(s, n):
                    src = T[(n - 1) % 2][:, :]
                    if s[0] == "oT":
                        hi_, lo_ = (oT[:, h, :, :].rearrange("p k t -> p (k t)") for h in range(2))
                    else:
                        a = xT if s[0] == "xT" else cT
                        hi_, lo_ = (a[:, s[1] % 2, h, :, s[2] * S:(s[2] + 1) * S] for h in range(2))
                        src = src.rearrange("p (k t) -> p k t", k=KC)
                    dve.tensor_tensor(lo_, src, hi_.bitcast(F32), ALU.subtract).then_inc(t_lo.sem, 1)

                def mask_row(tile, b):
                    dve.tensor_scalar(mrow[:, b:b + 1, :], mask_all[:, bass.ds(tile, 1), :],
                                      -1.0, -MASKED, ALU.add, ALU.mult).then_inc(mrow_ready.sem, 1)
                norm(0, 0)
                norm(1, 1)
                dve.wait_ge(mask_all_in, 16)
                for b in range(GB):
                    mask_row(b, b)
                tf = mf = 0
                for s in prologue:
                    if s[0] in T_KINDS:
                        tf += 1
                        t_hi.wait(dve, 0, tf - 4)
                        lo(s, tf)

                with dve.Fori(0, NG) as g:
                    tf = mf = 0
                    def stats(b):
                        added.wait(dve, g, b + 1, c["passed_dve"])
                        dve.bn_stats(c["bst"][:, g * GB + b, :], X[:, g * GB + b, :])

                    for s in plan:
                        kind = s[0]
                        if kind == "xT":
                            j = s[2]
                            t_fill.wait(dve, g, at(T_KINDS, ("xT", 1, j)) if s[1] == 2 else 0)
                            norm(tile_of(g, s[1], j), j)
                        if kind in T_KINDS:
                            tf += 1
                            if kind in SPLIT:
                                t_hi.wait(dve, g, tf)
                                lo(s, tf)
                        elif kind in M_KINDS:
                            mf += 1
                            if kind not in BY_DVE:
                                continue
                            b = s[1]
                            m_fill.wait(dve, g, mf)
                            if kind == "v":
                                pv.wait(dve, g, (b - 1) * HQ)
                                dve.tensor_scalar(va[:, b % 2, :, 0:HD],
                                                  M[(mf - 1) % 2][:, :].rearrange("p (h d) -> p h d", h=NH),
                                                  mcol[:, bass.ds(g * GB + b, 1)], None, ALU.mult).then_inc(m_dve.sem, 1)
                            else:
                                m_act.wait(dve, g, at(BY_ACT, ("g", b)))
                                added.wait(dve, g, b - 1)
                                dve.scalar_tensor_tensor(out=upd[:, b % 2, :], in0=gs[:, b % 2, :], scalar=1.0,
                                                         in1=M[(mf - 1) % 2][:, :], op0=ALU.add, op1=ALU.mult)\
                                    .then_inc(m_dve.sem, 1)
                                if b:
                                    stats(b - 1)
                        elif kind == "S":
                            n = s[1]
                            s_fill.wait(dve, g, n + 1)
                            sc = SC[n % 2][:, :].rearrange("p (j m) -> p j m", j=HQ)
                            dve.tensor_reduce(mx[:, n % 2, :], sc, AX.X, ALU.max).then_inc(s_max.sem, 1)
                            s_max.wait(dve, g, n + 1)
                            t_fill.wait(dve, g, at(T_KINDS, ("pT", n - 2)))
                            dve.tensor_tensor(pr[:, n % 2, :, :], sc, mx[:, n % 2, :].unsqueeze(2).to_broadcast([P, HQ, S]),
                                              ALU.subtract).then_inc(s_out.sem, 1)
                            if n % HQ == HQ - 1:
                                mask_row(tile_of(g, 2, n // HQ), n // HQ)
                        elif kind == "on":
                            n = s[1]
                            b, half = n // 2, n % 2
                            pv.wait(dve, g, 2 * n + 2)
                            ov = O[half][:, 0:2 * HQ * (HD + 1)].rearrange("p (r j d) -> p r j d", r=2, j=HQ)
                            dve.reciprocal(rs[:, half, :, :], ov[:, :, :, HD]).then_inc(o_rec.sem, 1)
                            o_rec.wait(dve, g, n + 1)
                            if half == 0:
                                t_fill.wait(dve, g, at(T_KINDS, ("oT", b - 2)))
                            oo = o[:, b % 2, :].rearrange("p (j r d) -> p r j d", j=KC, r=HQ)
                            dve.tensor_tensor(oo[:, 2 * half:2 * half + 2, :, :], ov[:, :, :, 0:HD],
                                              rs[:, half, :, :].unsqueeze(3).to_broadcast([P, 2, HQ, HD]),
                                              ALU.mult).then_inc(o_norm.sem, 1)
                    stats(GB - 1)


def ternary_ffn(nc, c, fw, fb):
    X = c["X"]
    PAIR = 2
    with ExitStack() as st:
        def sb(name, shape, dt=F32):
            return st.enter_context(nc.sbuf_tensor(name, shape, dt))

        def sem(name):
            return st.enter_context(nc.semaphore(name))

        def bank(name, n):
            return [st.enter_context(nc.psum_tensor(f"{name}{i}", [P, 512], F32)) for i in range(n)]

        raw = sb("fraw", [P, KC, D])
        sm = sb("fsm", [P, 4, KC])
        wr = sb("fwr", [P, KC, D])
        wt = sb("fwt", [P, KC, D], BF16)
        wT = sb("fwT", [P, KC, D], BF16)
        dg = sb("fdg", [P, KC, P])
        bias1 = sb("fbias", [1, D])
        grow = sb("fgrow", [P, D])
        brow = sb("fbrow", [P, D])
        u = sb("fu", [P, 2, PAIR, D])
        ur = sb("fur", [P, 2, PAIR, D])
        uT = sb("fuT", [P, 2, PAIR, D], BF16)
        sc = sb("fsc", [P, 2, 4, PAIR])
        upd = sb("fupd", [P, 2, PAIR, D])
        TB = bank("fTB", 4)
        M = bank("fM", 4)
        u_done = sem("f_u_done")
        w_in, b_in, prep, w_tr, w_out, rows, rows_out, scales = (sem(f"f_{n}") for n in (
            "w_in", "b_in", "prep", "w_tr", "w_out", "rows", "rows_out", "scales"))
        with nc.Block() as block:
            @block.sync
            def _(sp):
                sp.dma_start(raw[:, :, :], fw.rearrange("(o p) k -> p o k", p=P)).then_inc(w_in, 16)
                sp.dma_start(bias1[:, :], fb.rearrange("(a n) -> a n", a=1)).then_inc(b_in, 16)

            @block.gpsimd
            def _(pool):
                row_scale(pool, c, scales, 1e-5, 1e-8)

            @block.vector
            def _(dve):
                n = 0

                def step(instr):
                    nonlocal n
                    n += 1
                    instr.then_inc(prep, 1)
                    dve.wait_ge(prep, n)
                dve.wait_ge(w_in, 16)
                step(dve.tensor_reduce(sm[:, 0, :], raw[:, :, :], AX.X, ALU.add, apply_absolute_value=True))
                step(dve.tensor_scalar(sm[:, 1, :], sm[:, 0, :], 1.0 / D, None, ALU.mult))
                step(dve.tensor_scalar(sm[:, 2, :], sm[:, 1, :], 1e-8, None, ALU.add))
                step(dve.reciprocal(sm[:, 3, :], sm[:, 2, :]))
                for o in range(KC):
                    step(dve.tensor_scalar(wr[:, o, :], raw[:, o, :], sm[:, 3, o:o + 1], ROUND, ALU.mult, ALU.add))
                step(dve.tensor_scalar(wr[:, :, :], wr[:, :, :], -ROUND, 1.0, ALU.add, ALU.min))
                for o in range(KC):
                    step(dve.tensor_scalar(dg[:, o, :], c["identF"][:, :], sm[:, 1, o:o + 1], None, ALU.mult))
                step(dve.tensor_scalar(wt[:, :, :], wr[:, :, :], -1.0, None, ALU.max))
                for k in range(KC):
                    dve.wait_ge(w_tr, k + 1)
                    dve.tensor_copy(wT[:, k, :], TB[k % 2][:, :].bitcast(BF16)[:, 0:D]).then_inc(w_out, 1)
                for i, (dst, s) in enumerate(((grow, 2), (brow, 2))):
                    dve.wait_ge(rows, i + 1)
                    dve.tensor_scalar(dst[:, :], M[i][:, :], c["tg"][:, s:s + 1], None, ALU.mult).then_inc(rows_out, 1)

            @block.tensor
            def _(pe):
                pe.wait_ge(prep, 4 + KC + 1 + KC + 1)
                for k in range(KC):
                    if k >= 2:
                        pe.wait_ge(w_out, k - 1)
                    for o in range(KC):
                        i = pe.transpose(TB[k % 2][:, :].bitcast(BF16)[:, o * P:(o + 1) * P],
                                         wt[:, o, k * P:(k + 1) * P], c["identB"][:, :])
                    i.then_inc(w_tr, 1)
                for o in range(KC):
                    i = pe.matmul(M[0][:, o * P:(o + 1) * P], c["onesF"][:, :], dg[:, o, :], start=True, stop=True)
                i.then_inc(rows, 1)
                pe.wait_ge(b_in, 16)
                pe.matmul(M[1][:, :], c["onesF"][0:1, :], bias1[:, :], start=True, stop=True).then_inc(rows, 1)

        q_sc = Count(sem("q_sc"), 2)
        q_small = Count(sem("q_small"), 3 * 2)
        q_done = Count(sem("q_done"), 2 * PAIR, True)
        t_fill = Count(sem("ft_fill"), 2 * PAIR, True)
        t_out = Count(sem("ft_out"), 2 * PAIR, True)
        m_fill = Count(sem("fm_fill"), 2 * PAIR, True)
        m_out = Count(sem("fm_out"), 2 * PAIR, True)
        biased = Count(sem("f_biased"), 2 * PAIR)
        added = Count(sem("f_added"), 2 * PAIR, True)

        def of(g, p, b):
            return ((g + 1) * GB) % NB + b if p == 2 else (g * GB + NB - PAIR) % NB + b if p < 0 else g * GB + PAIR * p + b

        with nc.Block() as block:
            @block.vector
            def _(dve):
                m_out.grant(dve)
                q_done.grant(dve)

                def quantise(g, p):
                    par, k = p % 2, PAIR * p
                    for b in range(PAIR):
                        t = of(g, p, b)
                        dve.tensor_scalar(u[:, par, b, :], X[:, t, :], c["mean"][:, bass.ds(t, 1)], c["rstd"][:, bass.ds(t, 1)],
                                          ALU.subtract, ALU.mult).then_inc(u_done, 1)
                    dve.wait_ge(u_done, PAIR * (2 * g + p + 1))
                    dve.tensor_reduce(sc[:, par, 0, :], u[:, par, :, :], AX.X, ALU.max, apply_absolute_value=True)\
                        .then_inc(q_sc.sem, 1)
                    q_sc.wait(dve, g, p + 1)
                    for n, f in enumerate((lambda o, i: dve.tensor_scalar(o, i, 1.0 / 127.0, None, ALU.mult),
                                           lambda o, i: dve.tensor_scalar(o, i, 1e-8, None, ALU.add), dve.reciprocal)):
                        f(sc[:, par, n + 1, :], sc[:, par, n, :]).then_inc(q_small.sem, 1)
                        q_small.wait(dve, g, 3 * p + n + 1)
                    for b in range(PAIR):
                        t_fill.wait(dve, g, k + b + 1 - 2 * PAIR)
                        dve.tensor_scalar(ur[:, par, b, :], u[:, par, b, :], sc[:, par, 3, b:b + 1], ROUND, ALU.mult, ALU.add)\
                            .then_inc(q_done.sem, 1)
                quantise(0, 0)
                with dve.Fori(0, NG) as g:
                    for p in range(2):
                        quantise(g, p + 1)
                        for b in range(PAIR):
                            m_fill.wait(dve, g, PAIR * p + b + 1)
                            added.wait(dve, g, PAIR * (p - 2) + b + 1)
                            dve.scalar_tensor_tensor(out=upd[:, p, b, :], in0=M[PAIR * p + b][:, :], scalar=sc[:, p, 1, b:b + 1],
                                                     in1=grow[:, :], op0=ALU.mult, op1=ALU.mult).then_inc(m_out.sem, 1)
                        for b in range(PAIR):
                            t = of(g, p - 1, b)
                            added.wait(dve, g, PAIR * (p - 1) + b + 1, c["passed_dve"])
                            dve.bn_stats(c["bst"][:, t, :], X[:, t, :])
                for b in range(PAIR):
                    t = NB - PAIR + b
                    added.wait(dve, NG - 1, PAIR + b + 1)
                    dve.bn_stats(c["bst"][:, t, :], X[:, t, :])

            @block.gpsimd
            def _(pool):
                added.grant(pool)
                with pool.Fori(0, NG) as g:
                    for p in range(2):
                        for b in range(PAIR):
                            t, k = of(g, p, b), PAIR * p + b + 1
                            q_done.wait(pool, g, k, c["passed_pool"])
                            pool.tensor_tensor(X[:, t, :], X[:, t, :], brow[:, :], ALU.add).then_inc(biased.sem, 1)
                        for b in range(PAIR):
                            t, k = of(g, p, b), PAIR * p + b + 1
                            m_out.wait(pool, g, k, c["passed_pool"])
                            biased.wait(pool, g, k, c["passed_pool"])
                            pool.tensor_tensor(X[:, t, :], X[:, t, :], upd[:, p, b, :], ALU.add).then_inc(added.sem, 1)

            @block.scalar
            def _(act):
                t_out.grant(act)

                def uT_out(g, p):
                    for b in range(PAIR):
                        k = PAIR * p + b + 1
                        t_fill.wait(act, g, k)
                        m_fill.wait(act, g, k - 2 * PAIR)
                        act.activation(uT[:, p % 2, b, :], TB[(PAIR * p + b) % 4][:, :], ACT.Copy, bias=-ROUND)\
                            .then_inc(t_out.sem, 1)
                uT_out(0, 0)
                with act.Fori(0, NG) as g:
                    for p in range(2):
                        uT_out(g, p + 1)

            @block.tensor
            def _(pe):
                t_fill.grant(pe)
                m_fill.grant(pe)

                def transposes(g, p):
                    for b in range(PAIR):
                        k = PAIR * p + b + 1
                        q_done.wait(pe, g, k)
                        t_out.wait(pe, g, k - 2 * PAIR)
                        for j in range(KC):
                            x_ = pe.transpose(TB[(PAIR * p + b) % 4][:, j * P:(j + 1) * P], ur[:, p % 2, b, j * P:(j + 1) * P],
                                              c["identF"][:, :])
                        x_.then_inc(t_fill.sem, 1)
                transposes(0, 0)
                with pe.Fori(0, NG) as g:
                    for p in range(2):
                        transposes(g, p + 1)
                        for b in range(PAIR):
                            k = PAIR * p + b + 1
                            t_out.wait(pe, g, k)
                            m_out.wait(pe, g, k - 2 * PAIR)
                            for j in range(KC):
                                x_ = pe.matmul(M[PAIR * p + b][:, :], uT[:, p, b, j * P:(j + 1) * P], wT[:, j, :],
                                               start=j == 0, stop=j == KC - 1)
                            x_.then_inc(m_fill.sem, 1)


def attention_features(nc, c, ctx_in):
    X = c["X"]
    with ExitStack() as st:
        def sb(name, shape, dt=F32):
            return st.enter_context(nc.sbuf_tensor(name, shape, dt))

        def sem(name):
            return st.enter_context(nc.semaphore(name))

        def bank(name, n):
            return [st.enter_context(nc.psum_tensor(f"{name}{i}", [P, 512], F32)) for i in range(n)]

        CX = sb("aCX", [P, GB, D])
        xn = sb("axn", [P, 2, D])
        q = sb("aq", [P, 2, 2, D], F32R)
        k_ = sb("ak", [P, 2, 2, D], F32R)
        vT = sb("avT", [P, 2, 2, D], F32R)
        sg = sb("asg", [P, KC, D])
        s = sb("as", [P, KC, 2, D], F32R)
        T, SC, O = bank("aT", 2), bank("aSC", KC), bank("aO", 2)
        scales = sem("a_scales")
        with nc.Block() as block:
            @block.gpsimd
            def _(pool):
                row_scale(pool, c, scales, 1e-5)
        NS = GB * KC
        c_in = [sem(f"ac_in{b}") for b in range(GB)]
        normed, q_hi, k_hi, v_hi, q_lo, k_lo, t_fill = (
            Count(sem(f"a_{n}"), GB) for n in ("normed", "q_hi", "k_hi", "v_hi", "q_lo", "k_lo", "t_fill"))
        v_lo, x_new = Count(sem("a_v_lo"), GB, True), Count(sem("a_x_new"), GB, True)
        s_fill = Count(sem("as_fill"), NS)
        s_hi = Count(sem("as_hi"), NS, True)
        s_lo = Count(sem("as_lo"), NS, True)
        s_used = Count(sem("as_used"), NS, True)

        def tile_of(g, b):
            return g * GB + b if b < GB else ((g + 1) * GB) % NB + b - GB

        with nc.Block() as block:
            @block.sync
            def _(sp):
                def load(tile, b):
                    sp.dma_start(CX[:, b, :], ctx_in[bass.ds(tile, 1)].rearrange("b p d -> p (b d)")).then_inc(c_in[b], 16)
                for b in range(GB):
                    load(b, b)
                with sp.Fori(0, NG) as g:
                    for b in range(GB):
                        t_fill.wait(sp, g, b + 1, c["passed_sp"])
                        k_lo.wait(sp, g, b + 1, c["passed_sp"])
                        load(tile_of(g, b + GB), b)
                for b in range(GB):
                    sp.wait_ge(c_in[b], 16 * (NG + 1))

            @block.vector
            def _(dve):
                for s_ in (s_lo, x_new, v_lo):
                    s_.grant(dve)

                def norm(g, b):
                    t = tile_of(g, b)
                    dve.tensor_scalar(xn[:, b % 2, :], X[:, t, :], c["mean"][:, bass.ds(t, 1)], c["rstd"][:, bass.ds(t, 1)],
                                      ALU.subtract, ALU.mult).then_inc(normed.sem, 1)

                def v_low(g, b):
                    v_hi.wait(dve, g, b + 1)
                    dve.tensor_tensor(vT[:, b % 2, 1, :], T[b % 2][:, :], vT[:, b % 2, 0, :].bitcast(F32), ALU.subtract)\
                        .then_inc(v_lo.sem, 1)

                def s_low(g, m):
                    s_hi.wait(dve, g, m + 1)
                    dve.tensor_tensor(s[:, m % KC, 1, :], sg[:, m % KC, :], s[:, m % KC, 0, :].bitcast(F32), ALU.subtract)\
                        .then_inc(s_lo.sem, 1)
                norm(0, 0)
                norm(0, 1)
                v_low(0, 0)
                s_low(0, 0)
                s_low(0, 1)
                with dve.Fori(0, NG) as g:
                    for m in range(NS):
                        b, n = m // KC, m % KC
                        s_low(g, m + 2)
                        if n == 0:
                            q_lo.wait(dve, g, b + 1)
                            norm(g, b + 2)
                        if n == 2:
                            v_low(g, b + 1)
                        if n == KC - 1:
                            t = tile_of(g, b)
                            s_used.wait(dve, g, m + 1)
                            dve.scalar_tensor_tensor(out=X[:, t, :], in0=O[b % 2][:, :], scalar=c["tg"][:, 1:2], in1=X[:, t, :],
                                                     op0=ALU.mult, op1=ALU.add).then_inc(x_new.sem, 1)
                            x_new.wait(dve, g, b + 1, c["passed_dve"])
                            dve.bn_stats(c["bst"][:, t, :], X[:, t, :])

            @block.gpsimd
            def _(pool):
                def split(g, b):
                    pool.tensor_copy(k_[:, b % 2, 0, :], CX[:, b % GB, :]).then_inc(k_hi.sem, 1)
                    k_hi.wait(pool, g, b + 1, c["passed_pool"])
                    pool.tensor_tensor(k_[:, b % 2, 1, :], CX[:, b % GB, :], k_[:, b % 2, 0, :].bitcast(F32), ALU.subtract)\
                        .then_inc(k_lo.sem, 1)
                    q_hi.wait(pool, g, b + 1, c["passed_pool"])
                    pool.tensor_tensor(q[:, b % 2, 1, :], xn[:, b % 2, :], q[:, b % 2, 0, :].bitcast(F32), ALU.subtract)\
                        .then_inc(q_lo.sem, 1)
                for b in range(2):
                    pool.wait_ge(c_in[b], 16)
                    split(0, b)
                with pool.Fori(0, NG) as g:
                    for b in range(GB):
                        s_fill.wait(pool, g, (b + 1) * KC, c["passed_pool"])
                        pool.wait_ge(c_in[(b + 2) % GB], 16 * (g + 1) if b + 2 < GB else 16 * (g + 2))
                        pool.sem_inc(c["passed_pool"], 1)
                        split(g, b + 2)

            @block.scalar
            def _(act):
                s_hi.grant(act)

                def sigmoids(g, m):
                    s_fill.wait(act, g, m + 1)
                    s_lo.wait(act, g, m + 1 - KC)
                    act.activation(sg[:, m % KC, :], SC[m % KC][:, :], ACT.Sigmoid, scale=SCALE1)
                    s_used.wait(act, g, m + 1 - KC)
                    act.activation(s[:, m % KC, 0, :], SC[m % KC][:, :], ACT.Sigmoid, scale=SCALE1).then_inc(s_hi.sem, 1)

                def q_high(g, b):
                    normed.wait(act, g, b + 1)
                    act.activation(q[:, b % 2, 0, :], xn[:, b % 2, :], ACT.Copy).then_inc(q_hi.sem, 1)

                def v_high(g, b):
                    t_fill.wait(act, g, b + 1)
                    act.activation(vT[:, b % 2, 0, :], T[b % 2][:, :], ACT.Copy).then_inc(v_hi.sem, 1)
                q_high(0, 0)
                v_high(0, 0)
                q_high(0, 1)
                sigmoids(0, 0)
                sigmoids(0, 1)
                with act.Fori(0, NG) as g:
                    for m in range(NS):
                        b, n = m // KC, m % KC
                        sigmoids(g, m + 2)
                        if n == 2:
                            s_used.wait(act, g, b * KC)
                            v_high(g, b + 1)
                        if n == 3:
                            s_fill.wait(act, g, (b + 1) * KC)
                            q_high(g, b + 2)

            @block.tensor
            def _(pe):
                s_used.grant(pe)

                def transposes(g, b):
                    for k in range(KC):
                        x_ = pe.transpose(T[b % 2][:, k * P:(k + 1) * P], CX[:, b % GB, k * P:(k + 1) * P], c["identF"][:, :])
                    x_.then_inc(t_fill.sem, 1)

                def score(g, m):
                    b, n = m // KC, m % KC
                    if n == 0:
                        q_lo.wait(pe, g, b + 1)
                    mm3(pe, SC[m % KC][:, :], lambda h: q[:, b % 2, h, n * P:(n + 1) * P], lambda h: k_[:, b % 2, h, :],
                        True, True).then_inc(s_fill.sem, 1)
                pe.wait_ge(c_in[0], 16)
                transposes(0, 0)
                for m in range(3):
                    score(0, m)
                with pe.Fori(0, NG) as g:
                    for m in range(NS):
                        b, n = m // KC, m % KC
                        s_hi.wait(pe, g, m)
                        score(g, m + 3)
                        s_lo.wait(pe, g, m + 1)
                        if n == 0:
                            v_lo.wait(pe, g, b + 1)
                            x_new.wait(pe, g, b - 1)
                        mm3(pe, O[b % 2][:, :], lambda h: vT[:, b % 2, h, n * P:(n + 1) * P], lambda h: s[:, m % KC, h, :],
                            n == 0, n == KC - 1).then_inc(s_used.sem, 1)
                        if n == 1:
                            pe.wait_ge(c_in[(b + 1) % GB], 16 * (g + 1) if b + 1 < GB else 16 * (g + 2))
                            v_lo.wait(pe, g, b)
                            transposes(g, b + 1)


def route(dve, c, r, done, start):
    n = start

    def step(instr):
        nonlocal n
        n += 1
        instr.then_inc(done, 1)
        dve.wait_ge(done, n)
    T16 = [P, NB, E]
    s, sb_, big, eq, tri = r["s"], r["sb"], r["big"], r["eq"], r["tri"]
    step(dve.tensor_tensor(sb_[:, :, :], s[:, :, :], r["bias"][:, :].unsqueeze(1).to_broadcast(T16), ALU.add))

    def ranks(v, m, out):
        full = [P, NB, m, m]
        mine, other = v.unsqueeze(3).to_broadcast(full), v.unsqueeze(2).to_broadcast(full)
        a, b = (x_[:, 0:NB * m * m].rearrange("p (t i j) -> p t i j", t=NB, i=m) for x_ in (big, eq))
        step(dve.tensor_tensor(a, other, mine, ALU.is_gt))
        step(dve.tensor_tensor(b, other, mine, ALU.is_equal))
        step(dve.tensor_tensor(b, b, tri[:, 0:m, 0:m].unsqueeze(1).to_broadcast(full), ALU.mult))
        step(dve.tensor_tensor(a, a, b, ALU.add))
        step(dve.tensor_reduce(out, a, AX.X, ALU.add))
    gm, gr, gs = r["g"][:, 0, :, :], r["g"][:, 1, :, :], r["g"][:, 2, :, :]
    step(dve.tensor_reduce(gm, sb_[:, :, :].rearrange("p t (g e) -> p t g e", g=EG), AX.X, ALU.max))
    ranks(gm, EG, gr)
    step(dve.tensor_scalar(gr, gr, float(TOPG), None, ALU.is_lt))
    step(dve.tensor_scalar(gs, gr, -1.0, -MASKED, ALU.add, ALU.mult))
    in_groups = sb_[:, :, :].rearrange("p t (g e) -> p t g e", g=EG)
    wide = [P, NB, EG, E // EG]
    step(dve.tensor_tensor(in_groups, in_groups, gr.unsqueeze(3).to_broadcast(wide), ALU.mult))
    step(dve.tensor_tensor(in_groups, in_groups, gs.unsqueeze(3).to_broadcast(wide), ALU.add))
    ranks(sb_[:, :, :], E, r["rank"][:, :, :])
    step(dve.tensor_scalar(r["sel"][:, :, :], r["rank"][:, :, :], float(TOPK), None, ALU.is_lt))
    step(dve.tensor_tensor(sb_[:, :, :], s[:, :, :], r["sel"][:, :, :], ALU.mult))
    step(dve.tensor_reduce(r["sum"][:, 0, :], sb_[:, :, :], AX.X, ALU.add))
    step(dve.reciprocal(r["sum"][:, 1, :], r["sum"][:, 0, :]))
    step(dve.tensor_scalar(r["sum"][:, 1, :], r["sum"][:, 1, :], c["tg"][:, 3:4], None, ALU.mult))
    return step


def experts(nc, c, gate_w, ebias, w1, w2, w3, sw1, sw2, sw3, out):
    rows_d = nc.dram_tensor("rows_d", [T_ALL + PADS, D], F32, kind="Internal").ap()
    acc_d = nc.dram_tensor("acc_d", [T_ALL + PADS, D], F32, kind="Internal").ap()
    table_d = nc.dram_tensor("table_d", [NT * P, 2], F32, kind="Internal").ap()
    with ExitStack() as st:
        def sb(name, shape, dt=F32):
            return st.enter_context(nc.sbuf_tensor(name, shape, dt))
        m = dict(ej=sb("m_ej", [P, NT + 3]), meta=sb("m_meta", [1, 3, NT + 3], I32),
                 pos=sb("m_pos", [P, NB, 8]), posu=sb("m_posu", [P, NB, TOPK], U32),
                 pair=sb("m_pair", [P, NB, TOPK, 2]), rows_d=rows_d, acc_d=acc_d, table_d=table_d)
        with ExitStack() as st2:
            XT = st2.enter_context(nc.sbuf_tensor("XT", [P, 2, KC, NB * S], F32R))
            routing(nc, c, m, XT, gate_w, ebias)
            shared_expert(nc, c, m, XT, sw1, sw2, sw3)
        expert_tiles(nc, c, m, w1, w2, w3, out)


def routing(nc, c, m, XT, gate_w, ebias):
    X = c["X"]
    with ExitStack() as st2:
        def sem(name):
            return st2.enter_context(nc.semaphore(name))

        def sb2(name, shape, dt=F32):
            return st2.enter_context(nc.sbuf_tensor(name, shape, dt))
        NX = 4
        xn = sb2("exn", [P, NX, D])
        gw = sb2("egw", [E, D])
        gwT = sb2("egwT", [P, 2, KC, E], F32R)
        b1 = sb2("eb1", [1, E])
        zrow = sb2("zrow", [P, D])
        triB = sb2("r_triB", [P, P], BF16)
        selB = sb2("r_selB", [P, NB, E], BF16)
        iE = sb2("r_iE", [P, E])
        iJ = sb2("r_iJ", [P, NT + 3])
        pad = sb2("r_pad", [NT, P, 2])
        tok = sb2("r_tok", [P, NB])
        ti = sb2("r_ti", [P, NT + 3], I32)
        tp = sb2("r_tp", [NT, P], I32)
        r = dict(s=sb2("r_s", [P, NB, E]), sb=sb2("r_sb", [P, NB, E]), big=sb2("r_big", [P, NB * E * E]),
                 eq=sb2("r_eq", [P, NB * E * E]), tri=sb2("r_tri", [P, E, E]), bias=sb2("r_bias", [P, E]),
                 g=sb2("r_g", [P, 3, NB, EG]), rank=sb2("r_rank", [P, NB, E]), sel=sb2("r_sel", [P, NB, E]),
                 sum=sb2("r_sum", [P, 2, NB]), run=sb2("r_run", [P, 2, NB, E]), n=sb2("r_n", [P, 6, E]))
        T = [st2.enter_context(nc.psum_tensor(f"eT{i}", [P, 512], F32)) for i in range(2)]
        L = st2.enter_context(nc.psum_tensor("eL", [P, 512], F32))
        G = st2.enter_context(nc.psum_tensor("eG", [P, 512], F32))
        CT_ = st2.enter_context(nc.psum_tensor("eC", [P, 512], F32))
        PT = st2.enter_context(nc.psum_tensor("eP", [P, 512], F32))
        (g_in, scales, tri_ok, gt, g_hi, g_lo, bias_ps, normed, t_fill, t_hi, t_lo, logits, sig, routed, iotas, counted,
         sel_ok, pads_in) = (
            sem(f"e_{n}") for n in ("g_in", "scales", "tri", "gt", "g_hi", "g_lo", "bias_ps", "normed", "t_fill",
                                    "t_hi", "t_lo", "logits", "sig", "routed", "iotas", "counted", "sel_ok", "pads_in"))
        row_out = [sem(f"e_row_out{b}") for b in range(NX)]
        with nc.Block() as block:
            @block.gpsimd
            def _(pool):
                row_scale(pool, c, scales, 1e-5)
                n = 0

                def step(instr):
                    nonlocal n
                    n += 1
                    instr.then_inc(iotas, 1)
                    pool.wait_ge(iotas, n)
                pool.memset(r["tri"][:, :, :], 1.0).then_inc(tri_ok, 1)
                pool.memset(triB[:, :], 1.0).then_inc(tri_ok, 1)
                pool.wait_ge(tri_ok, 2)
                pool.affine_select(out=r["tri"][:, :, :], in_=r["tri"][:, :, :], compare_op=ALU.is_gt, fill=0.0,
                                   base=0, pattern=[[1, E], [-1, E]], channel_multiplier=0).then_inc(tri_ok, 1)
                pool.affine_select(out=triB[:, :], in_=triB[:, :], compare_op=ALU.is_gt, fill=0.0,
                                   base=0, pattern=[[1, P]], channel_multiplier=-1).then_inc(tri_ok, 1)
                step(pool.memset(zrow[:, :], 0.0))
                step(pool.memset(pad[:, :, :], 0.0))
                step(pool.iota(ti[:, :], pattern=[[1, NT + 3]], base=0, channel_multiplier=0))
                step(pool.tensor_copy(iJ[:, :], ti[:, :]))
                step(pool.tensor_copy(iE[:, :], ti[:, 0:E]))
                step(pool.iota(ti[:, 0:NB], pattern=[[P, NB]], base=0, channel_multiplier=1))
                step(pool.tensor_copy(tok[:, :], ti[:, 0:NB]))
                step(pool.iota(tp[:, :], pattern=[[1, P]], base=T_ALL, channel_multiplier=0))
                step(pool.tensor_copy(pad[:, :, 0], tp[:, :]))

            @block.sync
            def _(sp):
                sp.dma_start(gw[:, :], gate_w).then_inc(g_in, 16)
                sp.dma_start(b1[:, :], ebias.rearrange("(a n) -> a n", a=1)).then_inc(g_in, 16)
                for t in range(NB):
                    sp.wait_ge(normed, t + 1)
                    sp.dma_start(m["rows_d"][t * P:(t + 1) * P, :], xn[:, t % NX, :]).then_inc(row_out[t % NX], 16)
                sp.wait_ge(iotas, 9)
                sp.dma_start(m["rows_d"][T_ALL:T_ALL + PADS, :], zrow[:, :]).then_inc(pads_in, 16)
                sp.dma_start(m["acc_d"][T_ALL:T_ALL + PADS, :], zrow[:, :]).then_inc(pads_in, 16)
                sp.dma_start(m["table_d"].rearrange("(j p) a -> j (p a)", p=P), pad[:, :, :].rearrange("j p a -> j (p a)"))\
                    .then_inc(pads_in, 16)
                sp.wait_ge(pads_in, 48)
                for b in range(NX):
                    sp.wait_ge(row_out[b], 16 * NB // NX)

            @block.tensor
            def _(pe):
                pe.wait_ge(g_in, 32)
                for k in range(KC):
                    i = pe.transpose(G[:, k * E:(k + 1) * E], gw[:, k * P:(k + 1) * P], c["identF"][0:E, 0:E])
                i.then_inc(gt, 1)
                pe.matmul(L[:, 0:E], c["onesF"][0:1, :], b1[:, :], start=True, stop=True).then_inc(bias_ps, 1)
                pe.wait_ge(g_lo, 1)

                def logit(t):
                    pe.wait_ge(t_lo, t + 1)
                    if t == 0:
                        pe.wait_ge(tri_ok, 4)
                        pe.wait_ge(routed, 1)
                    for k in range(KC):
                        i = mm3(pe, L[:, t * E:(t + 1) * E], lambda h: XT[:, h, k, t * P:(t + 1) * P],
                                lambda h: gwT[:, h, k, :], k == 0, k == KC - 1)
                    i.then_inc(logits, 1)
                for t in range(NB):
                    pe.wait_ge(normed, t + 1)
                    if t >= 2:
                        pe.wait_ge(t_lo, t - 1)
                        pe.wait_ge(t_hi, t - 1)
                    for k in range(KC):
                        i = pe.transpose(T[t % 2][:, k * P:(k + 1) * P], xn[:, t % NX, k * P:(k + 1) * P], c["identF"][:, :])
                    i.then_inc(t_fill, 1)
                    if t:
                        logit(t - 1)
                logit(NB - 1)
                pe.wait_ge(sel_ok, 1)
                sel = selB[:, :, :].rearrange("p t e -> p (t e)")
                pe.matmul(PT[:, 0:NB * E], triB[:, :], sel, start=True, stop=True)
                pe.matmul(CT_[:, 0:NB * E], c["onesB"][:, :], sel, start=True, stop=True).then_inc(counted, 1)

            @block.scalar
            def _(act):
                act.wait_ge(gt, 1)
                act.activation(gwT[:, 0, :, :], G[:, 0:KC * E].rearrange("p (k e) -> p k e", k=KC), ACT.Copy).then_inc(g_hi, 1)
                for t in range(NB):
                    act.wait_ge(t_fill, t + 1)
                    act.activation(XT[:, 0, :, t * P:(t + 1) * P], T[t % 2][:, :].rearrange("p (k n) -> p k n", k=KC),
                                   ACT.Copy).then_inc(t_hi, 1)
                act.wait_ge(logits, NB)
                act.activation(r["s"][:, :, :], L[:, 0:NB * E].rearrange("p (t e) -> p t e", t=NB), ACT.Sigmoid)\
                    .then_inc(sig, 1)

            @block.vector
            def _(dve):
                dve.wait_ge(g_hi, 1)
                dve.tensor_tensor(gwT[:, 1, :, :], G[:, 0:KC * E].rearrange("p (k e) -> p k e", k=KC),
                                  gwT[:, 0, :, :].bitcast(F32), ALU.subtract).then_inc(g_lo, 1)
                dve.wait_ge(bias_ps, 1)
                dve.tensor_copy(r["bias"][:, :], L[:, 0:E]).then_inc(routed, 1)
                dve.wait_ge(scales, 10)
                for t in range(NB):
                    if t >= NX:
                        dve.wait_ge(t_fill, t - NX + 1)
                        dve.wait_ge(row_out[t % NX], 16 * (t // NX))
                    dve.tensor_scalar(xn[:, t % NX, :], X[:, t, :], c["mean"][:, t:t + 1], c["rstd"][:, t:t + 1],
                                      ALU.subtract, ALU.mult).then_inc(normed, 1)
                    dve.wait_ge(t_hi, t + 1)
                    dve.tensor_tensor(XT[:, 1, :, t * P:(t + 1) * P], T[t % 2][:, :].rearrange("p (k n) -> p k n", k=KC),
                                      XT[:, 0, :, t * P:(t + 1) * P].bitcast(F32), ALU.subtract).then_inc(t_lo, 1)
                dve.wait_ge(sig, 1)
                step = route(dve, c, r, routed, 1)
                dve.tensor_copy(selB[:, :, :], r["sel"][:, :, :]).then_inc(sel_ok, 1)
                T16 = [P, NB, E]
                step(dve.tensor_tensor(r["sb"][:, :, :], r["sb"][:, :, :], r["sum"][:, 1, :].unsqueeze(2).to_broadcast(T16),
                                       ALU.mult))
                dve.wait_ge(counted, 1)
                dve.wait_ge(iotas, 9)
                run = r["run"]
                step(dve.tensor_copy(run[:, 0, :, :], CT_[:, 0:NB * E].rearrange("p (t e) -> p t e", t=NB)))
                a = 0
                for d in (1, 2, 4, 8):
                    step(dve.tensor_copy(run[:, 1 - a, 0:d, :], run[:, a, 0:d, :]))
                    step(dve.tensor_tensor(run[:, 1 - a, d:NB, :], run[:, a, d:NB, :], run[:, a, 0:NB - d, :], ALU.add))
                    a = 1 - a
                nt, acc = r["n"][:, 0, :], (r["n"][:, 1, :], r["n"][:, 2, :])
                step(dve.tensor_scalar(nt, run[:, a, NB - 1, :], 1.0 / P, 0.5 - 0.5 / P, ALU.mult, ALU.add))
                step(dve.tensor_scalar(nt, nt, ROUND, -ROUND, ALU.add, ALU.add))
                step(dve.tensor_copy(acc[0], nt))
                q = 0
                for d in (1, 2, 4, 8):
                    step(dve.tensor_copy(acc[1 - q][:, 0:d], acc[q][:, 0:d]))
                    step(dve.tensor_tensor(acc[1 - q][:, d:E], acc[q][:, d:E], acc[q][:, 0:E - d], ALU.add))
                    q = 1 - q
                upto, start = acc[q], r["n"][:, 3, :]
                step(dve.tensor_tensor(start, upto, nt, ALU.subtract))
                step(dve.tensor_scalar(start, start, float(P), 1.0, ALU.mult, ALU.add))
                pl = run[:, 1 - a, :, :]
                cnt = CT_[:, 0:NB * E].rearrange("p (t e) -> p t e", t=NB)
                step(dve.tensor_tensor(pl, run[:, a, :, :], cnt, ALU.subtract))
                step(dve.tensor_tensor(pl, pl, PT[:, 0:NB * E].rearrange("p (t e) -> p t e", t=NB), ALU.add))
                step(dve.tensor_tensor(pl, pl, start.unsqueeze(1).to_broadcast(T16), ALU.add))
                step(dve.tensor_tensor(pl, pl, r["sel"][:, :, :], ALU.mult))
                for t in range(NB):
                    ins = dve.max(m["pos"][:, t, :], pl[:, t, :])
                step(ins)
                top = m["pos"][:, :, 0:TOPK]
                full = [P, NB, TOPK, E]
                hit = r["big"][:, 0:NB * TOPK * E].rearrange("p (t k e) -> p t k e", t=NB, k=TOPK)
                step(dve.tensor_tensor(hit, pl.unsqueeze(2).to_broadcast(full), top.unsqueeze(3).to_broadcast(full), ALU.is_equal))
                step(dve.tensor_tensor(hit, hit, r["sb"][:, :, :].unsqueeze(2).to_broadcast(full), ALU.mult))
                step(dve.tensor_reduce(m["pair"][:, :, :, 1], hit, AX.X, ALU.add))
                step(dve.tensor_copy(m["pair"][:, :, :, 0], tok[:, :].unsqueeze(2).to_broadcast([P, NB, TOPK])))
                step(dve.tensor_scalar(m["posu"][:, :, :], top, -1.0, None, ALU.add))
                J = NT + 3
                je = [P, J, E]
                cmp = r["eq"][:, 0:J * E].rearrange("p (j e) -> p j e", j=J)
                ej, first = m["ej"][:, :], r["big"][:, 2048:2048 + J]
                step(dve.tensor_tensor(cmp, upto.unsqueeze(1).to_broadcast(je), iJ[:, :].unsqueeze(2).to_broadcast(je), ALU.is_le))
                step(dve.tensor_reduce(ej, cmp, AX.X, ALU.add))
                step(dve.tensor_scalar(ej, ej, float(E - 1), None, ALU.min))
                step(dve.memset(first[:, 0:1], 1.0))
                step(dve.tensor_tensor(first[:, 1:J], ej[:, 1:J], ej[:, 0:J - 1], ALU.not_equal))
                far = r["n"][:, 4, :]
                step(dve.tensor_scalar(far, nt, 0.5, 1000.0, ALU.is_lt, ALU.mult))
                step(dve.tensor_tensor(far, far, iE[:, :], ALU.add))
                step(dve.tensor_tensor(cmp, iE[:, :].unsqueeze(1).to_broadcast(je), ej.unsqueeze(2).to_broadcast(je), ALU.is_le))
                step(dve.tensor_scalar(cmp, cmp, 1000.0, None, ALU.mult))
                step(dve.tensor_tensor(cmp, cmp, far.unsqueeze(1).to_broadcast(je), ALU.add))
                nxt = r["big"][:, 3072:3072 + J]
                step(dve.tensor_reduce(nxt, cmp, AX.X, ALU.min))
                step(dve.tensor_scalar(m["meta"][:, 1, :], nxt[0:1, :], float(E - 1), None, ALU.min))
                step(dve.tensor_copy(m["meta"][:, 0, :], first[0:1, :]))
                step(dve.tensor_copy(m["meta"][:, 2, :], ej[0:1, :]))


def shared_expert(nc, c, m, XT, sw1, sw2, sw3):
    X = c["X"]
    with ExitStack() as st:
        def sb(name, shape, dt=F32):
            return st.enter_context(nc.sbuf_tensor(name, shape, dt))

        def sem(name):
            return st.enter_context(nc.semaphore(name))

        def bank(name, n):
            return [st.enter_context(nc.psum_tensor(f"{name}{i}", [P, 512], F32)) for i in range(n)]
        r1, r3, r2 = sb("er1", [P, KC, I]), sb("er3", [P, KC, I]), sb("er2", [P, 3, D])
        W1 = [sb(f"eW1{i}", [P, 2, KC, I], F32R) for i in range(2)]
        W3 = [sb(f"eW3{i}", [P, 2, KC, I], F32R) for i in range(2)]
        W2 = [sb(f"eW2{i}", [P, 2, 3, D], F32R) for i in range(2)]
        sl = sb("esl", [P, 2, D])
        h = sb("eh", [P, 1, D])
        hT = sb("ehT", [P, 2, 3, GT], F32R)
        A, B, Y = bank("eA", 2), bank("eB", 2), bank("eY", 2)
        w_in, w_split = sem("ew_in"), sem("ew_split")
        NU = NSH * NG
        ab_fill, a_out, b_out, h_hi, h_lo, y_fill, y_out = (sem(f"e{n}") for n in (
            "ab_fill", "a_out", "b_out", "h_hi", "h_lo", "y_fill", "y_out"))
        placed, stored = sem("placed"), sem("e_stored")

        def wait(eng, s, n):
            if n > 0:
                eng.wait_ge(s, n)
        with nc.Block() as block:
            @block.sync
            def _(sp):
                for b in range(NSH):
                    wait(sp, w_split, 8 * b)
                    cols = slice(b * I, (b + 1) * I)
                    sp.dma_start(r1[:, :, :], sw1[:, cols].rearrange("(k p) i -> p k i", p=P)).then_inc(w_in, 16)
                    sp.dma_start(r3[:, :, :], sw3[:, cols].rearrange("(k p) i -> p k i", p=P)).then_inc(w_in, 16)
                    sp.dma_start(r2[:, 0:2, :], sw2[b * I:b * I + 2 * P, :].rearrange("(k p) i -> p k i", p=P)).then_inc(w_in, 16)
                    sp.dma_start(r2[0:IC[2], 2, :], sw2[b * I + 2 * P:(b + 1) * I, :]).then_inc(w_in, 16)
                for g in range(NG):
                    sp.wait_ge(y_out, GB * (NU - NG + g + 1))
                    sp.dma_start(m["acc_d"][g * GT:(g + 1) * GT, :].rearrange("(b p) d -> p b d", p=P),
                                 X[:, g * GB:(g + 1) * GB, :]).then_inc(stored, 16)
                sp.wait_ge(stored, 16 * NG)

            @block.gpsimd
            def _(pool):
                n = 0
                for b in range(NSH):
                    pool.wait_ge(w_in, 64 * (b + 1))
                    for raw, dst, pp in ((r1[:, :, :], W1[b], P), (r3[:, :, :], W3[b], P), (r2[:, 0:2, :], W2[b], P),
                                         (r2[0:IC[2], 2:3, :], W2[b], IC[2])):
                        hi, lo = (dst[0:pp, j, 0:raw.shape[1], :] if pp == P else dst[0:pp, j, 2:3, :] for j in range(2))
                        pool.tensor_copy(hi, raw).then_inc(w_split, 1)
                        n += 1
                        pool.wait_ge(w_split, n)
                        pool.tensor_tensor(lo, raw, hi.bitcast(F32), ALU.subtract).then_inc(w_split, 1)
                        n += 1
                for t in range(NB):
                    for k in range(TOPK):
                        pool.indirect_dma_start(
                            out=m["table_d"][:, :], out_offset=bass.IndirectOffsetOnAxis(ap=m["posu"][:, t, k:k + 1], axis=0),
                            in_=m["pair"][:, t, k, :], in_offset=None).then_inc(placed, 16)
                pool.wait_ge(placed, 16 * NB * TOPK)

            @block.tensor
            def _(pe):
                def hidden(q):
                    u, ch = q // 3, q % 3
                    b, gr = u // NG, u % NG
                    if gr == 0 and ch == 0:
                        pe.wait_ge(w_split, 8 * (b + 1))
                    wait(pe, b_out, q - 1)
                    cols = slice(ch * P, ch * P + IC[ch])
                    for W_, bk in ((W1[b], A[q % 2]), (W3[b], B[q % 2])):
                        for k in range(KC):
                            x_ = mm3(pe, bk[0:IC[ch], :], lambda j: W_[:, j, k, cols],
                                     lambda j: XT[:, j, k, gr * GT:(gr + 1) * GT], k == 0, k == KC - 1)
                    x_.then_inc(ab_fill, 1)

                def outer(u):
                    b = u // NG
                    pe.wait_ge(h_lo, 3 * u + 3)
                    for t in range(GB):
                        n = u * GB + t
                        wait(pe, y_out, n - 1)
                        for ch in range(3):
                            x_ = mm3(pe, Y[n % 2][:, :], lambda j: hT[0:IC[ch], j, ch, t * P:(t + 1) * P],
                                     lambda j: W2[b][0:IC[ch], j, ch, :], ch == 0, ch == 2)
                        x_.then_inc(y_fill, 1)
                hidden(0)
                for u in range(NU):
                    hidden(3 * u + 1)
                    hidden(3 * u + 2)
                    if u + 1 < NU:
                        hidden(3 * u + 3)
                    outer(u)

            @block.scalar
            def _(act):
                for q in range(3 * NU):
                    n = IC[q % 3]
                    act.wait_ge(ab_fill, q + 1)
                    wait(act, b_out, q - 1)
                    act.activation(sl[0:n, q % 2, :], A[q % 2][0:n, :], ACT.Silu).then_inc(a_out, 1)
                    act.wait_ge(b_out, q + 1)
                    wait(act, y_fill, GB * (q // 3))
                    act.activation(hT[0:n, 0, q % 3, :], h[0:n, 0, :], ACT.Copy).then_inc(h_hi, 1)

            @block.vector
            def _(dve):
                for u in range(NU):
                    for ch in range(3):
                        q = 3 * u + ch
                        n = IC[ch]
                        dve.wait_ge(a_out, q + 1)
                        wait(dve, h_lo, q)
                        dve.tensor_tensor(h[0:n, 0, :], B[q % 2][0:n, :], sl[0:n, q % 2, :], ALU.mult).then_inc(b_out, 1)
                        dve.wait_ge(h_hi, q + 1)
                        dve.tensor_tensor(hT[0:n, 1, q % 3, :], h[0:n, 0, :], hT[0:n, 0, q % 3, :].bitcast(F32),
                                          ALU.subtract).then_inc(h_lo, 1)
                    for t in range(GB):
                        n = u * GB + t
                        tt = u % NG * GB + t
                        dve.wait_ge(y_fill, n + 1)
                        wait(dve, y_out, n - NG * GB + 1)
                        dve.scalar_tensor_tensor(out=X[:, tt, :], in0=Y[n % 2][:, :], scalar=c["tg"][:, 3:4],
                                                 in1=X[:, tt, :], op0=ALU.mult, op1=ALU.add).then_inc(y_out, 1)


def expert_tiles(nc, c, m, w1, w2, w3, out):
    identF = c["identF"]
    J = NT + 3
    with ExitStack() as st:
        def sb(name, shape, dt=F32):
            return st.enter_context(nc.sbuf_tensor(name, shape, dt))

        def sem(name):
            return st.enter_context(nc.semaphore(name))

        def bank(name, n):
            return [st.enter_context(nc.psum_tensor(f"{name}{i}", [P, 512], F32)) for i in range(n)]
        tab = sb("t_tab", [NT, P, 2])
        rowid = sb("t_rowid", [P, J], U32)
        wgt = sb("t_wgt", [P, J])
        ids = sb("t_ids", [P, UT], U32)
        wcol = sb("t_wcol", [P, UT])
        pidx = sb("t_pidx", [P, 3], I32)
        r13, r2 = sb("t_r13", [P, KC, 2, I]), sb("t_r2", [P, 3, D])
        W13, W2 = sb("t_W13", [P, 2, KC, 2, I], F32R), sb("t_W2", [P, 2, 3, D], F32R)
        xg = sb("t_xg", [P, UT, D])
        xT = sb("t_xT", [P, 2, 2, KC, P], F32R)
        sl = sb("t_sl", [P, I])
        h = sb("t_h", [P, I])
        hT = sb("t_hT", [P, 2, 3, P], F32R)
        ys = sb("t_ys", [P, UT, D])
        H1, H3, Y = bank("t_H1", 2), bank("t_H3", 2), bank("t_Y", 2)
        TX, TH = bank("t_TX", 1)[0], bank("t_TH", 1)[0]
        tab_in, tab_tr, tab_ok, zeroed = sem("tab_in"), sem("tab_tr"), sem("tab_ok"), sem("t_zeroed")
        r13_in, r2_in, w13_hi, w13_lo, w2_hi, w2_lo = (sem(f"t_{n}") for n in ("r13_in", "r2_in", "w13_hi", "w13_lo", "w2_hi", "w2_lo"))
        tx_fill, tx_hi, tx_lo, h_fill, silu, hmul, th_fill, th_hi, th_lo, y_fill, y_evac, scattered = (
            sem(f"t_{n}") for n in ("tx_fill", "tx_hi", "tx_lo", "h_fill", "silu", "hmul", "th_fill", "th_hi", "th_lo",
                                    "y_fill", "y_evac", "scattered"))
        g_in = [sem(f"t_g_in{b}") for b in range(UT)]
        sc_done, out_done = sem("t_sc_done"), sem("t_out_done")
        own_pool, own_act, own_dve, own_sp = c["passed_pool"], c["passed_act"], c["passed_dve"], c["passed_sp"]

        with nc.Block() as block:
            @block.sync
            def _(sp):
                def load13(e):
                    for j, w in enumerate((w1, w3)):
                        sp.dma_start(r13[:, :, j, :], w[bass.ds(e, 1)].rearrange("e (k p) i -> p (e k) i", p=P)).then_inc(r13_in, 16)

                def load2(e):
                    sp.dma_start(r2[:, 0:2, :], w2[bass.ds(e, 1), 0:2 * P, :].rearrange("e (k p) i -> p (e k) i", p=P))\
                        .then_inc(r2_in, 16)
                    sp.dma_start(r2[0:IC[2], 2, :], w2[bass.ds(e, 1), 2 * P:I, :].rearrange("e p i -> p (e i)")).then_inc(r2_in, 16)
                sp.dma_start(tab[:, :, :].rearrange("j p a -> j (p a)"), m["table_d"].rearrange("(j p) a -> j (p a)", p=P))\
                    .then_inc(tab_in, 16)
                e0 = sp.value_load(m["meta"][0:1, 2, 0:1], min_val=0, max_val=E - 1)
                load13(e0)
                load2(e0)
                with sp.Fori(0, NT // UT) as i:
                    for b in range(UT):
                        n = i * UT + b
                        first = sp.value_load(m["meta"][0:1, 0, bass.ds(n, 1)], min_val=0, max_val=1)
                        nxt = sp.value_load(m["meta"][0:1, 1, bass.ds(n, 1)], min_val=0, max_val=E - 1)
                        with sp.If(first):
                            sp.wait_ge(w13_lo, 4 * (n + 1))
                            sp.sem_inc(own_sp, 1)
                            load13(nxt)
                            sp.wait_ge(w2_lo, 2 * (n + 1) + 2)
                            sp.sem_inc(own_sp, 1)
                            load2(nxt)
                        with sp.Else():
                            sp.wait_ge(r13_in, 32 * (n + 1))
                            sp.sem_inc(r13_in, 32)
                            sp.wait_ge(r2_in, 32 * (n + 1))
                            sp.sem_inc(r2_in, 32)
                sp.wait_ge(r13_in, 32 * (NT + 1))
                sp.wait_ge(r2_in, 32 * (NT + 1))
                sp.wait_ge(sc_done, 16 * NT)
                sp.dma_start(out.rearrange("b p d -> (b p) d"), m["acc_d"][0:T_ALL, :]).then_inc(out_done, 16)
                sp.wait_ge(out_done, 16)

            @block.gpsimd
            def _(pool):
                scattered_credit = UT + 1
                pool.sem_inc(scattered, scattered_credit)
                pool.memset(hT[:, :, :, :].bitcast(F32), 0.0).then_inc(th_lo, 1)
                for j in range(2):
                    pool.memset(W2[:, j, :, :].bitcast(F32), 0.0).then_inc(w2_lo, 1)
                pool.iota(pidx[:, :], pattern=[[0, 3]], base=T_ALL, channel_multiplier=1).then_inc(zeroed, 1)
                pool.wait_ge(zeroed, 1)
                pool.tensor_copy(rowid[:, NT:J], pidx[:, :]).then_inc(zeroed, 1)
                pool.wait_ge(zeroed, 2)
                pool.wait_ge(tab_ok, 2)

                def gather(n, b):
                    pool.tensor_copy(ids[:, b:b + 1], rowid[:, bass.ds(n, 1)]).then_inc(zeroed, 1)

                for n in range(3):
                    gather(n, n)
                    pool.wait_ge(zeroed, 3 + n)
                    pool.indirect_dma_start(out=xg[:, n, :], out_offset=None, in_=m["rows_d"][:, :],
                                            in_offset=bass.IndirectOffsetOnAxis(ap=ids[:, n:n + 1], axis=0)).then_inc(g_in[n], 16)
                with pool.Fori(0, NT // UT) as i:
                    for b in range(UT):
                        n = i * UT + b
                        b3 = (b + 3) % UT
                        pool.wait_ge(tx_fill, n + 1)
                        pool.sem_inc(own_pool, 1)
                        gather(n + 3, b3)
                        pool.wait_ge(zeroed, n + 6)
                        pool.sem_inc(own_pool, 1)
                        pool.indirect_dma_start(out=xg[:, b3, :], out_offset=None, in_=m["rows_d"][:, :],
                                                in_offset=bass.IndirectOffsetOnAxis(ap=ids[:, b3:b3 + 1], axis=0))\
                            .then_inc(g_in[b3], 16)
                        pool.wait_ge(y_evac, n + 4)
                        pool.sem_inc(own_pool, 1)
                        pool.indirect_dma_start(out=m["acc_d"][:, :],
                                                out_offset=bass.IndirectOffsetOnAxis(ap=ids[:, b:b + 1], axis=0),
                                                in_=ys[:, b, :], in_offset=None, compute_op=ALU.add).then_inc(sc_done, 16)
                        pool.wait_ge(sc_done, 16 * (n + 1))
                        pool.sem_inc(scattered, 1)
                for b in range(3):
                    pool.wait_ge(g_in[b], 16 * (NT // UT + 1))

            @block.tensor
            def _(pe):
                pe.wait_ge(tab_in, 16)
                for j in range(2):
                    pe.transpose(H1[j][:, 0:NT], tab[:, :, j], identF[0:NT, 0:NT]).then_inc(tab_tr, 1)

                def tx(turn, b):
                    pe.wait_ge(g_in[b % UT], 16 * turn)
                    for k in range(KC):
                        x_ = pe.transpose(TX[:, k * P:(k + 1) * P], xg[:, b % UT, k * P:(k + 1) * P], identF[:, :])
                    x_.then_inc(tx_fill, 1)

                def y(b):
                    for ch in range(3):
                        x_ = mm3(pe, Y[(b - 1) % 2][:, :], lambda j: hT[0:IC[ch], j, ch, :],
                                 lambda j: W2[0:IC[ch], j, ch, :], ch == 0, ch == 2)
                    x_.then_inc(y_fill, 1)
                tx(1, 0)
                pe.wait_ge(tab_ok, 2)
                with pe.Fori(0, NT // UT) as i:
                    for b in range(UT):
                        n = i * UT + b
                        pe.wait_ge(tx_lo, n + 1)
                        for k in range(KC):
                            pe.wait_ge(w13_lo, 4 * n + k + 1)
                            for jx, jw in ((0, 0), (0, 1), (1, 0)):
                                for bk, j in ((H1, 0), (H3, 1)):
                                    x_ = pe.matmul(bk[b % 2][:, 0:I], xT[:, b % 2, jx, k, :], W13[:, jw, k, j, :],
                                                   start=k == 0 and jx == jw, stop=k == KC - 1 and jx == 1)
                        x_.then_inc(h_fill, 1)
                        tx(i + 1 if b < UT - 1 else i + 2, b + 1)
                        pe.wait_ge(th_lo, n + 1)
                        pe.wait_ge(w2_lo, 2 * n + 2)
                        pe.wait_ge(y_evac, n + 1)
                        y(b)
                        pe.wait_ge(hmul, n + 2)
                        pe.wait_ge(th_lo, n + 1)
                        for ch in range(3):
                            x_ = pe.transpose(TH[0:IC[ch], ch * P:(ch + 1) * P], h[:, ch * P:ch * P + IC[ch]], identF[:, :])
                        x_.then_inc(th_fill, 1)
                pe.wait_ge(th_lo, NT + 1)
                pe.wait_ge(w2_lo, 2 * NT + 2)
                pe.wait_ge(y_evac, NT + 1)
                y(UT)

            @block.scalar
            def _(act):
                def x_hi(b):
                    act.activation(xT[:, b % 2, 0, :, :], TX[:, :].rearrange("p (k t) -> p k t", k=KC), ACT.Copy).then_inc(tx_hi, 1)

                def w13():
                    for k in range(KC):
                        act.activation(W13[:, 0, k, :, :], r13[:, k, :, :], ACT.Copy).then_inc(w13_hi, 1)

                def y_out(b):
                    act.activation(ys[:, (b - 1) % UT, :], Y[(b - 1) % 2][:, :], ACT.Copy,
                                   scale=wcol[:, (b - 1) % UT:(b - 1) % UT + 1]).then_inc(y_evac, 1)
                act.sem_inc(y_evac, 2)
                act.wait_ge(r13_in, 32)
                w13()
                act.wait_ge(tx_fill, 1)
                x_hi(0)
                with act.Fori(0, NT // UT) as i:
                    first = act.value_load(m["meta"][0:1, 0, bass.ds(i * UT, 1)], min_val=0, max_val=1)
                    for b in range(UT):
                        n = i * UT + b
                        this, first = first, act.value_load(m["meta"][0:1, 0, bass.ds(n + 1, 1)], min_val=0, max_val=1)
                        act.wait_ge(h_fill, n + 1)
                        act.wait_ge(hmul, n + 1)
                        act.activation(sl[:, :], H1[b % 2][:, 0:I], ACT.Silu).then_inc(silu, 1)
                        act.wait_ge(tx_fill, n + 2)
                        x_hi(b + 1)
                        with act.If(first):
                            act.wait_ge(r13_in, 32 * (n + 2))
                            w13()
                        with act.Else():
                            act.drain()
                            act.sem_inc(w13_hi, KC)
                        act.wait_ge(y_fill, n + 1)
                        act.wait_ge(scattered, n + 1)
                        y_out(b)
                        with act.If(this):
                            act.wait_ge(r2_in, 32 * (n + 1))
                            act.activation(W2[:, 0, 0:2, :], r2[:, 0:2, :], ACT.Copy).then_inc(w2_hi, 1)
                            act.activation(W2[0:IC[2], 0, 2, :], r2[0:IC[2], 2, :], ACT.Copy).then_inc(w2_hi, 1)
                        with act.Else():
                            act.drain()
                            act.sem_inc(w2_hi, 2)
                        act.wait_ge(th_fill, n + 1)
                        act.activation(hT[:, 0, 0:2, :], TH[:, 0:2 * P].rearrange("p (k t) -> p k t", k=2), ACT.Copy)
                        act.activation(hT[0:IC[2], 0, 2, :], TH[0:IC[2], 2 * P:3 * P], ACT.Copy).then_inc(th_hi, 1)
                act.wait_ge(y_fill, NT + 1)
                act.wait_ge(scattered, NT + 1)
                y_out(UT)

            @block.vector
            def _(dve):
                def x_lo(b):
                    dve.tensor_tensor(xT[:, b % 2, 1, :, :], TX[:, :].rearrange("p (k t) -> p k t", k=KC),
                                      xT[:, b % 2, 0, :, :].bitcast(F32), ALU.subtract).then_inc(tx_lo, 1)

                def w13_k(k):
                    dve.tensor_tensor(W13[:, 1, k, :, :], r13[:, k, :, :], W13[:, 0, k, :, :].bitcast(F32), ALU.subtract)\
                        .then_inc(w13_lo, 1)
                dve.sem_inc(hmul, 1)
                dve.wait_ge(tab_tr, 2)
                dve.tensor_copy(rowid[:, 0:NT], H1[0][:, 0:NT]).then_inc(tab_ok, 1)
                dve.tensor_copy(wgt[:, 0:NT], H1[1][:, 0:NT]).then_inc(tab_ok, 1)
                dve.memset(wcol[:, :], 0.0).then_inc(tab_ok, 1)
                dve.wait_ge(tab_ok, 3)
                for k in range(KC):
                    dve.wait_ge(w13_hi, k + 1)
                    w13_k(k)
                dve.wait_ge(tx_hi, 1)
                x_lo(0)
                with dve.Fori(0, NT // UT) as i:
                    first = dve.value_load(m["meta"][0:1, 0, bass.ds(i * UT, 1)], min_val=0, max_val=1)
                    for b in range(UT):
                        n = i * UT + b
                        this, first = first, dve.value_load(m["meta"][0:1, 0, bass.ds(n + 1, 1)], min_val=0, max_val=1)
                        dve.tensor_copy(wcol[:, b:b + 1], wgt[:, bass.ds(n, 1)])
                        dve.wait_ge(silu, n + 1)
                        dve.tensor_tensor(h[:, :], H3[b % 2][:, 0:I], sl[:, :], ALU.mult).then_inc(hmul, 1)
                        dve.wait_ge(tx_hi, n + 2)
                        x_lo(b + 1)
                        with dve.If(first):
                            for k in range(KC):
                                dve.wait_ge(w13_hi, 4 * (n + 1) + k + 1)
                                w13_k(k)
                        with dve.Else():
                            dve.drain()
                            dve.sem_inc(w13_lo, KC)
                        with dve.If(this):
                            dve.wait_ge(y_fill, n + 1)
                            dve.wait_ge(w2_hi, 2 * n + 1)
                            dve.tensor_tensor(W2[:, 1, 0:2, :], r2[:, 0:2, :], W2[:, 0, 0:2, :].bitcast(F32), ALU.subtract)\
                                .then_inc(w2_lo, 1)
                            dve.wait_ge(w2_hi, 2 * n + 2)
                            dve.tensor_tensor(W2[0:IC[2], 1, 2, :], r2[0:IC[2], 2, :], W2[0:IC[2], 0, 2, :].bitcast(F32),
                                              ALU.subtract).then_inc(w2_lo, 1)
                        with dve.Else():
                            dve.drain()
                            dve.sem_inc(w2_lo, 2)
                        dve.wait_ge(th_hi, n + 1)
                        dve.tensor_tensor(hT[:, 1, 0:2, :], TH[:, 0:2 * P].rearrange("p (k t) -> p k t", k=2),
                                          hT[:, 0, 0:2, :].bitcast(F32), ALU.subtract)
                        dve.tensor_tensor(hT[0:IC[2], 1, 2, :], TH[0:IC[2], 2 * P:3 * P],
                                          hT[0:IC[2], 0, 2, :].bitcast(F32), ALU.subtract).then_inc(th_lo, 1)


_INS = ['x', 'ctx_2048', 'mask_BxS2_bk0', 'g_xattn', 'g_ffn', 'L0_xattn_norm_w', 'L0_xattn_wq', 'L0_xattn_wk',
        'L0_xattn_wv', 'L0_xattn_wo', 'L0_xattn_wg', 'L0_ffn_weight', 'L0_ffn_bias', 'L1_ffn_gate_w',
        'L1_ffn_expert_bias', 'L1_ffn_w1', 'L1_ffn_w2', 'L1_ffn_w3', 'L1_ffn_sw1', 'L1_ffn_sw2', 'L1_ffn_sw3']
_OUTS = [((NB, S, D), 'float32')]


def kernel(**inputs):
    import numpy as _np
    import concourse.bacc as _bacc
    from concourse import mybir as _mybir
    from concourse.bass_utils import run_bass_kernel_spmd as _run

    nc = _bacc.Bacc("TRN2", target_bir_lowering=False, num_devices=1)
    arrays, args = {}, []
    for name in _INS:
        a = _np.ascontiguousarray(inputs[name])
        arrays[f"in_{name}_dram"] = a
        args.append(nc.dram_tensor(f"in_{name}_dram", a.shape, _mybir.dt.from_np(a.dtype), kind="ExternalInput").ap())
    for i, (shape, dtype) in enumerate(_OUTS):
        args.append(nc.dram_tensor(f"out_{i}_dram", shape, _mybir.dt.from_np(_np.dtype(dtype)), kind="ExternalOutput").ap())
    program(nc, *args)
    r = _run(nc, [arrays], core_ids=[0])
    return r.results[0]["out_0_dram"]
```

```python
from contextlib import ExitStack

import concourse.bass as bass
from concourse import mybir

ALU = mybir.AluOpType
ACT = mybir.ActivationFunctionType
AX = mybir.AxisListType
F32 = mybir.dt.float32
F32R = mybir.dt.float32r
BF16 = mybir.dt.bfloat16
U8 = mybir.dt.uint8
U32 = mybir.dt.uint32
I32 = mybir.dt.int32

P = 128
NB, S, D = 16, 128, 512
KC = D // P
GB = 4
NG = NB // GB
GT = GB * S
NH, HD = 16, 32
HQ = P // HD
SCALE0 = float(HD) ** -0.5
SCALE1 = float(S) ** -0.5
MASKED = -1.0e30
ROUND = 1.5 * 2.0 ** 23
E, I, TOPK = 16, 352, 4
EG, TOPG = 4, 2
T_ALL = NB * S
NT = T_ALL * TOPK // P + E
PADS = P
NSH = 2
UT = 4
TRIPS = NT // UT
SCALE_STEPS = 11
IC = [P, P, I - 2 * P]


class Count:

    def __init__(self, sem, per, credit=False, before=0):
        self.sem, self.per, self.base = sem, per, before + (per if credit else 0)

    def grant(self, eng):
        eng.sem_inc(self.sem, self.per)

    def wait(self, eng, trip, k, own=None):
        eng.wait_ge(self.sem, trip * self.per + (self.base + k))
        if own is not None:
            eng.sem_inc(own, 1)


def mm3(pe, out, lhs, rhs, first, last):
    pe.matmul(out, lhs(0), rhs(0), start=first, stop=False)
    pe.matmul(out, lhs(0), rhs(1), start=False, stop=False)
    return pe.matmul(out, lhs(1), rhs(0), start=False, stop=last)


def program(nc, x, ctx_in, mask, g_x, g_f, norm_w, wq, wk, wv, wo, wg, fw, fb,
            gate_w, ebias, w1, w2, w3, sw1, sw2, sw3, out):
    with ExitStack() as top:
        def sb(name, shape, dt=F32):
            return top.enter_context(nc.sbuf_tensor(name, shape, dt))

        X = sb("X", [P, NB, D])
        bst = sb("bst", [P, NB, 6])
        mean = sb("mean", [P, NB])
        rstd = sb("rstd", [P, NB])
        tmp16 = sb("tmp16", [P, 7, NB])
        nhalf = sb("nhalf", [P, NB])
        identF = sb("identF", [P, P])
        identB = sb("identB", [P, P], BF16)
        onesF = sb("onesF", [P, P])
        onesB = sb("onesB", [P, P], BF16)
        tg = sb("tg", [P, 4])
        parts = dict(X=X, bst=bst, mean=mean, rstd=rstd, tmp16=tmp16, identF=identF, identB=identB, onesF=onesF,
                     onesB=onesB, nhalf=nhalf, tg=tg, fw_in=top.enter_context(nc.semaphore("fw_in")))
        for e in ("pool", "sp", "dve", "act"):
            parts[f"passed_{e}"] = top.enter_context(nc.semaphore(f"passed_{e}"))
        with ExitStack() as both:
            parts["CT"] = both.enter_context(nc.sbuf_tensor("CT", [P, 2, GB // 2, D], F32))
            attention_heads(nc, parts, x, g_x, g_f, fw, ctx_in, mask, norm_w, wq, wk, wv, wo, wg)
            ternary_ffn(nc, parts, fb)
        attention_features(nc, parts, ctx_in)
        experts(nc, parts, gate_w, ebias, w1, w2, w3, sw1, sw2, sw3, out)


def row_scale(dve, c, done, powered, eps, ms_eps=None, meanwhile=(), half=None):
    tiles, n = (slice(0, NB), 0) if half is None else (slice(half * NB // 2, (half + 1) * NB // 2), half * SCALE_STEPS)
    t, bst = c["tmp16"][:, :, tiles], c["bst"][:, tiles, :]
    mean, rstd = c["mean"][:, tiles], c["rstd"][:, tiles]
    diff, squares, var, r1, _, r2, ms = (t[:, k, :] for k in range(7))
    powers = 2 * (half or 0)

    def step(*instrs):
        nonlocal n
        for instr in instrs:
            instr.then_inc(done, 1)
        n += len(instrs)
        dve.wait_ge(done, n)
    step(dve.tensor_tensor(mean, bst[:, :, 1], bst[:, :, 4], ALU.add),
         dve.tensor_tensor(diff, bst[:, :, 1], bst[:, :, 4], ALU.subtract),
         dve.tensor_tensor(squares, bst[:, :, 2], bst[:, :, 5], ALU.add))
    step(dve.tensor_scalar(mean, mean, 0.5, None, ALU.mult),
         dve.scalar_tensor_tensor(out=r1, in0=diff, scalar=0.25, in1=diff, op0=ALU.mult, op1=ALU.mult))
    step(dve.scalar_tensor_tensor(out=var, in0=squares, scalar=1.0 / D, in1=r1, op0=ALU.mult, op1=ALU.add))
    step(dve.tensor_scalar(t[:, 4, :], var, eps, None, ALU.add))
    if meanwhile:
        meanwhile[0]()
    dve.wait_ge(powered, powers + 1)
    if ms_eps is None:
        return
    step(dve.tensor_tensor(ms, r1, r1, ALU.mult))
    step(dve.tensor_tensor(ms, ms, var, ALU.mult))
    step(dve.tensor_scalar(ms, ms, ms_eps, None, ALU.add))
    if meanwhile:
        meanwhile[1]()
    dve.wait_ge(powered, powers + 2)
    step(dve.tensor_tensor(rstd, r1, r2, ALU.mult))


def row_power(pool, c, done, powered, twice=False, half=None):
    tiles, n = (slice(0, NB), 0) if half is None else (slice(half * NB // 2, (half + 1) * NB // 2), half * SCALE_STEPS)
    t, nhalf = c["tmp16"][:, :, tiles], c["nhalf"][:, tiles]
    pool.wait_ge(done, n + 7)
    pool.tensor_tensor(t[:, 3, :] if twice else c["rstd"][:, tiles], t[:, 4, :], nhalf, ALU.pow).then_inc(powered, 1)
    if twice:
        pool.wait_ge(done, n + 10)
        pool.tensor_tensor(t[:, 5, :], t[:, 6, :], nhalf, ALU.pow).then_inc(powered, 1)


def attention_heads(nc, c, x, g_x, g_f, fw, ctx_in, mask, norm_w, wq, wk, wv, wo, wg):
    X, identF = c["X"], c["identF"]
    with ExitStack() as st:
        def sb(name, shape, dt=F32):
            return st.enter_context(nc.sbuf_tensor(name, shape, dt))

        def sem(name):
            return st.enter_context(nc.semaphore(name))

        def bank(name, n):
            return [st.enter_context(nc.psum_tensor(f"{name}{i}", [P, 512], F32)) for i in range(n)]

        W = [sb(f"W{n}", [P, 2, KC, D], F32R) for n in "qkvgo"]
        WQ, WK, WV, WG, WO = W
        nw = sb("nw", [P, KC])
        hg = sb("hg", [P, 1])
        mcol = sb("mcol", [P, NB])
        mrow = sb("mrow", [P, GB, S], BF16)
        CT = c["CT"]
        xn = sb("xn", [P, 2, D])
        xT = sb("xT", [P, 2, 2, KC, GT // 2], F32R)
        cT = sb("cT", [P, 2, 2, KC, GT // 2], F32R)
        qT = sb("qT", [P, 2, KC, GT // 2])
        kT = sb("kT", [P, 2, KC, GT // 2])
        va = sb("va", [P, 2, NH, HD + 1])
        gs = sb("gs", [P, 2, D])
        pr = sb("pr", [P, 2, HQ, S])
        pT = sb("pT", [P, 2, HQ, S])
        mx = sb("mx", [P, 2, HQ])
        rs = sb("rs", [P, 2, 2, HQ])
        o = sb("o", [P, 2, D])
        oT = sb("oT", [P, 2, KC, S], F32R)
        upd = sb("upd", [P, 2, D])
        mask_u8 = sb("mask_u8", [NB, S], U8)
        mask_f = sb("mask_f", [NB, S])
        mask_all = sb("mask_all", [P, NB, S], U8)
        T, M, SC, O = bank("T", 2), bank("M", 2), bank("SC", 2), bank("O", 2)

        raw = [t_[:, :, :, :].rearrange("p a k t -> p (a k t)").rearrange("p (o k) -> p o k", o=KC) for t_ in (qT, kT)]
        names = [(WQ, wq, "norm"), (WK, wk, None), (WV, wv, None), (WG, wg, "norm"), (WO, wo, "gate")]

        def scale_of(how, kc):
            return nw[:, kc:kc + 1] if how == "norm" else hg[:, 0:1] if how == "gate" else 1.0
        w_in = [sem(f"w_in{i}") for i in range(2)]
        nw_in, mask_in, w_tr, w_hi, w_lo = sem("nw_in"), sem("mask_in"), sem("w_tr"), sem("w_hi"), sem("w_lo")
        powered, m_ready, m_tr, m_col, scales = sem("powered"), sem("m_ready"), sem("m_tr"), sem("m_col"), sem("scales")
        ones_set, hg_ready, tg_ready, gates_bc = sem("ones_set"), sem("hg_ready"), sem("tg_ready"), sem("gates_bc")
        x_in, g_in = [sem(f"x_in{q}") for q in range(NG)], sem("g_in")
        zeroed, consts, seen = sem("zeroed"), sem("consts"), sem("seen")

        def rows_stats(dve, q):
            dve.wait_ge(x_in[q], 16)
            for t in range(q * GB, (q + 1) * GB):
                dve.bn_stats(c["bst"][:, t, :], X[:, t, :]).then_inc(seen, 1)
        TW = T + M

        def weight_lo(dve, n):
            dst, _, normed = names[n]
            for kc in range(KC):
                f = KC * n + kc
                dve.wait_ge(w_hi, f + 1)
                dve.scalar_tensor_tensor(out=dst[:, 1, kc, :], in0=TW[f % len(TW)][:, :],
                                         scalar=scale_of(normed, kc),
                                         in1=dst[:, 0, kc, :].bitcast(F32), op0=ALU.mult,
                                         op1=ALU.subtract).then_inc(w_lo, 1)
        gates = sb("gates", [1, 4])

        def prep(grp):
            return [[("xT", grp, 0), ("cT", grp, 0)], [("xT", grp, 1), ("cT", grp, 1)]] + \
                [[(n, grp, i)] for n in "qk" for i in range(KC)]

        NQ = GB * HQ
        ahead = {0: prep(1), GB // 2: prep(2)}
        plan = []
        for b in range(GB):
            if b in ahead:
                todo = ahead[b]
            mine = [[("v", b)], [("g", b)], [("oT", b - 1)] if b else [], [("oP", b - 1)] if b else []]
            for r in range(HQ):
                n = b * HQ + r
                fill = list(mine[r])
                take = ((1, 1, 2, 1), (1, 1, 2, 2), (1, 1, 1, 1), (1, 0, 1, 0))[b][r]
                for _ in range(min(take, len(todo))):
                    fill += todo.pop(0)
                plan += [("S", n)] + fill[:1]
                plan += [("pT", n - 1)] if n >= 1 else []
                plan += fill[1:]
                plan += [("pv", n - 2)] if n >= 2 else []
                if n >= 2 and (n - 2) % 2:
                    plan += [("on", (n - 2) // 2)]
        rest = [x_ for y_ in todo for x_ in y_]
        plan += rest[:1] + [("pT", NQ - 1)] + rest[1:2] + [("pv", NQ - 2), ("pv", NQ - 1), ("on", NQ // 2 - 1)] + rest[2:3] + \
            [("oT", GB - 1)] + rest[3:] + [("oP", GB - 1)]
        prologue = [(n, 2, i) for n, count in (("cT", GB // 2), ("k", KC), ("xT", GB // 2), ("q", KC)) for i in range(count)]

        T_KINDS, M_KINDS = ("xT", "cT", "pT", "oT"), ("q", "k", "v", "g", "oP")
        SPLIT, BY_ACT, BY_DVE = ("xT", "cT", "oT"), ("q", "k", "g"), ("v", "oP")

        def of(kinds, steps=None):
            return [s for s in (plan if steps is None else steps) if s[0] in kinds]

        def at(kinds, s):
            back = 0
            if s[0] in ("xT", "cT", "q", "k") and s[1] == 0:
                s, back = (s[0], 2, s[2]), 1
            elif s[0] in ("oT", "oP", "v", "g") and s[1] < 0:
                s, back = (s[0], s[1] + GB), 1
            elif s[0] in ("pT", "pv") and s[1] < 0:
                s, back = (s[0], s[1] + NQ), 1
            some = of(kinds)
            return some.index(s) + 1 - back * len(some)

        def upto(kinds, sub, n):
            some = of(kinds)
            if n >= 0:
                return len([s for s in some[:n] if s[0] in sub])
            return len([s for s in some[:n] if s[0] in sub]) - len(of(sub))

        assert len(of(T_KINDS)) % 2 == 0 and len(of(M_KINDS)) % 2 == 0
        c_in = [sem(f"c_in{q}") for q in range(2)]
        mask_all_in = sem("mask_all_in")
        mrow_ready = Count(sem("mrow_ready"), GB, before=GB)
        x_norm = Count(sem("x_norm"), GB, before=2)
        t_fill = Count(sem("t_fill"), len(of(T_KINDS)), True, 4)
        t_hi = Count(sem("t_hi"), len(of(T_KINDS)), True, 4)
        t_lo = Count(sem("t_lo"), len(of(SPLIT)), True, 4)
        m_fill = Count(sem("m_fill"), len(of(M_KINDS)), True, 2 * KC)
        m_act = Count(sem("m_act"), len(of(BY_ACT)), True, 2 * KC)
        m_dve = Count(sem("m_dve"), len(of(BY_DVE)), True)
        s_fill = Count(sem("s_fill"), NQ)
        s_max = Count(sem("s_max"), NQ)
        s_out = Count(sem("s_out"), NQ, True)
        p_exp = Count(sem("p_exp"), NQ)
        pv = Count(sem("pv"), NQ, True)
        o_rec = Count(sem("o_rec"), 2 * GB)
        o_norm = Count(sem("o_norm"), 2 * GB, True)
        added = Count(sem("added"), GB, True)
        HG = GB // 2
        GC = HG * S

        def tile_of(g, grp, j):
            return ((g + 1) * GB) % NB + j if grp == 2 else g * GB + grp * HG + j

        with nc.Block() as block:
            @block.sync
            def _(sp):
                sp.dma_start(gates[:, 0:2], g_x.rearrange("(a n) -> a n", a=1)).then_inc(g_in, 16)
                sp.dma_start(gates[:, 2:4], g_f.rearrange("(a n) -> a n", a=1)).then_inc(g_in, 16)
                with nc.allow_non_contiguous_dma(reason="512 scales once"):
                    sp.dma_start(nw[:, :], norm_w.rearrange("(k p) -> p k", p=P)).then_inc(nw_in, 16)
                for n, (_, w, _) in enumerate(names):
                    if n >= 2:
                        sp.wait_ge(w_tr, KC * (n - 1))
                    sp.dma_start(raw[n % 2][:, :, :], w.rearrange("(o p) k -> p o k", p=P)).then_inc(w_in[n % 2], 16)
                    if n == 2:
                        sp.dma_start(CT[:, 0, :, :], ctx_in[0:HG].rearrange("b p d -> p b d")).then_inc(c_in[0], 16)
                        sp.dma_start(mask_all[:, :, :], mask.rearrange("(a b) m -> a b m", a=1).to_broadcast([P, NB, S]))\
                            .then_inc(mask_all_in, 16)
                    if n == 0:
                        sp.dma_start(mask_u8[:, :], mask).then_inc(mask_in, 16)
                    else:
                        sp.dma_start(X[:, (n - 1) * GB:n * GB, :], x[(n - 1) * GB:n * GB].rearrange("b p d -> p b d"))\
                            .then_inc(x_in[n - 1], 16)

            @block.gpsimd
            def _(pool):
                pool.memset(c["identF"][:, :], 0.0).then_inc(zeroed, 1)
                pool.memset(c["onesF"][:, :], 1.0).then_inc(consts, 1)
                pool.memset(c["nhalf"][:, :], -0.5).then_inc(consts, 1)
                pool.wait_ge(zeroed, 1)
                pool.affine_select(out=c["identF"][:, :], in_=c["identF"][:, :], compare_op=ALU.not_equal, fill=1.0,
                                   base=0, pattern=[[-1, P]], channel_multiplier=1).then_inc(consts, 1)
                pool.memset(c["identB"][:, :], 0.0).then_inc(zeroed, 1)
                pool.memset(c["onesB"][:, :], 1.0).then_inc(consts, 1)
                pool.wait_ge(zeroed, 2)
                pool.affine_select(out=c["identB"][:, :], in_=c["identB"][:, :], compare_op=ALU.not_equal, fill=1.0,
                                   base=0, pattern=[[-1, P]], channel_multiplier=1).then_inc(consts, 1)
                pool.wait_ge(tg_ready, 1)
                pool.tensor_scalar(hg[:, :], c["tg"][:, 0:1], 0.5, None, ALU.mult).then_inc(hg_ready, 1)
                for b in range(2):
                    pool.memset(va[:, b, :, HD:HD + 1], 1.0).then_inc(ones_set, 1)

            @block.tensor
            def _(pe):
                pe.wait_ge(consts, 3)
                pe.wait_ge(g_in, 32)
                pe.matmul(SC[0][:, 0:4], c["onesF"][0:1, :], gates[0:1, :], start=True, stop=True).then_inc(gates_bc, 1)
                for n in range(len(names)):
                    pe.wait_ge(w_in[n % 2], 16 * (n // 2 + 1))
                    for kc in range(KC):
                        f = KC * n + kc
                        if f >= len(TW):
                            pe.wait_ge(w_hi, f - len(TW) + 1)
                            pe.wait_ge(w_lo, f - len(TW) + 1)
                        for oc in range(KC):
                            m = pe.transpose(TW[f % len(TW)][:, oc * P:(oc + 1) * P],
                                             raw[n % 2][:, oc, kc * P:(kc + 1) * P], identF[:, :])
                        m.then_inc(w_tr, 1)
                pe.wait_ge(m_ready, 1)
                pe.transpose(SC[1][:, 0:NB], mask_f[:, :], identF[0:NB, 0:NB]).then_inc(m_tr, 1)

            @block.scalar
            def _(act):
                act.wait_ge(gates_bc, 1)
                act.activation(c["tg"][:, :], SC[0][:, 0:4], ACT.Tanh).then_inc(tg_ready, 1)
                act.wait_ge(nw_in, 16)
                act.wait_ge(hg_ready, 1)
                for n, (dst, _, normed) in enumerate(names):
                    for kc in range(KC):
                        f = KC * n + kc
                        act.wait_ge(w_tr, f + 1)
                        act.activation(dst[:, 0, kc, :], TW[f % len(TW)][:, :], ACT.Copy,
                                       scale=scale_of(normed, kc)).then_inc(w_hi, 1)

            @block.vector
            def _(dve):
                dve.wait_ge(mask_in, 16)
                dve.tensor_copy(mask_f[:, :], mask_u8[:, :]).then_inc(m_ready, 1)
                dve.wait_ge(nw_in, 16)
                dve.wait_ge(hg_ready, 1)
                weight_lo(dve, 0)
                weight_lo(dve, 1)
                weight_lo(dve, 2)
                rows_stats(dve, 0)
                weight_lo(dve, 3)
                rows_stats(dve, 1)

            @block.sync
            def _(sp):
                def load(par, tile):
                    sp.dma_start(CT[:, par, :, :], ctx_in[bass.ds(tile, HG)].rearrange("b p d -> p b d"))\
                        .then_inc(c_in[par], 16)
                with sp.Fori(0, NG) as g:
                    for grp in (1, 2):
                        t_lo.wait(sp, g, at(SPLIT, ("cT", 1, HG - 1)) - len(of(SPLIT)) if grp == 1 else 0, c["passed_sp"])
                        load(grp % 2, tile_of(g, grp, 0))
                t_lo.wait(sp, NG - 1, at(SPLIT, ("cT", 1, HG - 1)))
                sp.dma_start(CT[:, 1, :, :], fw[0:2 * P, :].rearrange("(o p) k -> p o k", p=P)).then_inc(c["fw_in"], 16)
                sp.wait_ge(c_in[0], 16 * (NG + 1))
                t_lo.wait(sp, NG - 1, at(SPLIT, ("cT", 2, HG - 1)))
                sp.dma_start(CT[:, 0, :, :], fw[2 * P:4 * P, :].rearrange("(o p) k -> p o k", p=P)).then_inc(c["fw_in"], 16)

            @block.gpsimd
            def _(pool):
                added.grant(pool)
                for half in range(2):
                    row_power(pool, c, scales, powered, True, half)

                def add(b):
                    pool.tensor_tensor(X[:, g * GB + b, :], X[:, g * GB + b, :], upd[:, b % 2, :], ALU.add)\
                        .then_inc(added.sem, 1)
                with pool.Fori(0, NG) as g:
                    for b in range(GB):
                        m_dve.wait(pool, g, at(BY_DVE, ("oP", b)), c["passed_pool"])
                        add(b)

            @block.tensor
            def _(pe):
                def transposes(s, g, n):
                    kind = s[0]
                    bk = T[(n - 1) % 2]
                    if kind == "xT":
                        src = lambda k: xn[:, s[2] % 2, k * P:(k + 1) * P]
                    elif kind == "cT":
                        src = lambda k: CT[:, s[1] % 2, s[2], k * P:(k + 1) * P]
                    elif kind == "pT":
                        src = lambda k: pr[:, s[1] % 2, k, :]
                    else:
                        src = lambda k: o[:, s[1] % 2, k * P:(k + 1) * P]
                    for k in range(KC):
                        i = pe.transpose(bk[:, k * P:(k + 1) * P], src(k), identF[:, :])
                    i.then_inc(t_fill.sem, 1)

                def project(s, n):
                    kind, bk = s[0], M[(n - 1) % 2]
                    if kind in ("q", "k"):
                        w, a = (WQ, xT) if kind == "q" else (WK, cT)
                        for k in range(KC):
                            i = mm3(pe, bk[:, 0:GC], lambda h: w[:, h, k, s[2] * P:(s[2] + 1) * P],
                                    lambda h: a[:, s[1] % 2, h, k, :], k == 0, k == KC - 1)
                    else:
                        b = s[1]
                        w = {"v": WV, "g": WG, "oP": WO}[kind]
                        cols = slice(b % HG * S, b % HG * S + S)
                        for k in range(KC):
                            lhs = {"v": lambda h: cT[:, b // HG, h, k, cols], "g": lambda h: xT[:, b // HG, h, k, cols],
                                   "oP": lambda h: oT[:, h, k, :]}[kind]
                            i = mm3(pe, bk[:, :], lhs, lambda h: w[:, h, k, :], k == 0, k == KC - 1)
                    i.then_inc(m_fill.sem, 1)
                for s_ in (t_fill, m_fill, pv):
                    s_.grant(pe)
                pe.wait_ge(w_hi, KC * len(names))
                pe.wait_ge(w_lo, KC * len(names))
                pe.wait_ge(tg_ready, 1)
                pe.wait_ge(ones_set, 2)
                tf = mf = 0
                for s in prologue:
                    if s[0] in T_KINDS:
                        tf += 1
                        t_hi.wait(pe, 0, tf - 2 - 4)
                        t_lo.wait(pe, 0, tf - 2 - 4)
                        if s[0] == "xT":
                            pe.wait_ge(x_norm.sem, s[2] + 1)
                        else:
                            pe.wait_ge(c_in[0], 16)
                        transposes(s, None, tf)
                    else:
                        mf += 1
                        t_hi.wait(pe, 0, tf - 4)
                        t_lo.wait(pe, 0, tf - 4)
                        m_act.wait(pe, 0, mf - 2 - 2 * KC)
                        project(s, mf)
                m_act.wait(pe, 0, 0)
                pe.wait_ge(m_col, 1)
                with pe.Fori(0, NG) as g:
                    tf = mf = 0
                    for s in plan:
                        kind = s[0]
                        if kind in T_KINDS:
                            tf += 1
                            t_hi.wait(pe, g, tf - 2)
                            t_lo.wait(pe, g, upto(T_KINDS, SPLIT, tf - 2))
                            if kind == "xT":
                                x_norm.wait(pe, g, (s[1] - 1) * HG + s[2] + 1)
                            if kind == "cT" and s[2] == 0:
                                pe.wait_ge(c_in[s[1] % 2], 16 * g + 16 * s[1])
                            if kind == "pT":
                                p_exp.wait(pe, g, s[1] + 1)
                            if kind == "oT":
                                o_norm.wait(pe, g, 2 * s[1] + 2)
                            transposes(s, g, tf)
                        elif kind in M_KINDS:
                            mf += 1
                            m_act.wait(pe, g, upto(M_KINDS, BY_ACT, mf - 2))
                            m_dve.wait(pe, g, upto(M_KINDS, BY_DVE, mf - 2))
                            if kind in ("q", "k") and s[2] == 0:
                                t_lo.wait(pe, g, at(SPLIT, ("cT", s[1], HG - 1)))
                            if kind in ("v", "g"):
                                t_lo.wait(pe, g, at(SPLIT, ("cT", s[1] // HG, HG - 1)))
                            if kind == "oP":
                                t_lo.wait(pe, g, at(SPLIT, ("oT", s[1])))
                            project(s, mf)
                        elif kind == "S":
                            n = s[1]
                            b, r = n // HQ, n % HQ * HD
                            bk = SC[n % 2]
                            s_out.wait(pe, g, n - 1)
                            if r == 0:
                                mrow_ready.wait(pe, g, b + 1 - GB)
                                m_act.wait(pe, g, at(BY_ACT, ("k", b // HG, KC - 1)))
                            pe.matmul(bk[:, :].rearrange("p (j m) -> p j m", j=HQ), c["onesB"][r:r + 1, :],
                                      mrow[r:r + 1, b:b + 1, :].to_broadcast([1, HQ, S]), start=True, stop=False)
                            cols = slice(b % HG * S, b % HG * S + S)
                            for j in range(KC):
                                i = pe.matmul(bk[:, j * S:(j + 1) * S], qT[r:r + HD, b // HG, j, cols],
                                              kT[r:r + HD, b // HG, j, cols], start=False, stop=j == KC - 1)
                            i.then_inc(s_fill.sem, 1)
                        elif kind == "pv":
                            n = s[1]
                            b, r = n // HQ, n % HQ
                            t_hi.wait(pe, g, at(T_KINDS, ("pT", n)))
                            if r == 0:
                                m_dve.wait(pe, g, at(BY_DVE, ("v", b)))
                            if r % 2 == 0:
                                o_norm.wait(pe, g, 2 * b + r // 2 - 1)
                            for j in range(KC):
                                col = (r % 2 * HQ + j) * (HD + 1)
                                i = pe.matmul(O[r // 2][:, col:col + HD + 1], pT[:, n % 2, j, :],
                                              va[:, b % 2, j * HQ + r, :], start=True, stop=True)
                            i.then_inc(pv.sem, 1)

            @block.scalar
            def _(act):
                t_hi.grant(act)
                m_act.grant(act)

                def evac(s, n):
                    kind, src = s[0], (T if s[0] in T_KINDS else M)[(n - 1) % 2][:, :]
                    if kind in ("xT", "cT"):
                        dst = (xT if kind == "xT" else cT)[:, s[1] % 2, 0, :, s[2] * S:(s[2] + 1) * S]
                        act.activation(dst, src.rearrange("p (k t) -> p k t", k=KC), ACT.Copy).then_inc(t_hi.sem, 1)
                    elif kind == "pT":
                        act.activation(pT[:, s[1] % 2, :, :].rearrange("p j m -> p (j m)"), src, ACT.Copy).then_inc(t_hi.sem, 1)
                    elif kind == "oT":
                        act.activation(oT[:, 0, :, :].rearrange("p k t -> p (k t)"), src, ACT.Copy).then_inc(t_hi.sem, 1)
                    elif kind == "g":
                        act.activation(gs[:, s[1] % 2, :], src, ACT.Tanh, scale=0.5).then_inc(m_act.sem, 1)
                    else:
                        act.activation((qT if kind == "q" else kT)[:, s[1] % 2, s[2], :], src[:, 0:GC], ACT.Copy)\
                            .then_inc(m_act.sem, 1)
                tf = mf = 0
                for s in prologue:
                    if s[0] in T_KINDS:
                        tf += 1
                        t_fill.wait(act, 0, tf - 4)
                        evac(s, tf)
                    else:
                        mf += 1
                        m_fill.wait(act, 0, mf - 2 * KC)
                        evac(s, mf)
                with act.Fori(0, NG) as g:
                    tf = mf = 0
                    for s in plan:
                        kind = s[0]
                        if kind in T_KINDS:
                            tf += 1
                            t_fill.wait(act, g, tf)
                            if kind in ("xT", "cT"):
                                if s[1] == 1:
                                    m_fill.wait(act, g, at(M_KINDS, ("g", -1)))
                                else:
                                    m_fill.wait(act, g, at(M_KINDS, ("g", HG - 1)))
                            elif kind == "pT":
                                pv.wait(act, g, s[1] - 1)
                            else:
                                m_fill.wait(act, g, at(M_KINDS, ("oP", s[1] - 1)))
                            evac(s, tf)
                        elif kind in M_KINDS:
                            mf += 1
                            if kind not in BY_ACT:
                                continue
                            m_fill.wait(act, g, mf)
                            if kind == "g":
                                m_dve.wait(act, g, at(BY_DVE, ("oP", s[1] - 2)))
                            else:
                                s_out.wait(act, g, 0 if s[1] == 1 else NQ // 2)
                            evac(s, mf)
                        elif kind == "S":
                            n = s[1]
                            s_out.wait(act, g, n + 1)
                            pp = pr[:, n % 2, :, :].rearrange("p j m -> p (j m)")
                            act.activation(pp, pp, ACT.Exp, scale=SCALE0).then_inc(p_exp.sem, 1)

            @block.vector
            def _(dve):
                for s_ in (t_lo, m_dve, s_out, o_norm):
                    s_.grant(dve)

                def norm(tile, j):
                    dve.tensor_scalar(xn[:, j % 2, :], X[:, tile, :], c["mean"][:, bass.ds(tile, 1)],
                                      c["rstd"][:, bass.ds(tile, 1)], ALU.subtract, ALU.mult).then_inc(x_norm.sem, 1)

                def lo(s, n):
                    src = T[(n - 1) % 2][:, :]
                    if s[0] == "oT":
                        hi_, lo_ = (oT[:, h, :, :].rearrange("p k t -> p (k t)") for h in range(2))
                    else:
                        a = xT if s[0] == "xT" else cT
                        hi_, lo_ = (a[:, s[1] % 2, h, :, s[2] * S:(s[2] + 1) * S] for h in range(2))
                        src = src.rearrange("p (k t) -> p k t", k=KC)
                    dve.tensor_tensor(lo_, src, hi_.bitcast(F32), ALU.subtract).then_inc(t_lo.sem, 1)

                def mask_row(tile, b):
                    dve.tensor_scalar(mrow[:, b:b + 1, :], mask_all[:, bass.ds(tile, 1), :],
                                      -1.0, -MASKED, ALU.add, ALU.mult).then_inc(mrow_ready.sem, 1)

                def prologue_lo(kind):
                    for n, s in enumerate([s for s in prologue if s[0] in T_KINDS]):
                        if s[0] == kind:
                            t_hi.wait(dve, 0, n + 1 - 4)
                            lo(s, n + 1)
                dve.wait_ge(seen, NB // 2)
                row_scale(dve, c, scales, powered, 1e-5, 1e-6, (lambda: weight_lo(dve, 4), lambda: prologue_lo("cT")), half=0)
                norm(0, 0)
                norm(1, 1)
                dve.wait_ge(m_tr, 1)
                dve.tensor_copy(mcol[:, :], SC[1][:, 0:NB]).then_inc(m_col, 1)
                dve.wait_ge(mask_all_in, 16)
                for b in range(GB):
                    mask_row(b, b)
                rows_stats(dve, 2)
                rows_stats(dve, 3)
                dve.wait_ge(seen, NB)
                row_scale(dve, c, scales, powered, 1e-5, 1e-6, (lambda: prologue_lo("xT"), lambda: None), half=1)
                with dve.Fori(0, NG) as g:
                    tf = mf = 0
                    def stats(b):
                        tile = g * GB + b if b >= 0 else (g * GB + NB - 1) % NB
                        added.wait(dve, g, b + 1, c["passed_dve"])
                        dve.bn_stats(c["bst"][:, tile, :], X[:, tile, :])

                    t_fill.wait(dve, g, 0)
                    norm(tile_of(g, 1, 0), 0)
                    for s in plan:
                        kind = s[0]
                        if kind in T_KINDS:
                            tf += 1
                            if kind in SPLIT:
                                t_hi.wait(dve, g, tf)
                                lo(s, tf)
                        elif kind in M_KINDS:
                            mf += 1
                            if kind not in BY_DVE:
                                continue
                            b = s[1]
                            m_fill.wait(dve, g, mf)
                            if kind == "v":
                                pv.wait(dve, g, (b - 1) * HQ)
                                dve.tensor_scalar(va[:, b % 2, :, 0:HD],
                                                  M[(mf - 1) % 2][:, :].rearrange("p (h d) -> p h d", h=NH),
                                                  mcol[:, bass.ds(g * GB + b, 1)], None, ALU.mult).then_inc(m_dve.sem, 1)
                            else:
                                m_act.wait(dve, g, at(BY_ACT, ("g", b)))
                                added.wait(dve, g, b - 1)
                                dve.scalar_tensor_tensor(out=upd[:, b % 2, :], in0=gs[:, b % 2, :], scalar=1.0,
                                                         in1=M[(mf - 1) % 2][:, :], op0=ALU.add, op1=ALU.mult)\
                                    .then_inc(m_dve.sem, 1)
                                if b:
                                    stats(b - 1)
                        elif kind == "S":
                            n = s[1]
                            s_fill.wait(dve, g, n + 1)
                            sc = SC[n % 2][:, :].rearrange("p (j m) -> p j m", j=HQ)
                            dve.tensor_reduce(mx[:, n % 2, :], sc, AX.X, ALU.max).then_inc(s_max.sem, 1)
                            s_max.wait(dve, g, n + 1)
                            t_fill.wait(dve, g, at(T_KINDS, ("pT", n - 2)))
                            dve.tensor_tensor(pr[:, n % 2, :, :], sc, mx[:, n % 2, :].unsqueeze(2).to_broadcast([P, HQ, S]),
                                              ALU.subtract).then_inc(s_out.sem, 1)
                            if n == 0:
                                norm(tile_of(g, 1, 1), 1)
                            if n == 1:
                                stats(-1)
                            if n == NQ // 2 - 1:
                                for j in range(HG):
                                    t_fill.wait(dve, g, at(T_KINDS, ("xT", 1, j)))
                                    norm(tile_of(g, 2, j), j)
                            if n % HQ == HQ - 1:
                                mask_row(tile_of(g, 2, n // HQ), n // HQ)
                        elif kind == "on":
                            n = s[1]
                            b, half = n // 2, n % 2
                            pv.wait(dve, g, 2 * n + 2)
                            ov = O[half][:, 0:2 * HQ * (HD + 1)].rearrange("p (r j d) -> p r j d", r=2, j=HQ)
                            dve.reciprocal(rs[:, half, :, :], ov[:, :, :, HD]).then_inc(o_rec.sem, 1)
                            o_rec.wait(dve, g, n + 1)
                            if half == 0:
                                t_fill.wait(dve, g, at(T_KINDS, ("oT", b - 2)))
                            oo = o[:, b % 2, :].rearrange("p (j r d) -> p r j d", j=KC, r=HQ)
                            dve.tensor_tensor(oo[:, 2 * half:2 * half + 2, :, :], ov[:, :, :, 0:HD],
                                              rs[:, half, :, :].unsqueeze(3).to_broadcast([P, 2, HQ, HD]),
                                              ALU.mult).then_inc(o_norm.sem, 1)
                added.wait(dve, NG - 1, GB)
                dve.bn_stats(c["bst"][:, NB - 1, :], X[:, NB - 1, :])


def ternary_ffn(nc, c, fb):
    X = c["X"]
    PAIR = 2
    with ExitStack() as st:
        def sb(name, shape, dt=F32):
            return st.enter_context(nc.sbuf_tensor(name, shape, dt))

        def sem(name):
            return st.enter_context(nc.semaphore(name))

        def bank(name, n):
            return [st.enter_context(nc.psum_tensor(f"{name}{i}", [P, 512], F32)) for i in range(n)]

        raw = [c["CT"][:, 1 - o // 2, o % 2, :] for o in range(KC)]
        sm = sb("fsm", [P, 4, KC])
        wr = sb("fwr", [P, KC, D])
        wt = sb("fwt", [P, KC, D], BF16)
        wT = sb("fwT", [P, KC, D], BF16)
        dg = sb("fdg", [P, KC, P])
        bias1 = sb("fbias", [1, D])
        grow = sb("fgrow", [P, D])
        brow = sb("fbrow", [P, D])
        u = sb("fu", [P, 2, PAIR, D])
        ur = sb("fur", [P, 2, PAIR, D])
        uT = sb("fuT", [P, 2, PAIR, D], BF16)
        sc = sb("fsc", [P, 2, 4, PAIR])
        upd = sb("fupd", [P, 2, PAIR, D])
        TB = bank("fTB", 4)
        M = bank("fM", 4)
        u_done, powered = sem("f_u_done"), sem("f_powered")
        b_in, prep, w_tr, w_out, rows, rows_out, scales = (sem(f"f_{n}") for n in (
            "b_in", "prep", "w_tr", "w_out", "rows", "rows_out", "scales"))
        q_sc = Count(sem("q_sc"), 2)
        q_small = Count(sem("q_small"), 3 * 2)
        q_done = Count(sem("q_done"), 2 * PAIR, True)
        t_fill = Count(sem("ft_fill"), 2 * PAIR, True)
        t_out = Count(sem("ft_out"), 2 * PAIR, True)
        m_fill = Count(sem("fm_fill"), 2 * PAIR, True)
        m_out = Count(sem("fm_out"), 2 * PAIR, True)
        biased = Count(sem("f_biased"), 2 * PAIR)
        added = Count(sem("f_added"), 2 * PAIR, True)

        def of(g, p, b):
            return ((g + 1) * GB) % NB + b if p == 2 else (g * GB + NB - PAIR) % NB + b if p < 0 else g * GB + PAIR * p + b

        PREP = 2 + 3 + KC + 1 + KC + 1
        with nc.Block() as block:
            @block.sync
            def _(sp):
                sp.dma_start(bias1[:, :], fb.rearrange("(a n) -> a n", a=1)).then_inc(b_in, 16)

            @block.vector
            def _(dve):
                m_out.grant(dve)
                q_done.grant(dve)
                n = 0

                def step(instr):
                    nonlocal n
                    n += 1
                    instr.then_inc(prep, 1)
                    dve.wait_ge(prep, n)

                def magnitudes():
                    dve.wait_ge(c["fw_in"], 32)
                    for half in range(2):
                        step(dve.tensor_reduce(sm[:, 0, 2 * half:2 * half + 2], c["CT"][:, 1 - half, :, :], AX.X, ALU.add,
                                               apply_absolute_value=True))
                    step(dve.tensor_scalar(sm[:, 1, :], sm[:, 0, :], 1.0 / D, None, ALU.mult))
                    step(dve.tensor_scalar(sm[:, 2, :], sm[:, 1, :], 1e-8, None, ALU.add))
                    step(dve.reciprocal(sm[:, 3, :], sm[:, 2, :]))

                def rounded():
                    for o in range(KC):
                        step(dve.tensor_scalar(wr[:, o, :], raw[o], sm[:, 3, o:o + 1], ROUND, ALU.mult, ALU.add))
                    step(dve.tensor_scalar(wr[:, :, :], wr[:, :, :], -ROUND, 1.0, ALU.add, ALU.min))
                row_scale(dve, c, scales, powered, 1e-5, 1e-8, (magnitudes, rounded))
                for o in range(KC):
                    step(dve.tensor_scalar(dg[:, o, :], c["identF"][:, :], sm[:, 1, o:o + 1], None, ALU.mult))
                step(dve.tensor_scalar(wt[:, :, :], wr[:, :, :], -1.0, None, ALU.max))

                def quantise(g, p):
                    par, k = p % 2, PAIR * p
                    for b in range(PAIR):
                        t = of(g, p, b)
                        dve.tensor_scalar(u[:, par, b, :], X[:, t, :], c["mean"][:, bass.ds(t, 1)], c["rstd"][:, bass.ds(t, 1)],
                                          ALU.subtract, ALU.mult).then_inc(u_done, 1)
                    dve.wait_ge(u_done, PAIR * (2 * g + p + 1))
                    dve.tensor_reduce(sc[:, par, 0, :], u[:, par, :, :], AX.X, ALU.max, apply_absolute_value=True)\
                        .then_inc(q_sc.sem, 1)
                    q_sc.wait(dve, g, p + 1)
                    for n, f in enumerate((lambda o, i: dve.tensor_scalar(o, i, 1.0 / 127.0, None, ALU.mult),
                                           lambda o, i: dve.tensor_scalar(o, i, 1e-8, None, ALU.add), dve.reciprocal)):
                        f(sc[:, par, n + 1, :], sc[:, par, n, :]).then_inc(q_small.sem, 1)
                        q_small.wait(dve, g, 3 * p + n + 1)
                    for b in range(PAIR):
                        t_fill.wait(dve, g, k + b + 1 - 2 * PAIR)
                        dve.tensor_scalar(ur[:, par, b, :], u[:, par, b, :], sc[:, par, 3, b:b + 1], ROUND, ALU.mult, ALU.add)\
                            .then_inc(q_done.sem, 1)
                quantise(0, 0)
                dve.wait_ge(rows_out, 1)
                with dve.Fori(0, NG) as g:
                    for p in range(2):
                        quantise(g, p + 1)
                        for b in range(PAIR):
                            m_fill.wait(dve, g, PAIR * p + b + 1)
                            added.wait(dve, g, PAIR * (p - 2) + b + 1)
                            dve.scalar_tensor_tensor(out=upd[:, p, b, :], in0=M[PAIR * p + b][:, :], scalar=sc[:, p, 1, b:b + 1],
                                                     in1=grow[:, :], op0=ALU.mult, op1=ALU.mult).then_inc(m_out.sem, 1)
                        for b in range(PAIR):
                            t = of(g, p - 1, b)
                            added.wait(dve, g, PAIR * (p - 1) + b + 1, c["passed_dve"])
                            dve.bn_stats(c["bst"][:, t, :], X[:, t, :])
                for b in range(PAIR):
                    t = NB - PAIR + b
                    added.wait(dve, NG - 1, PAIR + b + 1)
                    dve.bn_stats(c["bst"][:, t, :], X[:, t, :])

            @block.gpsimd
            def _(pool):
                added.grant(pool)
                row_power(pool, c, scales, powered, True)
                pool.wait_ge(rows_out, 2)
                with pool.Fori(0, NG) as g:
                    for p in range(2):
                        for b in range(PAIR):
                            t, k = of(g, p, b), PAIR * p + b + 1
                            q_done.wait(pool, g, k, c["passed_pool"])
                            pool.tensor_tensor(X[:, t, :], X[:, t, :], brow[:, :], ALU.add).then_inc(biased.sem, 1)
                        for b in range(PAIR):
                            t, k = of(g, p, b), PAIR * p + b + 1
                            m_out.wait(pool, g, k, c["passed_pool"])
                            biased.wait(pool, g, k, c["passed_pool"])
                            pool.tensor_tensor(X[:, t, :], X[:, t, :], upd[:, p, b, :], ALU.add).then_inc(added.sem, 1)

            @block.scalar
            def _(act):
                t_out.grant(act)

                def uT_out(g, p):
                    for b in range(PAIR):
                        k = PAIR * p + b + 1
                        t_fill.wait(act, g, k)
                        m_fill.wait(act, g, k - 2 * PAIR)
                        act.activation(uT[:, p % 2, b, :], TB[(PAIR * p + b) % 4][:, :], ACT.Copy, bias=-ROUND)\
                            .then_inc(t_out.sem, 1)
                for k in range(KC):
                    act.wait_ge(w_tr, k + 1)
                    act.activation(wT[:, k, :], TB[k][:, :].bitcast(BF16)[:, 0:D], ACT.Copy).then_inc(w_out, 1)
                for i, (dst, n) in enumerate(((grow, 2), (brow, 2))):
                    act.wait_ge(rows, i + 1)
                    act.activation(dst[:, :], M[i][:, :], ACT.Copy, scale=c["tg"][:, n:n + 1]).then_inc(rows_out, 1)
                uT_out(0, 0)
                with act.Fori(0, NG) as g:
                    for p in range(2):
                        uT_out(g, p + 1)

            @block.tensor
            def _(pe):
                t_fill.grant(pe)
                m_fill.grant(pe)

                def transposes(g, p):
                    for b in range(PAIR):
                        k = PAIR * p + b + 1
                        q_done.wait(pe, g, k)
                        t_out.wait(pe, g, k - 2 * PAIR)
                        for j in range(KC):
                            x_ = pe.transpose(TB[(PAIR * p + b) % 4][:, j * P:(j + 1) * P], ur[:, p % 2, b, j * P:(j + 1) * P],
                                              c["identF"][:, :])
                        x_.then_inc(t_fill.sem, 1)
                pe.wait_ge(prep, PREP)
                for k in range(KC):
                    for o in range(KC):
                        i = pe.transpose(TB[k][:, :].bitcast(BF16)[:, o * P:(o + 1) * P],
                                         wt[:, o, k * P:(k + 1) * P], c["identB"][:, :])
                    i.then_inc(w_tr, 1)
                for o in range(KC):
                    i = pe.matmul(M[0][:, o * P:(o + 1) * P], c["onesF"][:, :], dg[:, o, :], start=True, stop=True)
                i.then_inc(rows, 1)
                pe.wait_ge(b_in, 16)
                pe.matmul(M[1][:, :], c["onesF"][0:1, :], bias1[:, :], start=True, stop=True).then_inc(rows, 1)
                pe.wait_ge(w_out, KC)
                transposes(0, 0)
                pe.wait_ge(rows_out, 2)
                with pe.Fori(0, NG) as g:
                    for p in range(2):
                        for b in range(PAIR):
                            k = PAIR * p + b + 1
                            t_out.wait(pe, g, k)
                            m_out.wait(pe, g, k - 2 * PAIR)
                            for j in range(KC):
                                x_ = pe.matmul(M[PAIR * p + b][:, :], uT[:, p, b, j * P:(j + 1) * P], wT[:, j, :],
                                               start=j == 0, stop=j == KC - 1)
                            x_.then_inc(m_fill.sem, 1)
                        transposes(g, p + 1)


def attention_features(nc, c, ctx_in):
    X = c["X"]
    with ExitStack() as st:
        def sb(name, shape, dt=F32):
            return st.enter_context(nc.sbuf_tensor(name, shape, dt))

        def sem(name):
            return st.enter_context(nc.semaphore(name))

        def bank(name, n):
            return [st.enter_context(nc.psum_tensor(f"{name}{i}", [P, 512], F32)) for i in range(n)]

        CX = sb("aCX", [P, GB, D])
        xn = sb("axn", [P, 2, D])
        q = sb("aq", [P, 2, 2, D], F32R)
        k_ = sb("ak", [P, 2, 2, D], F32R)
        vT = sb("avT", [P, 2, 2, D], F32R)
        sg = sb("asg", [P, KC, D])
        s = sb("as", [P, KC, 2, D], F32R)
        T, SC, O = bank("aT", 2), bank("aSC", KC), bank("aO", 2)
        scales, powered = sem("a_scales"), sem("a_powered")
        NS = GB * KC
        c_in = [sem(f"ac_in{b}") for b in range(GB)]
        normed, q_hi, k_hi, v_hi, q_lo, k_lo, t_fill = (
            Count(sem(f"a_{n}"), GB) for n in ("normed", "q_hi", "k_hi", "v_hi", "q_lo", "k_lo", "t_fill"))
        v_lo, x_new = Count(sem("a_v_lo"), GB, True), Count(sem("a_x_new"), GB, True)
        s_fill = Count(sem("as_fill"), NS)
        s_hi = Count(sem("as_hi"), NS, True)
        s_lo = Count(sem("as_lo"), NS, True)
        s_used = Count(sem("as_used"), NS, True)

        def tile_of(g, b):
            return g * GB + b if b < GB else ((g + 1) * GB) % NB + b - GB

        with nc.Block() as block:
            @block.sync
            def _(sp):
                def load(tile, b):
                    sp.dma_start(CX[:, b, :], ctx_in[bass.ds(tile, 1)].rearrange("b p d -> p (b d)")).then_inc(c_in[b], 16)
                for b in range(GB):
                    load(b, b)
                with sp.Fori(0, NG) as g:
                    for b in range(GB):
                        t_fill.wait(sp, g, b + 1, c["passed_sp"])
                        k_lo.wait(sp, g, b + 1, c["passed_sp"])
                        load(tile_of(g, b + GB), b)
                for b in range(GB):
                    sp.wait_ge(c_in[b], 16 * (NG + 1))

            @block.vector
            def _(dve):
                for s_ in (s_lo, x_new, v_lo):
                    s_.grant(dve)
                row_scale(dve, c, scales, powered, 1e-5)

                def norm(g, b):
                    t = tile_of(g, b)
                    dve.tensor_scalar(xn[:, b % 2, :], X[:, t, :], c["mean"][:, bass.ds(t, 1)], c["rstd"][:, bass.ds(t, 1)],
                                      ALU.subtract, ALU.mult).then_inc(normed.sem, 1)

                def v_low(g, b):
                    v_hi.wait(dve, g, b + 1)
                    dve.tensor_tensor(vT[:, b % 2, 1, :], T[b % 2][:, :], vT[:, b % 2, 0, :].bitcast(F32), ALU.subtract)\
                        .then_inc(v_lo.sem, 1)

                def s_low(g, m):
                    s_hi.wait(dve, g, m + 1)
                    dve.tensor_tensor(s[:, m % KC, 1, :], sg[:, m % KC, :], s[:, m % KC, 0, :].bitcast(F32), ALU.subtract)\
                        .then_inc(s_lo.sem, 1)
                norm(0, 0)
                norm(0, 1)
                v_low(0, 0)
                s_low(0, 0)
                s_low(0, 1)
                with dve.Fori(0, NG) as g:
                    for m in range(NS):
                        b, n = m // KC, m % KC
                        s_low(g, m + 2)
                        if n == 0:
                            q_lo.wait(dve, g, b + 1)
                            norm(g, b + 2)
                        if n == 2:
                            v_low(g, b + 1)
                        if n == KC - 1:
                            t = tile_of(g, b)
                            s_used.wait(dve, g, m + 1)
                            dve.scalar_tensor_tensor(out=X[:, t, :], in0=O[b % 2][:, :], scalar=c["tg"][:, 1:2], in1=X[:, t, :],
                                                     op0=ALU.mult, op1=ALU.add).then_inc(x_new.sem, 1)
                            x_new.wait(dve, g, b + 1, c["passed_dve"])
                            dve.bn_stats(c["bst"][:, t, :], X[:, t, :])

            @block.gpsimd
            def _(pool):
                def split(g, b):
                    pool.tensor_copy(k_[:, b % 2, 0, :], CX[:, b % GB, :]).then_inc(k_hi.sem, 1)
                    k_hi.wait(pool, g, b + 1, c["passed_pool"])
                    pool.tensor_tensor(k_[:, b % 2, 1, :], CX[:, b % GB, :], k_[:, b % 2, 0, :].bitcast(F32), ALU.subtract)\
                        .then_inc(k_lo.sem, 1)
                    q_hi.wait(pool, g, b + 1, c["passed_pool"])
                    pool.tensor_tensor(q[:, b % 2, 1, :], xn[:, b % 2, :], q[:, b % 2, 0, :].bitcast(F32), ALU.subtract)\
                        .then_inc(q_lo.sem, 1)
                row_power(pool, c, scales, powered)
                for b in range(2):
                    pool.wait_ge(c_in[b], 16)
                    split(0, b)
                with pool.Fori(0, NG) as g:
                    for b in range(GB):
                        s_fill.wait(pool, g, (b + 1) * KC, c["passed_pool"])
                        pool.wait_ge(c_in[(b + 2) % GB], 16 * (g + 1) if b + 2 < GB else 16 * (g + 2))
                        pool.sem_inc(c["passed_pool"], 1)
                        split(g, b + 2)

            @block.scalar
            def _(act):
                s_hi.grant(act)

                def sigmoids(g, m):
                    s_fill.wait(act, g, m + 1)
                    s_lo.wait(act, g, m + 1 - KC)
                    act.activation(sg[:, m % KC, :], SC[m % KC][:, :], ACT.Sigmoid, scale=SCALE1)
                    s_used.wait(act, g, m + 1 - KC)
                    act.activation(s[:, m % KC, 0, :], SC[m % KC][:, :], ACT.Sigmoid, scale=SCALE1).then_inc(s_hi.sem, 1)

                def q_high(g, b):
                    normed.wait(act, g, b + 1)
                    act.activation(q[:, b % 2, 0, :], xn[:, b % 2, :], ACT.Copy).then_inc(q_hi.sem, 1)

                def v_high(g, b):
                    t_fill.wait(act, g, b + 1)
                    act.activation(vT[:, b % 2, 0, :], T[b % 2][:, :], ACT.Copy).then_inc(v_hi.sem, 1)
                q_high(0, 0)
                v_high(0, 0)
                q_high(0, 1)
                sigmoids(0, 0)
                sigmoids(0, 1)
                with act.Fori(0, NG) as g:
                    for m in range(NS):
                        b, n = m // KC, m % KC
                        sigmoids(g, m + 2)
                        if n == 2:
                            s_used.wait(act, g, b * KC)
                            v_high(g, b + 1)
                        if n == 3:
                            s_fill.wait(act, g, (b + 1) * KC)
                            q_high(g, b + 2)

            @block.tensor
            def _(pe):
                s_used.grant(pe)

                def transposes(g, b):
                    for k in range(KC):
                        x_ = pe.transpose(T[b % 2][:, k * P:(k + 1) * P], CX[:, b % GB, k * P:(k + 1) * P], c["identF"][:, :])
                    x_.then_inc(t_fill.sem, 1)

                def score(g, m):
                    b, n = m // KC, m % KC
                    if n == 0:
                        q_lo.wait(pe, g, b + 1)
                    mm3(pe, SC[m % KC][:, :], lambda h: q[:, b % 2, h, n * P:(n + 1) * P], lambda h: k_[:, b % 2, h, :],
                        True, True).then_inc(s_fill.sem, 1)
                pe.wait_ge(c_in[0], 16)
                transposes(0, 0)
                for m in range(3):
                    score(0, m)
                with pe.Fori(0, NG) as g:
                    for m in range(NS):
                        b, n = m // KC, m % KC
                        s_hi.wait(pe, g, m)
                        score(g, m + 3)
                        s_lo.wait(pe, g, m + 1)
                        if n == 0:
                            v_lo.wait(pe, g, b + 1)
                            x_new.wait(pe, g, b - 1)
                        mm3(pe, O[b % 2][:, :], lambda h: vT[:, b % 2, h, n * P:(n + 1) * P], lambda h: s[:, m % KC, h, :],
                            n == 0, n == KC - 1).then_inc(s_used.sem, 1)
                        if n == 1:
                            pe.wait_ge(c_in[(b + 1) % GB], 16 * (g + 1) if b + 1 < GB else 16 * (g + 2))
                            v_lo.wait(pe, g, b)
                            transposes(g, b + 1)


def experts(nc, c, gate_w, ebias, w1, w2, w3, sw1, sw2, sw3, out):
    rows_d = nc.dram_tensor("rows_d", [T_ALL + PADS, D], F32, kind="Internal").ap()
    acc_d = nc.dram_tensor("acc_d", [T_ALL + PADS, D], F32, kind="Internal").ap()
    table_d = nc.dram_tensor("table_d", [NT * P, 2], F32, kind="Internal").ap()
    with ExitStack() as st:
        def sb(name, shape, dt=F32):
            return st.enter_context(nc.sbuf_tensor(name, shape, dt))
        m = dict(meta=sb("m_meta", [1, 3, NT + 3], I32),
                 pos=sb("m_pos", [P, NB, 8]), posu=sb("m_posu", [P, NB, TOPK], U32),
                 pair=sb("m_pair", [P, NB, TOPK, 2]), rows_d=rows_d, acc_d=acc_d, table_d=table_d,
                 stored=st.enter_context(nc.semaphore("stored")),
                 rowid=sb("m_rowid", [P, NT + 3], U32), wgt=sb("m_wgt", [P, NT + 3]),
                 r13=sb("m_r13", [P, KC, 2, I]), r2=sb("m_r2", [P, 3, D]),
                 W13=sb("m_W13", [P, 2, KC, 2, I], F32R), W2=sb("m_W2", [P, 2, 3, D], F32R))
        routing_and_shared_expert(nc, c, m, gate_w, ebias, w1, w2, w3, sw1, sw2, sw3)
        expert_tiles(nc, c, m, w1, w2, w3, out)


def load_expert(sp, m, w1, w3, e, done):
    for j, w in enumerate((w1, w3)):
        sp.dma_start(m["r13"][:, :, j, :], w[bass.ds(e, 1)].rearrange("e (k p) i -> p (e k) i", p=P)).then_inc(done, 16)


def load_expert_out(sp, m, w2, e, done):
    sp.dma_start(m["r2"][:, 0:2, :], w2[bass.ds(e, 1), 0:2 * P, :].rearrange("e (k p) i -> p (e k) i", p=P)).then_inc(done, 16)
    sp.dma_start(m["r2"][0:IC[2], 2, :], w2[bass.ds(e, 1), 2 * P:I, :].rearrange("e p i -> p (e i)")).then_inc(done, 16)


def routing_and_shared_expert(nc, c, m, gate_w, ebias, w1, w2, w3, sw1, sw2, sw3):
    X = c["X"]
    with ExitStack() as st:
        def sb(name, shape, dt=F32):
            return st.enter_context(nc.sbuf_tensor(name, shape, dt))

        def sem(name):
            return st.enter_context(nc.semaphore(name))

        def bank(name, n):
            return [st.enter_context(nc.psum_tensor(f"{name}{i}", [P, 512], F32)) for i in range(n)]
        XT = sb("XT", [P, 2, KC, NB * S], F32R)
        r1, r3, r2 = m["r13"][:, :, 0, :], m["r13"][:, :, 1, :], m["r2"][:, :, :]
        W1, W3, W2 = [m["W13"][:, :, :, 0, :]], [m["W13"][:, :, :, 1, :]], [m["W2"][:, :, :, :]]
        sl = sb("esl", [P, 2, D])
        h = sb("eh", [P, 1, D])
        hT = sb("ehT", [P, 2, 3, GT], F32R)
        A, B, Y = bank("eA", 2), bank("eB", 2), bank("eY", 2)
        T = Y
        L, CP = bank("eL", 1)[0], bank("eC", 1)[0]
        G, CT_, PT = CP[:, 0:KC * E], CP[:, 0:NB * E], CP[:, NB * E:2 * NB * E]
        LR = PT
        gw = h[0:E, 0, :]
        gwT = sb("egwT", [P, 2, KC, E], F32R)
        b1 = sb("eb1", [1, E])
        triB = sb("r_triB", [P, P], BF16)
        selB = sb("r_selB", [P, NB, E], BF16)
        J = NT + 3
        iE = sb("r_iE", [P, E])
        iJ = sb("r_iJ", [P, NT + 3])
        tok = sb("r_tok", [P, NB])
        sb_ = sb("r_sb", [P, NB, E])
        tab = sb_[0:NT, :, :].rearrange("j t e -> j (t e)").rearrange("j (p a) -> j p a", a=2)
        tri, bias = sb("r_tri", [P, EG, EG]), sb("r_bias", [P, E])
        total, cnt_ = sb("r_sum", [P, 2, NB]), sb("r_n", [P, 5, E])
        NX = 4
        with ExitStack() as shortly:
            before_w1, before_w3, before_w2 = (shortly.enter_context(nc.sbuf_tensor(f"before_{n}", [P, w], F32))[:, :]
                                               for n, w in (("w1", 2 * KC * I), ("w3", 2 * KC * I), ("w2", 6 * D)))
        for W_, n, k, w in ((W1, "W1", KC, I), (W3, "W3", KC, I), (W2, "W2", 3, D)):
            W_.append(sb(f"e{n}1", [P, 2, k, w], F32R))
        early = before_w1
        xn = early[:, 0:NX * D].rearrange("p (b d) -> p b d", b=NX)
        zrow = early[:, NX * D:(NX + 1) * D]
        pad = early[0:NT, (NX + 1) * D:(NX + 1) * D + 2 * P].rearrange("j (p a) -> j p a", a=2)
        early = before_w3
        above, same, before0, before1, s, sel = (
            early[:, n * NB * E:(n + 1) * NB * E].rearrange("p (t e) -> p t e", t=NB) for n in range(6))
        early = early[:, 6 * NB * E:]
        top8 = early[:, 0:NB * 8].rearrange("p (t n) -> p t n", t=NB)
        grp = early[:, NB * 8:NB * 20].rearrange("p (n t g) -> p n t g", n=3, t=NB)
        lgT = early[0:E, NB * 28 + P:NB * 28 + P + GT]
        ti, tp = early[:, NB * 20:NB * 20 + NT + 3].bitcast(I32), early[0:NT, NB * 28:NB * 28 + P].bitcast(I32)
        early = before_w2
        run = early[:, 0:2 * NB * E].rearrange("p (a t e) -> p a t e", a=2, t=NB)
        big, eq = early[:, 2 * NB * E:6 * NB * E + 2 * J], early[:, 6 * NB * E + 2 * J:6 * NB * E + 2 * J + J * E]
        first, nxt = big[:, NB * TOPK * E:NB * TOPK * E + J], big[:, NB * TOPK * E + J:]
        (g_in, scales, powered, tri_ok, gt, g_hi, g_lo, bias_ps, normed, t_fill, t_hi, t_lo, logits, sig, routed,
         iotas, counted, sel_ok, meta_ok, pads_in) = (
            sem(f"e_{n}") for n in ("g_in", "scales", "powered", "tri", "gt", "g_hi", "g_lo", "bias_ps", "normed",
                                    "t_fill", "t_hi", "t_lo", "logits", "sig", "routed", "iotas", "counted", "sel_ok",
                                    "meta_ok", "pads_in"))
        row_out = [sem(f"e_row_out{b}") for b in range(NX)]
        w13_in, w2_in, w_hi, w_lo = sem("ew13_in"), sem("ew2_in"), sem("ew_hi"), sem("ew_lo")
        lg_fill, lg_out = sem("e_lg_fill"), sem("e_lg_out")
        x13_in, x2_in, x13_hi = sem("ex13_in"), sem("ex2_in"), sem("ex13_hi")
        tab_in, tab_tr = sem("e_tab_in"), sem("e_tab_tr")
        NU = NSH * NG
        ab_fill, a_out, b_out, h_hi, h_lo, y_fill, y_out = (sem(f"e{n}") for n in (
            "ab_fill", "a_out", "b_out", "h_hi", "h_lo", "y_fill", "y_out"))
        placed, stored = sem("placed"), m["stored"]
        PARTS = 4
        SPLIT_AT = (8, 10, 13, 14)
        EXPERT_AT = (18, 19, 20, 21)

        def part(b, n):
            raw, dst, pp, ks = ((r1, W1[b], P, slice(0, KC)), (r3, W3[b], P, slice(0, KC)), (r2, W2[b], P, slice(0, 2)),
                                (r2, W2[b], IC[2], slice(2, 3)))[n]
            return raw[0:pp, ks, :], dst[0:pp, 0, ks, :], dst[0:pp, 1, ks, :]

        def wait(eng, s_, n):
            if n > 0:
                eng.wait_ge(s_, n)
        with nc.Block() as block:
            @block.sync
            def _(sp):
                def load(b):
                    cols = slice(b * I, (b + 1) * I)
                    sp.dma_start(r1[:, :, :], sw1[:, cols].rearrange("(k p) i -> p k i", p=P)).then_inc(w13_in, 16)
                    sp.dma_start(r3[:, :, :], sw3[:, cols].rearrange("(k p) i -> p k i", p=P)).then_inc(w13_in, 16)
                    sp.dma_start(r2[:, 0:2, :], sw2[b * I:b * I + 2 * P, :].rearrange("(k p) i -> p k i", p=P)).then_inc(w2_in, 16)
                    sp.dma_start(r2[0:IC[2], 2, :], sw2[b * I + 2 * P:(b + 1) * I, :]).then_inc(w2_in, 16)
                sp.dma_start(gw, gate_w).then_inc(g_in, 16)
                sp.dma_start(b1[:, :], ebias.rearrange("(a n) -> a n", a=1)).then_inc(g_in, 16)
                load(0)
                for t in range(NB):
                    sp.wait_ge(normed, t + 1)
                    sp.dma_start(m["rows_d"][t * P:(t + 1) * P, :], xn[:, t % NX, :]).then_inc(row_out[t % NX], 16)
                sp.wait_ge(iotas, 9)
                sp.dma_start(m["rows_d"][T_ALL:T_ALL + PADS, :], zrow).then_inc(pads_in, 16)
                sp.dma_start(m["acc_d"][T_ALL:T_ALL + PADS, :], zrow).then_inc(pads_in, 16)
                sp.dma_start(m["table_d"].rearrange("(j p) a -> j (p a)", p=P), pad.rearrange("j p a -> j (p a)"))\
                    .then_inc(pads_in, 16)
                sp.wait_ge(w_lo, PARTS)
                load(1)
                sp.wait_ge(w_lo, 2 * PARTS)
                sp.wait_ge(meta_ok, 1)
                e0 = sp.value_load(m["meta"][0:1, 2, 0:1], min_val=0, max_val=E - 1)
                load_expert(sp, m, w1, w3, e0, x13_in)
                load_expert_out(sp, m, w2, e0, x2_in)
                sp.wait_ge(placed, 16 * NB * TOPK)
                sp.dma_start(tab.rearrange("j p a -> j (p a)"), m["table_d"].rearrange("(j p) a -> j (p a)", p=P))\
                    .then_inc(tab_in, 16)
                sp.wait_ge(x2_in, 32)
                for g in range(NG):
                    sp.wait_ge(y_out, GB * (NU - NG + g + 1))
                    sp.dma_start(m["acc_d"][g * GT:(g + 1) * GT, :].rearrange("(b p) d -> p b d", p=P),
                                 X[:, g * GB:(g + 1) * GB, :]).then_inc(stored, 16)

            @block.gpsimd
            def _(pool):
                row_power(pool, c, scales, powered)
                for n in range(PARTS):
                    raw, hi, lo = part(0, n)
                    pool.wait_ge(w_hi, n + 1)
                    pool.tensor_tensor(lo, raw, hi.bitcast(F32), ALU.subtract).then_inc(w_lo, 1)
                n = 0

                def step(instr):
                    nonlocal n
                    n += 1
                    instr.then_inc(iotas, 1)
                    pool.wait_ge(iotas, n)
                pool.memset(tri[:, :, :], 1.0).then_inc(tri_ok, 1)
                pool.memset(triB[:, :], 1.0).then_inc(tri_ok, 1)
                pool.wait_ge(tri_ok, 2)
                pool.affine_select(out=tri[:, :, :], in_=tri[:, :, :], compare_op=ALU.is_gt, fill=0.0,
                                   base=0, pattern=[[1, EG], [-1, EG]], channel_multiplier=0).then_inc(tri_ok, 1)
                pool.affine_select(out=triB[:, :], in_=triB[:, :], compare_op=ALU.is_gt, fill=0.0,
                                   base=0, pattern=[[1, P]], channel_multiplier=-1).then_inc(tri_ok, 1)
                step(pool.memset(zrow, 0.0))
                step(pool.memset(pad, 0.0))
                step(pool.iota(ti[:, :], pattern=[[1, J]], base=0, channel_multiplier=0))
                step(pool.tensor_copy(iJ[:, :], ti[:, :]))
                step(pool.tensor_copy(iE[:, :], ti[:, 0:E]))
                step(pool.iota(ti[:, 0:NB], pattern=[[P, NB]], base=0, channel_multiplier=1))
                step(pool.tensor_copy(tok[:, :], ti[:, 0:NB]))
                step(pool.iota(tp[:, :], pattern=[[1, P]], base=T_ALL, channel_multiplier=0))
                step(pool.tensor_copy(pad[:, :, 0], tp[:, :]))
                pool.wait_ge(pads_in, 48)
                pool.wait_ge(sel_ok, 2)
                for t in range(NB):
                    for k in range(TOPK):
                        pool.indirect_dma_start(
                            out=m["table_d"][:, :], out_offset=bass.IndirectOffsetOnAxis(ap=m["posu"][:, t, k:k + 1], axis=0),
                            in_=m["pair"][:, t, k, :], in_offset=None).then_inc(placed, 16)
                pool.wait_ge(placed, 16 * NB * TOPK)

            @block.tensor
            def _(pe):
                pe.wait_ge(g_in, 32)
                for k in range(KC):
                    i = pe.transpose(G[:, k * E:(k + 1) * E], gw[:, k * P:(k + 1) * P], c["identF"][0:E, 0:E])
                i.then_inc(gt, 1)
                pe.matmul(L[:, 0:E], c["onesF"][0:1, :], b1[:, :], start=True, stop=True).then_inc(bias_ps, 1)

                def logit(g):
                    pe.wait_ge(t_lo, GB * (g + 1))
                    if g == 0:
                        pe.wait_ge(g_lo, 1)
                        pe.wait_ge(routed, 1)
                    else:
                        pe.wait_ge(lg_out, g)
                    for k in range(KC):
                        i = mm3(pe, L[0:E, :], lambda h_: gwT[:, h_, k, :],
                                lambda h_: XT[:, h_, k, g * GT:(g + 1) * GT], k == 0, k == KC - 1)
                    i.then_inc(lg_fill, 1)

                def logit_rows(g):
                    pe.wait_ge(lg_out, g + 1)
                    for t in range(g * GB, (g + 1) * GB):
                        i = pe.transpose(LR[:, t * E:(t + 1) * E], lgT[:, t % GB * P:(t % GB + 1) * P],
                                         c["identF"][0:E, 0:E])
                    i.then_inc(logits, 1)

                def hidden(q):
                    u, ch = q // 3, q % 3
                    b, gr = u // NG, u % NG
                    if gr == 0 and ch == 0:
                        pe.wait_ge(w_lo, PARTS * b + 2)
                    if b == 0 and ch == 0:
                        pe.wait_ge(t_lo, GB * (gr + 1))
                    wait(pe, b_out, q - 1)
                    cols = slice(ch * P, ch * P + IC[ch])
                    for W_, bk in ((W1[b], A[q % 2]), (W3[b], B[q % 2])):
                        for k in range(KC):
                            x_ = mm3(pe, bk[0:IC[ch], :], lambda j: W_[:, j, k, cols],
                                     lambda j: XT[:, j, k, gr * GT:(gr + 1) * GT], k == 0, k == KC - 1)
                    x_.then_inc(ab_fill, 1)

                def outer(u):
                    b = u // NG
                    pe.wait_ge(w_lo, PARTS * (b + 1))
                    pe.wait_ge(h_lo, 3 * u + 3)
                    for t in range(GB):
                        n = u * GB + t
                        wait(pe, y_out, n - 1)
                        for ch in range(3):
                            x_ = mm3(pe, Y[n % 2][:, :], lambda j: hT[0:IC[ch], j, ch, t * P:(t + 1) * P],
                                     lambda j: W2[b][0:IC[ch], j, ch, :], ch == 0, ch == 2)
                        x_.then_inc(y_fill, 1)

                def counts():
                    pe.wait_ge(sel_ok, 1)
                    pe.wait_ge(tri_ok, 4)
                    chosen = selB[:, :, :].rearrange("p t e -> p (t e)")
                    pe.matmul(PT, triB[:, :], chosen, start=True, stop=True)
                    pe.matmul(CT_, c["onesB"][:, :], chosen, start=True, stop=True).then_inc(counted, 1)
                for t in range(NB):
                    pe.wait_ge(normed, t + 1)
                    if t >= 2:
                        pe.wait_ge(t_lo, t - 1)
                    for k in range(KC):
                        i = pe.transpose(T[t % 2][:, k * P:(k + 1) * P], xn[:, t % NX, k * P:(k + 1) * P], c["identF"][:, :])
                    i.then_inc(t_fill, 1)
                    if t % GB == 1 and t > GB:
                        logit(t // GB - 1)
                        hidden(t // GB - 1)
                        logit_rows(t // GB - 1)
                logit(NG - 1)
                hidden(3)
                logit_rows(NG - 1)
                for u in range(NU):
                    if u:
                        hidden(3 * u + 1)
                        if u == 2:
                            counts()
                        hidden(3 * u + 2)
                        if u + 1 < NU:
                            hidden(3 * u + 3)
                        else:
                            pe.wait_ge(tab_in, 16)
                            for j in range(2):
                                pe.transpose(L[:, j * NT:(j + 1) * NT], tab[:, :, j], c["identF"][0:NT, 0:NT]).then_inc(tab_tr, 1)
                    outer(u)

            @block.scalar
            def _(act):
                def split_hi(b, n):
                    raw, hi, _ = part(b, n)
                    act.wait_ge(w13_in if n < 2 else w2_in, 32 * (b + 1))
                    act.activation(hi, raw, ACT.Copy).then_inc(w_hi, 1)

                def logits_out(g):
                    act.wait_ge(lg_fill, g + 1)
                    wait(act, logits, g)
                    act.activation(lgT, L[0:E, :], ACT.Copy).then_inc(lg_out, 1)

                def gated(q):
                    n = IC[q % 3]
                    act.wait_ge(ab_fill, q + 1)
                    wait(act, b_out, q - 1)
                    act.activation(sl[0:n, q % 2, :], A[q % 2][0:n, :], ACT.Silu).then_inc(a_out, 1)
                    act.wait_ge(b_out, q + 1)
                    wait(act, y_fill, GB * (q // 3))
                    act.activation(hT[0:n, 0, q % 3, :], h[0:n, 0, :], ACT.Copy).then_inc(h_hi, 1)
                act.wait_ge(gt, 1)
                act.activation(gwT[:, 0, :, :], G.rearrange("p (k e) -> p k e", k=KC), ACT.Copy).then_inc(g_hi, 1)
                for t in range(NB):
                    act.wait_ge(t_fill, t + 1)
                    act.activation(XT[:, 0, :, t * P:(t + 1) * P], T[t % 2][:, :].rearrange("p (k n) -> p k n", k=KC),
                                   ACT.Copy).then_inc(t_hi, 1)
                    if t < PARTS:
                        split_hi(0, t)
                    if t % GB == 1 and t > GB:
                        logits_out(t // GB - 1)
                    if t % GB == GB - 1 and t > GB:
                        gated(t // GB - 1)
                logits_out(NG - 1)
                act.wait_ge(logits, NG)
                act.activation(s, LR.rearrange("p (t e) -> p t e", t=NB), ACT.Sigmoid).then_inc(sig, 1)
                for q in range(3, 3 * NU):
                    gated(q)
                    if q == SPLIT_AT[0]:
                        act.wait_ge(pads_in, 48)
                        for b in range(NX):
                            act.wait_ge(row_out[b], 16 * NB // NX)
                    if q == SPLIT_AT[1]:
                        act.wait_ge(sel_ok, 2)
                    if q == SPLIT_AT[2]:
                        act.wait_ge(meta_ok, 1)
                    if q in SPLIT_AT:
                        split_hi(1, SPLIT_AT.index(q))
                    if q in EXPERT_AT:
                        k = EXPERT_AT.index(q)
                        act.wait_ge(x13_in, 32)
                        act.activation(m["W13"][:, 0, k, :, :], m["r13"][:, k, :, :], ACT.Copy).then_inc(x13_hi, 1)

            @block.vector
            def _(dve):
                done = 1

                def step(instr):
                    nonlocal done
                    done += 1
                    instr.then_inc(routed, 1)
                    dve.wait_ge(routed, done)
                T16 = [P, NB, E]
                tiled = lambda a: a.rearrange("p (t e) -> p t e", t=NB)
                in_groups = sb_[:, :, :].rearrange("p t (g e) -> p t g e", g=EG)
                wide = [P, NB, EG, E // EG]
                gm, gr, gs = grp[:, 0, :, :], grp[:, 1, :, :], grp[:, 2, :, :]
                nt, acc, start, far = cnt_[:, 0, :], (cnt_[:, 1, :], cnt_[:, 2, :]), cnt_[:, 3, :], cnt_[:, 4, :]
                upto = acc[0]
                pl = run[:, 1, :, :]
                je = [P, J, E]
                cmp = eq[:, :].rearrange("p (j e) -> p j e", j=J)
                ej = big[:, 0:J]

                def best_groups():
                    dve.wait_ge(sig, 1)
                    dve.wait_ge(tri_ok, 4)
                    step(dve.tensor_tensor(sb_[:, :, :], s[:, :, :], bias[:, :].unsqueeze(1).to_broadcast(T16), ALU.add))
                    step(dve.tensor_reduce(gm, in_groups, AX.X, ALU.max))
                    full = [P, NB, EG, EG]
                    mine, other = gm.unsqueeze(3).to_broadcast(full), gm.unsqueeze(2).to_broadcast(full)
                    more, tie = (x_[:, 0:NB * EG * EG].rearrange("p (t i j) -> p t i j", t=NB, i=EG) for x_ in (big, eq))
                    step(dve.tensor_tensor(more, other, mine, ALU.is_gt))
                    step(dve.tensor_tensor(tie, other, mine, ALU.is_equal))
                    step(dve.tensor_tensor(tie, tie, tri[:, :, :].unsqueeze(1).to_broadcast(full), ALU.mult))
                    step(dve.tensor_tensor(more, more, tie, ALU.add))
                    step(dve.tensor_reduce(gr, more, AX.X, ALU.add))

                def drop_other_groups():
                    step(dve.tensor_scalar(gr, gr, float(TOPG), None, ALU.is_lt))
                    step(dve.tensor_scalar(gs, gr, -1.0, -MASKED, ALU.add, ALU.mult))
                    step(dve.tensor_tensor(in_groups, in_groups, gr.unsqueeze(3).to_broadcast(wide), ALU.mult))
                    step(dve.tensor_tensor(in_groups, in_groups, gs.unsqueeze(3).to_broadcast(wide), ALU.add))
                    for t in range(NB):
                        ins = dve.max(top8[:, t, :], sb_[:, t, :])
                    step(ins)

                def top_experts():
                    fourth = top8[:, :, TOPK - 1:TOPK].to_broadcast(T16)
                    step(dve.tensor_tensor(above, sb_[:, :, :], fourth, ALU.is_gt))
                    step(dve.tensor_tensor(same, sb_[:, :, :], fourth, ALU.is_equal))
                    step(dve.tensor_reduce(total[:, 0, :], above, AX.X, ALU.add))
                    step(dve.tensor_copy(before0, same))
                    before = (before0, before1)
                    a = 0
                    for d in (1, 2, 4, 8):
                        step(dve.tensor_copy(before[1 - a][:, :, 0:d], before[a][:, :, 0:d]))
                        step(dve.tensor_tensor(before[1 - a][:, :, d:E], before[a][:, :, d:E], before[a][:, :, 0:E - d], ALU.add))
                        a = 1 - a

                def select():
                    step(dve.tensor_tensor(before0, before0, total[:, 0, :].unsqueeze(2).to_broadcast(T16), ALU.add))
                    step(dve.tensor_scalar(before0, before0, float(TOPK), None, ALU.is_le))
                    step(dve.tensor_tensor(same, same, before0, ALU.mult))
                    step(dve.tensor_tensor(sel[:, :, :], above, same, ALU.add))
                    dve.tensor_copy(selB[:, :, :], sel[:, :, :]).then_inc(sel_ok, 1)
                    step(dve.tensor_tensor(sb_[:, :, :], s[:, :, :], sel[:, :, :], ALU.mult))
                    step(dve.tensor_reduce(total[:, 0, :], sb_[:, :, :], AX.X, ALU.add))
                    step(dve.reciprocal(total[:, 1, :], total[:, 0, :]))
                    step(dve.tensor_scalar(total[:, 1, :], total[:, 1, :], c["tg"][:, 3:4], None, ALU.mult))
                    step(dve.tensor_tensor(sb_[:, :, :], sb_[:, :, :], total[:, 1, :].unsqueeze(2).to_broadcast(T16), ALU.mult))

                def running_counts():
                    dve.wait_ge(counted, 1)
                    step(dve.tensor_copy(run[:, 0, :, :], tiled(CT_)))
                    a = 0
                    for d in (1, 2, 4, 8):
                        step(dve.tensor_copy(run[:, 1 - a, 0:d, :], run[:, a, 0:d, :]))
                        step(dve.tensor_tensor(run[:, 1 - a, d:NB, :], run[:, a, d:NB, :], run[:, a, 0:NB - d, :], ALU.add))
                        a = 1 - a

                def expert_starts():
                    step(dve.tensor_scalar(nt, run[:, 0, NB - 1, :], 1.0 / P, 0.5 - 0.5 / P, ALU.mult, ALU.add))
                    step(dve.tensor_scalar(nt, nt, ROUND, -ROUND, ALU.add, ALU.add))
                    step(dve.tensor_copy(acc[0], nt))
                    a = 0
                    for d in (1, 2, 4, 8):
                        step(dve.tensor_copy(acc[1 - a][:, 0:d], acc[a][:, 0:d]))
                        step(dve.tensor_tensor(acc[1 - a][:, d:E], acc[a][:, d:E], acc[a][:, 0:E - d], ALU.add))
                        a = 1 - a
                    step(dve.tensor_tensor(start, upto, nt, ALU.subtract))
                    step(dve.tensor_scalar(start, start, float(P), 1.0, ALU.mult, ALU.add))

                def places():
                    step(dve.tensor_tensor(pl, run[:, 0, :, :], tiled(CT_), ALU.subtract))
                    step(dve.tensor_tensor(pl, pl, tiled(PT), ALU.add))
                    step(dve.tensor_tensor(pl, pl, start.unsqueeze(1).to_broadcast(T16), ALU.add))
                    step(dve.tensor_tensor(pl, pl, sel[:, :, :], ALU.mult))
                    for t in range(NB):
                        ins = dve.max(m["pos"][:, t, :], pl[:, t, :])
                    step(ins)

                def table_rows():
                    dve.wait_ge(iotas, 9)
                    top = m["pos"][:, :, 0:TOPK]
                    full = [P, NB, TOPK, E]
                    hit = big[:, 0:NB * TOPK * E].rearrange("p (t k e) -> p t k e", t=NB, k=TOPK)
                    step(dve.tensor_tensor(hit, pl.unsqueeze(2).to_broadcast(full), top.unsqueeze(3).to_broadcast(full),
                                           ALU.is_equal))
                    step(dve.tensor_tensor(hit, hit, sb_[:, :, :].unsqueeze(2).to_broadcast(full), ALU.mult))
                    step(dve.tensor_reduce(m["pair"][:, :, :, 1], hit, AX.X, ALU.add))
                    step(dve.tensor_copy(m["pair"][:, :, :, 0], tok[:, :].unsqueeze(2).to_broadcast([P, NB, TOPK])))
                    dve.tensor_scalar(m["posu"][:, :, :], top, -1.0, None, ALU.add).then_inc(sel_ok, 1)

                def tile_experts():
                    step(dve.tensor_tensor(cmp, upto.unsqueeze(1).to_broadcast(je), iJ[:, :].unsqueeze(2).to_broadcast(je),
                                           ALU.is_le))
                    step(dve.tensor_reduce(ej, cmp, AX.X, ALU.add))
                    step(dve.tensor_scalar(ej, ej, float(E - 1), None, ALU.min))
                    step(dve.memset(first[:, 0:1], 1.0))
                    step(dve.tensor_tensor(first[:, 1:J], ej[:, 1:J], ej[:, 0:J - 1], ALU.not_equal))

                def next_candidates():
                    step(dve.tensor_scalar(far, nt, 0.5, 1000.0, ALU.is_lt, ALU.mult))
                    step(dve.tensor_tensor(far, far, iE[:, :], ALU.add))
                    step(dve.tensor_tensor(cmp, iE[:, :].unsqueeze(1).to_broadcast(je), ej.unsqueeze(2).to_broadcast(je),
                                           ALU.is_le))
                    step(dve.tensor_scalar(cmp, cmp, 1000.0, None, ALU.mult))

                def next_expert():
                    step(dve.tensor_tensor(cmp, cmp, far.unsqueeze(1).to_broadcast(je), ALU.add))
                    step(dve.tensor_reduce(nxt, cmp, AX.X, ALU.min))
                    step(dve.tensor_scalar(m["meta"][:, 1, :], nxt[0:1, :], float(E - 1), None, ALU.min))
                    step(dve.tensor_copy(m["meta"][:, 0, :], first[0:1, :]))
                    step(dve.tensor_copy(m["meta"][:, 2, 0:1], ej[0:1, 0:1]))
                    step(dve.tensor_scalar(first[:, 0:TRIPS], iJ[:, 0:TRIPS], float(UT), upto[:, E - 1:E], ALU.mult, ALU.is_lt))
                    step(dve.tensor_reduce(first[:, TRIPS:TRIPS + 1], first[:, 0:TRIPS], AX.X, ALU.add))
                    dve.tensor_copy(m["meta"][:, 2, 1:TRIPS + 2], first[0:1, 0:TRIPS + 1]).then_inc(meta_ok, 1)

                def split_lo(n):
                    raw, hi, lo = part(1, n)
                    dve.wait_ge(w_hi, PARTS + n + 1)
                    dve.tensor_tensor(lo, raw, hi.bitcast(F32), ALU.subtract).then_inc(w_lo, 1)

                def gated(q):
                    n = IC[q % 3]
                    dve.wait_ge(a_out, q + 1)
                    wait(dve, h_lo, q)
                    dve.tensor_tensor(h[0:n, 0, :], B[q % 2][0:n, :], sl[0:n, q % 2, :], ALU.mult).then_inc(b_out, 1)
                    dve.wait_ge(h_hi, q + 1)
                    dve.tensor_tensor(hT[0:n, 1, q % 3, :], h[0:n, 0, :], hT[0:n, 0, q % 3, :].bitcast(F32),
                                      ALU.subtract).then_inc(h_lo, 1)

                def norm(t):
                    if t >= NX:
                        dve.wait_ge(t_fill, t - NX + 1)
                        dve.wait_ge(row_out[t % NX], 16 * (t // NX))
                    dve.tensor_scalar(xn[:, t % NX, :], X[:, t, :], c["mean"][:, t:t + 1], c["rstd"][:, t:t + 1],
                                      ALU.subtract, ALU.mult).then_inc(normed, 1)
                row_scale(dve, c, scales, powered, 1e-5)
                norm(0)
                norm(1)
                dve.wait_ge(g_hi, 1)
                dve.tensor_tensor(gwT[:, 1, :, :], G.rearrange("p (k e) -> p k e", k=KC),
                                  gwT[:, 0, :, :].bitcast(F32), ALU.subtract).then_inc(g_lo, 1)
                dve.wait_ge(bias_ps, 1)
                dve.tensor_copy(bias[:, :], L[:, 0:E]).then_inc(routed, 1)
                for t in range(NB):
                    if t + 2 < NB:
                        norm(t + 2)
                    dve.wait_ge(t_hi, t + 1)
                    dve.tensor_tensor(XT[:, 1, :, t * P:(t + 1) * P], T[t % 2][:, :].rearrange("p (k n) -> p k n", k=KC),
                                      XT[:, 0, :, t * P:(t + 1) * P].bitcast(F32), ALU.subtract).then_inc(t_lo, 1)
                    if t % GB == GB - 1 and t > GB:
                        gated(t // GB - 1)
                between = {3: drop_other_groups, 4: top_experts, 5: select, 7: running_counts,
                           8: expert_starts, 9: table_rows, 10: tile_experts, 11: next_candidates, 12: next_expert}
                best_groups()
                for u in range(NU):
                    for ch in range(3):
                        q = 3 * u + ch
                        if q > 2:
                            gated(q)
                            if q in between:
                                between[q]()
                        if q in SPLIT_AT:
                            split_lo(SPLIT_AT.index(q))
                        if q in EXPERT_AT:
                            k = EXPERT_AT.index(q)
                            dve.wait_ge(x13_hi, k + 1)
                            dve.tensor_tensor(m["W13"][:, 1, k, :, :], m["r13"][:, k, :, :], m["W13"][:, 0, k, :, :].bitcast(F32),
                                              ALU.subtract)
                        if q == 3 * NU - 1:
                            dve.wait_ge(tab_tr, 2)
                            dve.tensor_copy(m["rowid"][:, 0:NT], L[:, 0:NT])
                            dve.tensor_copy(m["wgt"][:, 0:NT], L[:, NT:2 * NT])
                    if u == 2:
                        places()
                    for t in range(GB):
                        n = u * GB + t
                        tt = u % NG * GB + t
                        dve.wait_ge(y_fill, n + 1)
                        wait(dve, y_out, n - NG * GB + 1)
                        dve.scalar_tensor_tensor(out=X[:, tt, :], in0=Y[n % 2][:, :], scalar=c["tg"][:, 3:4],
                                                 in1=X[:, tt, :], op0=ALU.mult, op1=ALU.add).then_inc(y_out, 1)


def expert_tiles(nc, c, m, w1, w2, w3, out):
    identF = c["identF"]
    J = NT + 3
    with ExitStack() as st:
        def sb(name, shape, dt=F32):
            return st.enter_context(nc.sbuf_tensor(name, shape, dt))

        def sem(name):
            return st.enter_context(nc.semaphore(name))

        def bank(name, n):
            return [st.enter_context(nc.psum_tensor(f"{name}{i}", [P, 512], F32)) for i in range(n)]
        rowid, wgt, r13, r2, W13, W2 = (m[n] for n in ("rowid", "wgt", "r13", "r2", "W13", "W2"))
        ids = sb("t_ids", [P, UT], U32)
        wcol = sb("t_wcol", [P, UT])
        pidx = sb("t_pidx", [P, 3], I32)
        xg = sb("t_xg", [P, UT, D])
        xT = sb("t_xT", [P, 2, 2, KC, P], F32R)
        sl = sb("t_sl", [P, I])
        h = sb("t_h", [P, I])
        hT = sb("t_hT", [P, 2, 3, P], F32R)
        ys = sb("t_ys", [P, UT, D])
        H1, H3, Y = bank("t_H1", 2), bank("t_H3", 2), bank("t_Y", 2)
        TX, TH = bank("t_TX", 1)[0], bank("t_TH", 1)[0]
        wcol_set, zeroed = sem("wcol_set"), sem("t_zeroed")
        r13_in, r2_in, w13_hi, w13_lo, w2_hi, w2_lo = (sem(f"t_{n}") for n in ("r13_in", "r2_in", "w13_hi", "w13_lo", "w2_hi", "w2_lo"))
        tx_fill, tx_hi, tx_lo, h_fill, silu, hmul, th_fill, th_hi, th_lo, y_fill, y_evac, scattered = (
            sem(f"t_{n}") for n in ("tx_fill", "tx_hi", "tx_lo", "h_fill", "silu", "hmul", "th_fill", "th_hi", "th_lo",
                                    "y_fill", "y_evac", "scattered"))
        g_in = [sem(f"t_g_in{b}") for b in range(UT)]
        sc_done, out_done = sem("t_sc_done"), sem("t_out_done")
        own_pool, own_act, own_dve, own_sp = c["passed_pool"], c["passed_act"], c["passed_dve"], c["passed_sp"]

        with nc.Block() as block:
            @block.sync
            def _(sp):
                sp.sem_inc(r13_in, 32)
                sp.sem_inc(r2_in, 32)
                trips = sp.value_load(m["meta"][0:1, 2, TRIPS + 1:TRIPS + 2], min_val=T_ALL * TOPK // P // UT, max_val=TRIPS)
                with sp.Fori(0, TRIPS) as i:
                    in_use = sp.value_load(m["meta"][0:1, 2, bass.ds(i + 1, 1)], min_val=0, max_val=1)
                    with sp.If(in_use):
                        for b in range(UT):
                            n = i * UT + b
                            first = sp.value_load(m["meta"][0:1, 0, bass.ds(n, 1)], min_val=0, max_val=1)
                            nxt = sp.value_load(m["meta"][0:1, 1, bass.ds(n, 1)], min_val=0, max_val=E - 1)
                            with sp.If(first):
                                sp.wait_ge(w13_lo, 4 * (n + 1))
                                sp.sem_inc(own_sp, 1)
                                load_expert(sp, m, w1, w3, nxt, r13_in)
                                sp.wait_ge(w2_lo, 2 * (n + 1) + 2)
                                sp.sem_inc(own_sp, 1)
                                load_expert_out(sp, m, w2, nxt, r2_in)
                            with sp.Else():
                                sp.wait_ge(r13_in, 32 * (n + 1))
                                sp.sem_inc(r13_in, 32)
                                sp.wait_ge(r2_in, 32 * (n + 1))
                                sp.sem_inc(r2_in, 32)
                sp.wait_ge(r13_in, trips * (32 * UT) + 32)
                sp.sem_inc(own_sp, 1)
                sp.wait_ge(r2_in, trips * (32 * UT) + 32)
                sp.sem_inc(own_sp, 1)
                sp.wait_ge(sc_done, trips * (16 * UT))
                sp.sem_inc(own_sp, 1)
                sp.dma_start(out.rearrange("b p d -> (b p) d"), m["acc_d"][0:T_ALL, :]).then_inc(out_done, 16)
                sp.wait_ge(out_done, 16)

            @block.gpsimd
            def _(pool):
                scattered_credit = UT + 1
                pool.sem_inc(scattered, scattered_credit)
                pool.iota(pidx[:, :], pattern=[[0, 3]], base=T_ALL, channel_multiplier=1).then_inc(zeroed, 1)
                pool.wait_ge(zeroed, 1)
                pool.tensor_copy(rowid[:, NT:J], pidx[:, :]).then_inc(zeroed, 1)
                pool.wait_ge(zeroed, 2)

                def gather(n, b):
                    pool.tensor_copy(ids[:, b:b + 1], rowid[:, bass.ds(n, 1)]).then_inc(zeroed, 1)

                for n in range(3):
                    gather(n, n)
                    pool.wait_ge(zeroed, 3 + n)
                    pool.indirect_dma_start(out=xg[:, n, :], out_offset=None, in_=m["rows_d"][:, :],
                                            in_offset=bass.IndirectOffsetOnAxis(ap=ids[:, n:n + 1], axis=0)).then_inc(g_in[n], 16)
                pool.wait_ge(m["stored"], 16 * NG)
                trips = pool.value_load(m["meta"][0:1, 2, TRIPS + 1:TRIPS + 2], min_val=T_ALL * TOPK // P // UT, max_val=TRIPS)
                with pool.Fori(0, TRIPS) as i:
                    in_use = pool.value_load(m["meta"][0:1, 2, bass.ds(i + 1, 1)], min_val=0, max_val=1)
                    with pool.If(in_use):
                        for b in range(UT):
                            n = i * UT + b
                            b3 = (b + 3) % UT
                            pool.wait_ge(tx_fill, n + 1)
                            pool.sem_inc(own_pool, 1)
                            gather(n + 3, b3)
                            pool.wait_ge(zeroed, n + 6)
                            pool.sem_inc(own_pool, 1)
                            pool.indirect_dma_start(out=xg[:, b3, :], out_offset=None, in_=m["rows_d"][:, :],
                                                    in_offset=bass.IndirectOffsetOnAxis(ap=ids[:, b3:b3 + 1], axis=0))\
                                .then_inc(g_in[b3], 16)
                            pool.wait_ge(y_evac, n + 4)
                            pool.sem_inc(own_pool, 1)
                            pool.indirect_dma_start(out=m["acc_d"][:, :],
                                                    out_offset=bass.IndirectOffsetOnAxis(ap=ids[:, b:b + 1], axis=0),
                                                    in_=ys[:, b, :], in_offset=None, compute_op=ALU.add).then_inc(sc_done, 16)
                            pool.wait_ge(sc_done, 16 * (n + 1))
                            pool.sem_inc(scattered, 1)
                for b in range(3):
                    pool.wait_ge(g_in[b], trips * 16 + 16)

            @block.tensor
            def _(pe):
                def tx(turn, b):
                    pe.wait_ge(g_in[b % UT], 16 * turn)
                    for k in range(KC):
                        x_ = pe.transpose(TX[:, k * P:(k + 1) * P], xg[:, b % UT, k * P:(k + 1) * P], identF[:, :])
                    x_.then_inc(tx_fill, 1)

                def y(b):
                    for ch in range(3):
                        x_ = mm3(pe, Y[(b - 1) % 2][:, :], lambda j: hT[0:IC[ch], j, ch, :],
                                 lambda j: W2[0:IC[ch], j, ch, :], ch == 0, ch == 2)
                    x_.then_inc(y_fill, 1)
                tx(1, 0)
                trips = pe.value_load(m["meta"][0:1, 2, TRIPS + 1:TRIPS + 2], min_val=T_ALL * TOPK // P // UT, max_val=TRIPS)
                with pe.Fori(0, TRIPS) as i:
                    in_use = pe.value_load(m["meta"][0:1, 2, bass.ds(i + 1, 1)], min_val=0, max_val=1)
                    with pe.If(in_use):
                        for b in range(UT):
                            n = i * UT + b
                            pe.wait_ge(tx_lo, n + 1)
                            for k in range(KC):
                                pe.wait_ge(w13_lo, 4 * n + k + 1)
                                for jx, jw in ((0, 0), (0, 1), (1, 0)):
                                    for bk, j in ((H1, 0), (H3, 1)):
                                        x_ = pe.matmul(bk[b % 2][:, 0:I], xT[:, b % 2, jx, k, :], W13[:, jw, k, j, :],
                                                       start=k == 0 and jx == jw, stop=k == KC - 1 and jx == 1)
                            x_.then_inc(h_fill, 1)
                            tx(i + 1 if b < UT - 1 else i + 2, b + 1)
                            pe.wait_ge(th_lo, n + 1)
                            pe.wait_ge(w2_lo, 2 * n + 2)
                            pe.wait_ge(y_evac, n + 1)
                            y(b)
                            pe.wait_ge(hmul, n + 2)
                            pe.wait_ge(th_lo, n + 1)
                            for ch in range(3):
                                x_ = pe.transpose(TH[0:IC[ch], ch * P:(ch + 1) * P], h[:, ch * P:ch * P + IC[ch]], identF[:, :])
                            x_.then_inc(th_fill, 1)
                pe.wait_ge(th_lo, trips * UT + 1)
                pe.wait_ge(w2_lo, trips * (2 * UT) + 2)
                pe.wait_ge(y_evac, trips * UT + 1)
                y(UT)

            @block.scalar
            def _(act):
                def x_hi(b):
                    act.activation(xT[:, b % 2, 0, :, :], TX[:, :].rearrange("p (k t) -> p k t", k=KC), ACT.Copy).then_inc(tx_hi, 1)

                def w13():
                    for k in range(KC):
                        act.activation(W13[:, 0, k, :, :], r13[:, k, :, :], ACT.Copy).then_inc(w13_hi, 1)

                def y_out(b):
                    act.activation(ys[:, (b - 1) % UT, :], Y[(b - 1) % 2][:, :], ACT.Copy,
                                   scale=wcol[:, (b - 1) % UT:(b - 1) % UT + 1]).then_inc(y_evac, 1)
                act.sem_inc(y_evac, 2)
                act.sem_inc(w13_hi, KC)
                act.wait_ge(tx_fill, 1)
                x_hi(0)
                trips = act.value_load(m["meta"][0:1, 2, TRIPS + 1:TRIPS + 2], min_val=T_ALL * TOPK // P // UT, max_val=TRIPS)
                with act.Fori(0, TRIPS) as i:
                    in_use = act.value_load(m["meta"][0:1, 2, bass.ds(i + 1, 1)], min_val=0, max_val=1)
                    with act.If(in_use):
                        first = act.value_load(m["meta"][0:1, 0, bass.ds(i * UT, 1)], min_val=0, max_val=1)
                        for b in range(UT):
                            n = i * UT + b
                            this, first = first, act.value_load(m["meta"][0:1, 0, bass.ds(n + 1, 1)], min_val=0, max_val=1)
                            act.wait_ge(h_fill, n + 1)
                            act.wait_ge(hmul, n + 1)
                            act.activation(sl[:, :], H1[b % 2][:, 0:I], ACT.Silu).then_inc(silu, 1)
                            act.wait_ge(tx_fill, n + 2)
                            x_hi(b + 1)
                            with act.If(first):
                                act.wait_ge(r13_in, 32 * (n + 2))
                                w13()
                            with act.Else():
                                act.drain()
                                act.sem_inc(w13_hi, KC)
                            act.wait_ge(y_fill, n + 1)
                            act.wait_ge(scattered, n + 1)
                            y_out(b)
                            with act.If(this):
                                act.wait_ge(r2_in, 32 * (n + 1))
                                act.activation(W2[:, 0, 0:2, :], r2[:, 0:2, :], ACT.Copy).then_inc(w2_hi, 1)
                                act.activation(W2[0:IC[2], 0, 2, :], r2[0:IC[2], 2, :], ACT.Copy).then_inc(w2_hi, 1)
                            with act.Else():
                                act.drain()
                                act.sem_inc(w2_hi, 2)
                            act.wait_ge(th_fill, n + 1)
                            act.activation(hT[:, 0, 0:2, :], TH[:, 0:2 * P].rearrange("p (k t) -> p k t", k=2), ACT.Copy)
                            act.activation(hT[0:IC[2], 0, 2, :], TH[0:IC[2], 2 * P:3 * P], ACT.Copy).then_inc(th_hi, 1)
                act.wait_ge(y_fill, trips * UT + 1)
                act.wait_ge(scattered, trips * UT + 1)
                y_out(UT)

            @block.vector
            def _(dve):
                def x_lo(b):
                    dve.tensor_tensor(xT[:, b % 2, 1, :, :], TX[:, :].rearrange("p (k t) -> p k t", k=KC),
                                      xT[:, b % 2, 0, :, :].bitcast(F32), ALU.subtract).then_inc(tx_lo, 1)

                def w13_k(k):
                    dve.tensor_tensor(W13[:, 1, k, :, :], r13[:, k, :, :], W13[:, 0, k, :, :].bitcast(F32), ALU.subtract)\
                        .then_inc(w13_lo, 1)
                dve.sem_inc(hmul, 1)
                dve.memset(hT[:, :, :, :].bitcast(F32), 0.0).then_inc(th_lo, 1)
                dve.memset(wcol[:, :], 0.0).then_inc(wcol_set, 1)
                dve.wait_ge(wcol_set, 1)
                dve.sem_inc(w2_lo, 2)
                dve.sem_inc(w13_lo, KC)
                dve.wait_ge(tx_hi, 1)
                x_lo(0)
                trips = dve.value_load(m["meta"][0:1, 2, TRIPS + 1:TRIPS + 2], min_val=T_ALL * TOPK // P // UT, max_val=TRIPS)
                with dve.Fori(0, TRIPS) as i:
                    in_use = dve.value_load(m["meta"][0:1, 2, bass.ds(i + 1, 1)], min_val=0, max_val=1)
                    with dve.If(in_use):
                        first = dve.value_load(m["meta"][0:1, 0, bass.ds(i * UT, 1)], min_val=0, max_val=1)
                        for b in range(UT):
                            n = i * UT + b
                            this, first = first, dve.value_load(m["meta"][0:1, 0, bass.ds(n + 1, 1)], min_val=0, max_val=1)
                            dve.tensor_copy(wcol[:, b:b + 1], wgt[:, bass.ds(n, 1)])
                            dve.wait_ge(silu, n + 1)
                            dve.tensor_tensor(h[:, :], H3[b % 2][:, 0:I], sl[:, :], ALU.mult).then_inc(hmul, 1)
                            dve.wait_ge(tx_hi, n + 2)
                            x_lo(b + 1)
                            with dve.If(first):
                                for k in range(KC):
                                    dve.wait_ge(w13_hi, 4 * (n + 1) + k + 1)
                                    w13_k(k)
                            with dve.Else():
                                dve.drain()
                                dve.sem_inc(w13_lo, KC)
                            with dve.If(this):
                                dve.wait_ge(y_fill, n + 1)
                                dve.wait_ge(w2_hi, 2 * n + 1)
                                dve.tensor_tensor(W2[:, 1, 0:2, :], r2[:, 0:2, :], W2[:, 0, 0:2, :].bitcast(F32), ALU.subtract)\
                                    .then_inc(w2_lo, 1)
                                dve.wait_ge(w2_hi, 2 * n + 2)
                                dve.tensor_tensor(W2[0:IC[2], 1, 2, :], r2[0:IC[2], 2, :], W2[0:IC[2], 0, 2, :].bitcast(F32),
                                                  ALU.subtract).then_inc(w2_lo, 1)
                            with dve.Else():
                                dve.drain()
                                dve.sem_inc(w2_lo, 2)
                            dve.wait_ge(th_hi, n + 1)
                            dve.tensor_tensor(hT[:, 1, 0:2, :], TH[:, 0:2 * P].rearrange("p (k t) -> p k t", k=2),
                                              hT[:, 0, 0:2, :].bitcast(F32), ALU.subtract)
                            dve.tensor_tensor(hT[0:IC[2], 1, 2, :], TH[0:IC[2], 2 * P:3 * P],
                                              hT[0:IC[2], 0, 2, :].bitcast(F32), ALU.subtract).then_inc(th_lo, 1)


_INS = ['x', 'ctx_2048', 'mask_BxS2_bk0', 'g_xattn', 'g_ffn', 'L0_xattn_norm_w', 'L0_xattn_wq', 'L0_xattn_wk',
        'L0_xattn_wv', 'L0_xattn_wo', 'L0_xattn_wg', 'L0_ffn_weight', 'L0_ffn_bias', 'L1_ffn_gate_w',
        'L1_ffn_expert_bias', 'L1_ffn_w1', 'L1_ffn_w2', 'L1_ffn_w3', 'L1_ffn_sw1', 'L1_ffn_sw2', 'L1_ffn_sw3']
_OUTS = [((NB, S, D), 'float32')]


def kernel(**inputs):
    import numpy as _np
    import concourse.bacc as _bacc
    from concourse import mybir as _mybir
    from concourse.bass_utils import run_bass_kernel_spmd as _run

    nc = _bacc.Bacc("TRN2", target_bir_lowering=False, num_devices=1)
    arrays, args = {}, []
    for name in _INS:
        a = _np.ascontiguousarray(inputs[name])
        arrays[f"in_{name}_dram"] = a
        args.append(nc.dram_tensor(f"in_{name}_dram", a.shape, _mybir.dt.from_np(a.dtype), kind="ExternalInput").ap())
    for i, (shape, dtype) in enumerate(_OUTS):
        args.append(nc.dram_tensor(f"out_{i}_dram", shape, _mybir.dt.from_np(_np.dtype(dtype)), kind="ExternalOutput").ap())
    program(nc, *args)
    r = _run(nc, [arrays], core_ids=[0])
    return r.results[0]["out_0_dram"]
```
